# Optimizing a Trainium2 kernel written in Bass

```python
import numpy as np
import jax
import jax.numpy as jnp

def _softmax(x, axis=-1):
    return jax.nn.softmax(x, axis=axis)

def _gelu(x):
    return jax.nn.gelu(x, approximate=True)

def _silu(x):
    return jax.nn.silu(x)

def _sigmoid(x):
    return jax.nn.sigmoid(x)

def _layernorm(x, axis=-1, eps=1e-05):
    m = jnp.mean(x, axis=axis, keepdims=True)
    v = jnp.var(x, axis=axis, keepdims=True)
    return (x - m) / jnp.sqrt(v + eps)

def _scatter_add(tgt, idx, src, axis=0):
    return tgt.at[idx].add(src)

def _segment_sum(src, seg, n):
    return jax.ops.segment_sum(src, seg, n)
kernel_name = 'mk_decoder_preln_d1_seqx_r4_f271b1'

def setup_inputs(seed: int=0):
    np.random.seed(seed)
    _w = jnp.asarray

    def _rec_inputs():
        import jax
        import jax.numpy as jnp
        _rk = jax.random.key(seed)
        x = -0.000125 + 0.9999 * jax.random.normal(jax.random.fold_in(_rk, 1), (4, 512, 512), jnp.float32)
        _lenS = 512 - jax.random.randint(jax.random.fold_in(_rk, 7), (4,), 0, max(1, 512 // 4) + 1, jnp.int32)
        _lenS2 = 512 - jax.random.randint(jax.random.fold_in(_rk, 8), (4,), 0, max(1, 512 // 4) + 1, jnp.int32)
        _ctx_2048P = jax.random.normal(jax.random.fold_in(_rk, 11), (4, 16, 512), jnp.float32)
        _ctx_2048c = jax.random.dirichlet(jax.random.fold_in(_rk, 511), 0.3 * jnp.ones((16,), jnp.float32), (4, 512))
        _ctx_2048t = jnp.einsum('bsk,bkd->bsd', _ctx_2048c, _ctx_2048P)
        _ctx_2048t = _ctx_2048t * jax.lax.rsqrt(jnp.mean(jnp.square(_ctx_2048t)) + 1e-12) * 0.953939
        ctx_2048 = -0.00010331 + 0.999899 * (_ctx_2048t + 0.3 * jax.random.normal(jax.random.fold_in(_rk, 611), (4, 512, 512), jnp.float32))
        _validS = jnp.arange(512)[None, :] < _lenS[:, None]
        _validS2 = jnp.arange(512)[None, :] < _lenS2[:, None]
        _causal = jnp.tril(jnp.ones((512, 512), dtype=bool))
        mask_Bx1xS2_ff0 = jnp.where(jnp.ones((4, 1, 512), dtype=bool), 0.0, -1000000000.0).astype(jnp.float32)
        return (x, ctx_2048, mask_Bx1xS2_ff0)
    x, ctx_2048, mask_Bx1xS2_ff0 = _rec_inputs()

    def _L0_attn_setup():
        import jax, jax.numpy as jnp
        import numpy as np
        B, T, D_MODEL = (2, 512, 512)
        N_HEADS, N_KV_HEADS, HEAD_DIM = (16, 4, 128)
        N_REP = N_HEADS // N_KV_HEADS
        EPS = 1e-06

        def _qknorm(t, scale):
            norm = jax.lax.rsqrt(jnp.mean(t * t, axis=-1, keepdims=True) + EPS)
            return t * norm * scale
        key = jax.random.key(seed)
        ks = jax.random.split(key, 5)
        return {'x': jax.random.normal(ks[0], (B, T, D_MODEL), dtype=jnp.float32), 'Wq': jax.random.normal(ks[1], (N_HEADS * HEAD_DIM, D_MODEL), dtype=jnp.float32) * 0.02, 'Wk': jax.random.normal(ks[2], (N_KV_HEADS * HEAD_DIM, D_MODEL), dtype=jnp.float32) * 0.02, 'Wv': jax.random.normal(ks[3], (N_KV_HEADS * HEAD_DIM, D_MODEL), dtype=jnp.float32) * 0.02, 'Wo': jax.random.normal(ks[4], (D_MODEL, N_HEADS * HEAD_DIM), dtype=jnp.float32) * 0.02, 'q_scale': jnp.ones((HEAD_DIM,), dtype=jnp.float32), 'k_scale': jnp.ones((HEAD_DIM,), dtype=jnp.float32)}
    _L0_attn_all = _L0_attn_setup()
    _L0_attn_in = {k: v for k, v in _L0_attn_all.items() if k in ('Wq', 'Wk', 'Wv', 'Wo', 'q_scale', 'k_scale')}
    del _L0_attn_all

    def _L0_xattn_setup():
        import jax, jax.numpy as jnp
        import numpy as np
        FP8_E4M3_MAX = 448.0
        EPS = 1e-12

        def _fp8_quant_dequant(x):
            amax = jnp.max(jnp.abs(x))
            scale = FP8_E4M3_MAX / jnp.maximum(amax, EPS)
            q = jnp.clip(x * scale, -FP8_E4M3_MAX, FP8_E4M3_MAX).astype(jnp.float8_e4m3fn)
            return q.astype(jnp.float32) / scale
        key = jax.random.key(seed)
        k1, k2 = jax.random.split(key)
        B, M, K, N = (32, 128, 512, 512)
        inp = jax.random.normal(k1, (B, M, K), dtype=jnp.float32)
        weight = jax.random.normal(k2, (B, K, N), dtype=jnp.float32)
        bias = jnp.zeros((B, 1, N), dtype=jnp.float32)
        return {'input': inp, 'weight': weight, 'bias': bias}
    _L0_xattn_all = _L0_xattn_setup()
    _L0_xattn_in = {k: v for k, v in _L0_xattn_all.items() if k in ()}
    del _L0_xattn_all

    def _L0_ffn_setup():
        import jax, jax.numpy as jnp
        import numpy as np
        B, S, D = (4, 512, 512)
        E = 8
        H = 704
        CAP_F = 1.0

        def _moe(x, Wg, W1, W3, W2, sw1, sw3, sw2):
            b, sl, d = x.shape
            T = b * sl
            C = int(CAP_F * T / E)
            xt = x.reshape(T, d)
            probs = jax.nn.softmax(xt @ Wg, axis=-1)
            eidx = jnp.argmax(probs, axis=-1)
            gate = jnp.take_along_axis(probs, eidx[:, None], 1)[:, 0]
            oh = jax.nn.one_hot(eidx, E, dtype=jnp.int32)
            pos = (jnp.cumsum(oh, axis=0) * oh).sum(-1) - 1
            keep = pos < C
            flat = jnp.where(keep, eidx * C + pos, E * C)
            xd = jnp.zeros((E * C, d), x.dtype).at[flat].set(xt, mode='drop')
            xd = xd.reshape(E, C, d)
            h = jax.nn.silu(jnp.einsum('ecd,edh->ech', xd, W1)) * jnp.einsum('ecd,edh->ech', xd, W3)
            oe = jnp.einsum('ech,ehd->ecd', h, W2).reshape(E * C, d)
            out = jnp.take(oe, jnp.minimum(flat, E * C - 1), axis=0)
            out = out * (gate * keep.astype(x.dtype))[:, None]
            shared = jax.nn.silu(xt @ sw1) * (xt @ sw3) @ sw2
            return (out + shared).reshape(b, sl, d)
        key = jax.random.key(seed)
        ks = jax.random.split(key, 8)
        s = lambda fan: 1.0 / np.sqrt(fan)
        return {'x': jax.random.normal(ks[0], (B, S, D), jnp.float32), 'Wg': jax.random.normal(ks[1], (D, E), jnp.float32) * s(D), 'W1': jax.random.normal(ks[2], (E, D, H), jnp.float32) * s(D), 'W3': jax.random.normal(ks[3], (E, D, H), jnp.float32) * s(D), 'W2': jax.random.normal(ks[4], (E, H, D), jnp.float32) * s(H), 'sw1': jax.random.normal(ks[5], (D, H), jnp.float32) * s(D), 'sw3': jax.random.normal(ks[6], (D, H), jnp.float32) * s(D), 'sw2': jax.random.normal(ks[7], (H, D), jnp.float32) * s(H)}
    _L0_ffn_all = _L0_ffn_setup()
    _L0_ffn_in = {k: v for k, v in _L0_ffn_all.items() if k in ('Wg', 'W1', 'W3', 'W2', 'sw1', 'sw3', 'sw2')}
    del _L0_ffn_all
    return {'x': x, 'ctx_2048': ctx_2048, 'mask_Bx1xS2_ff0': mask_Bx1xS2_ff0, 'L0_attn_Wq': _L0_attn_in['Wq'], 'L0_attn_Wk': _L0_attn_in['Wk'], 'L0_attn_Wv': _L0_attn_in['Wv'], 'L0_attn_Wo': _L0_attn_in['Wo'], 'L0_attn_q_scale': _L0_attn_in['q_scale'], 'L0_attn_k_scale': _L0_attn_in['k_scale'], 'L0_ffn_Wg': _L0_ffn_in['Wg'], 'L0_ffn_W1': _L0_ffn_in['W1'], 'L0_ffn_W3': _L0_ffn_in['W3'], 'L0_ffn_W2': _L0_ffn_in['W2'], 'L0_ffn_sw1': _L0_ffn_in['sw1'], 'L0_ffn_sw3': _L0_ffn_in['sw3'], 'L0_ffn_sw2': _L0_ffn_in['sw2']}

def reference(x, ctx_2048, mask_Bx1xS2_ff0, L0_attn_Wq, L0_attn_Wk, L0_attn_Wv, L0_attn_Wo, L0_attn_q_scale, L0_attn_k_scale, L0_ffn_Wg, L0_ffn_W1, L0_ffn_W3, L0_ffn_W2, L0_ffn_sw1, L0_ffn_sw3, L0_ffn_sw2):
    import jax
    import jax.numpy as jnp

    def _L0_attn_ref(x, Wq, Wk, Wv, Wo, q_scale, k_scale):
        import jax, jax.numpy as jnp
        import numpy as np
        B, T, D_MODEL = (2, 512, 512)
        N_HEADS, N_KV_HEADS, HEAD_DIM = (16, 4, 128)
        N_REP = N_HEADS // N_KV_HEADS
        EPS = 1e-06

        def _qknorm(t, scale):
            norm = jax.lax.rsqrt(jnp.mean(t * t, axis=-1, keepdims=True) + EPS)
            return t * norm * scale
        b, t, _ = x.shape
        q = (x @ Wq.T).reshape(b, t, N_HEADS, HEAD_DIM).transpose(0, 2, 1, 3)
        k = (x @ Wk.T).reshape(b, t, N_KV_HEADS, HEAD_DIM).transpose(0, 2, 1, 3)
        v = (x @ Wv.T).reshape(b, t, N_KV_HEADS, HEAD_DIM).transpose(0, 2, 1, 3)
        q = _qknorm(q, q_scale)
        k = _qknorm(k, k_scale)
        k = jnp.repeat(k, N_REP, axis=1)
        v = jnp.repeat(v, N_REP, axis=1)
        scale = 1.0 / np.sqrt(HEAD_DIM).astype(np.float32)
        scores = jnp.einsum('bhtd,bhsd->bhts', q, k) * scale
        causal = jnp.tril(jnp.ones((t, t), dtype=bool))
        scores = jnp.where(causal, scores, jnp.finfo(scores.dtype).min)
        attn = jax.nn.softmax(scores, axis=-1)
        out = jnp.einsum('bhts,bhsd->bhtd', attn, v)
        out = out.transpose(0, 2, 1, 3).reshape(b, t, N_HEADS * HEAD_DIM)
        return out @ Wo.T

    def _L0_xattn_ref(input, weight, bias):
        import jax, jax.numpy as jnp
        import numpy as np
        FP8_E4M3_MAX = 448.0
        EPS = 1e-12

        def _fp8_quant_dequant(x):
            amax = jnp.max(jnp.abs(x))
            scale = FP8_E4M3_MAX / jnp.maximum(amax, EPS)
            q = jnp.clip(x * scale, -FP8_E4M3_MAX, FP8_E4M3_MAX).astype(jnp.float8_e4m3fn)
            return q.astype(jnp.float32) / scale
        x_dq = _fp8_quant_dequant(input)
        w_dq = _fp8_quant_dequant(weight)
        out = jnp.einsum('bmk,bkn->bmn', x_dq, w_dq)
        out = out + bias
        return out

    def _L0_ffn_ref(x, Wg, W1, W3, W2, sw1, sw3, sw2):
        import jax, jax.numpy as jnp
        import numpy as np
        B, S, D = (4, 512, 512)
        E = 8
        H = 704
        CAP_F = 1.0

        def _moe(x, Wg, W1, W3, W2, sw1, sw3, sw2):
            b, sl, d = x.shape
            T = b * sl
            C = int(CAP_F * T / E)
            xt = x.reshape(T, d)
            probs = jax.nn.softmax(xt @ Wg, axis=-1)
            eidx = jnp.argmax(probs, axis=-1)
            gate = jnp.take_along_axis(probs, eidx[:, None], 1)[:, 0]
            oh = jax.nn.one_hot(eidx, E, dtype=jnp.int32)
            pos = (jnp.cumsum(oh, axis=0) * oh).sum(-1) - 1
            keep = pos < C
            flat = jnp.where(keep, eidx * C + pos, E * C)
            xd = jnp.zeros((E * C, d), x.dtype).at[flat].set(xt, mode='drop')
            xd = xd.reshape(E, C, d)
            h = jax.nn.silu(jnp.einsum('ecd,edh->ech', xd, W1)) * jnp.einsum('ecd,edh->ech', xd, W3)
            oe = jnp.einsum('ech,ehd->ecd', h, W2).reshape(E * C, d)
            out = jnp.take(oe, jnp.minimum(flat, E * C - 1), axis=0)
            out = out * (gate * keep.astype(x.dtype))[:, None]
            shared = jax.nn.silu(xt @ sw1) * (xt @ sw3) @ sw2
            return (out + shared).reshape(b, sl, d)
        return _moe(x, Wg, W1, W3, W2, sw1, sw3, sw2)
    x = x + _L0_attn_ref(_layernorm(x, axis=-1), L0_attn_Wq, L0_attn_Wk, L0_attn_Wv, L0_attn_Wo, L0_attn_q_scale, L0_attn_k_scale)
    x = x + _L0_xattn_ref(_layernorm(x, axis=-1), ctx_2048, mask_Bx1xS2_ff0)
    x = x + _L0_ffn_ref(_layernorm(x, axis=-1), L0_ffn_Wg, L0_ffn_W1, L0_ffn_W3, L0_ffn_W2, L0_ffn_sw1, L0_ffn_sw3, L0_ffn_sw2)
    return x

_drawn_inputs = setup_inputs


def setup_inputs(seed=0):
    import zlib

    import numpy as np

    out = dict(_drawn_inputs(seed))
    spreads = {'L0_attn_q_scale': (1.0, 0.555), 'L0_attn_k_scale': (1.0, 0.541)}
    factors = {'L0_ffn_Wg': 5.26,
     'L0_ffn_W1': 5.383,
     'L0_ffn_W3': 5.044,
     'L0_ffn_W2': 5.027,
     'L0_ffn_sw1': 8.0,
     'L0_ffn_sw3': 7.574,
     'L0_ffn_sw2': 7.612}
    for name, (base, spread) in spreads.items():
        noise = np.random.default_rng([zlib.crc32(name.encode()), seed]).standard_normal(out[name].shape)
        drawn = base * np.exp(spread * noise) if base else spread * noise
        out[name] = jnp.asarray(drawn.astype(out[name].dtype))
    for name, factor in factors.items():
        out[name] = (out[name] * factor).astype(out[name].dtype)
    return out
```

```python
from contextlib import ExitStack

import concourse.bass as bass
from concourse import mybir

P = 128
B, T, D = 4, 512, 512
NH, NKV, HD = 16, 4, 128
REP = NH // NKV
KC = D // P
TB = T // P
NT = B * TB
UNITS = NKV * B
LN_EPS = 1e-5
QK_EPS = 1e-6
SCALE = float(HD) ** -0.5
MASKED = -1e30
FP8_MAX = 448.0
FP8_EPS = 1e-12
FP8_LEAST = 2.0 ** -6
ROUND_AT = 1.5 * 2.0 ** 20
EXPONENT = 0x7F800000
NE, H = 8, 704
CAP = B * T // NE
CAP_T = CAP // P
HC = H // P
HT = H - HC * P
W13 = 2 * H
W3_TAIL, W3_FULL = H, H + HT
NS = HC + 1

ALU = mybir.AluOpType
ACT = mybir.ActivationFunctionType
AX = mybir.AxisListType
F32 = mybir.dt.float32
F32R = mybir.dt.float32r
BF16 = mybir.dt.bfloat16
I32 = mybir.dt.int32
RMAX = bass.bass_isa.ReduceOp.max

P_OFF = [P * (j * (j + 1) // 2) for j in range(TB + 1)]
PT_OFF = {0: 0, 1: 512, 3: 896, 2: 1024}
CHUNKS = {"A": (0, 512, [0]), "B": (512, 512, [1, 3]), "C": (1024, 256, [2])}

TILES = ["k", "q0", "q1", "q2", "q3", "v", "o0", "o1", "o2", "o3"]
QKV_TILES, O_TILES = TILES[:6], TILES[6:]
RING = 2


class Banks:

    def __init__(self, uses, base, filled, freed):
        self.filled, self.freed = filled, freed
        self.at, seen = {}, {}
        for name, bank in uses:
            self.at[name] = (bank, seen.get(bank, 0))
            seen[bank] = seen.get(bank, 0) + 1
        self.base = base

    def use(self, name):
        bank, n = self.at[name]
        return bank, self.base[bank] + n


def count(uses, of=range(8)):
    return {b: sum(1 for _, bank in uses if bank == b) for b in of}


def unit_uses(prep, final):
    uses = [(f"w_{t}", 4 + i % 4) for i, t in enumerate(QKV_TILES)] if prep else []
    for h in range(REP):
        uses += [(f"Q{h}", 7), (f"A{h}", 4), (f"B{h}", 5), (f"C{h}", 6)]
        uses += [("V", 6)] if h == 0 else [("K", 6)] if h == 2 else []
        uses += [(f"PV{h}", 4), (f"SS{h}", 5)]
    uses += [("VT", 6), ("O0", 7), ("O1", 4), ("RK", 5), ("O2", 6), ("O3", 4)]
    if prep:
        uses += [(f"w_{t}", 4 + i % 4) for i, t in enumerate(O_TILES)]
    if final:
        uses = [u for u in uses if u[0][0] in "ABCPO"]
    return uses


def shared_uses(ahead):
    uses = []
    for c in range(HC):
        uses += [(f"a{c}", 2 * (c % 2)), (f"b{c}", 2 * (c % 2) + 1)]
        if c == 0:
            uses += [("CS", 5)]
        if ahead:
            uses += [(f"QT{c}", 4)] if c < TB else []
            uses += [(f"XA{c - 1}", 5)] if c else []
    uses += [("ab", 2), ("D0", 6), ("D1", 7)]
    uses += [(f"XT{t}", 4 + t % 2) for t in range(TB if ahead else CAP_T)]
    uses += [("D2", 6), ("D3", 7)]
    return uses + ([("RT", 4)] if ahead else [])


def expert_uses(ahead):
    uses = []
    for c in range(HC):
        uses += [(f"a{c}", 2 * (c % 2)), (f"b{c}", 2 * (c % 2) + 1)]
    uses += [("ab", 2)]
    uses += [(f"XT{t}", 4 + t) for t in range(CAP_T)] if ahead else []
    return uses + [("D0", 6), ("D1", 7)]


def before_shared_uses():
    uses = []
    for t in range(TB):
        uses += [(f"QT{t}", 6 + t % 2), (f"XA{t}", 5)]
    return uses + [(f"XT{t}", t) for t in range(TB)] + [("RT", 4)]


def first_uses():
    uses = []
    for b in range(B):
        if b == 1:
            uses += [("V", 6), ("K", 7)]
            for h in range(REP):
                uses += [(f"Q{h}", 4 + h % 2), (f"SS{h}", 6)]
            uses += [("VT", 7), ("RK", 6)]
        if b == 0:
            uses += [(f"w_{t}", 4 + i % 4) for i, t in enumerate(TILES)]
        uses += [(f"x{b}{t}", 4 + t) for t in range(TB)]
    return uses


def decoder(nc, x, ctx_in_dram, mask_dram, Wq, Wk, Wv, Wo, q_scale, k_scale, Wg, W1, W3, W2, sw1, sw3, sw2, out):
    nc_stack = ExitStack()
    with nc_stack as stack:

        def sem(name):
            return stack.enter_context(nc.semaphore(name))

        base = nc.sbuf_base + (-nc.sbuf_base) % 32
        room = nc.sbuf_usable_end - 64 - base
        slab = stack.enter_context(nc.sbuf_tensor("slab", [P, (room - 64) // 4], F32))
        place = [base + 32]

        def sb(name, shape, dtype):
            n = 1
            for s in shape[1:]:
                n *= s
            size = n * (2 if dtype == BF16 else 4)
            t = nc.alloc_sbuf_tensor_at(name, shape, dtype, offset=place[0])
            place[0] += size + (-size) % 32
            assert place[0] <= base + room, (name, place[0] - base - room)
            return t

        psum = [stack.enter_context(nc.psum_tensor(f"bank{i}", [P, 512], F32)) for i in range(8)]

        xres = sb("xres", [P, NT, D], F32)
        ident = sb("ident", [P, P], F32)
        ident_b = sb("ident_b", [P, P], BF16)
        causal = sb("causal", [P, P], BF16)
        ones = sb("ones", [P, 2], F32)
        qs_col = sb("qs_col", [P, 2], F32)
        qk_scale = sb("qk_scale", [P, 1], F32)
        stats = sb("stats", [P, TB, 6], F32)
        mv = sb("mv", [P, TB, 2], F32)
        mean = sb("mean", [P, NT], F32)
        rstd = sb("rstd", [P, NT], F32)
        chain_v = sb("chain_v", [P, 20], F32)
        chain_t = sb("chain_t", [P, 20], F32)
        rowmax = sb("rowmax", [P, NT], F32)
        rowmin = sb("rowmin", [P, NT], F32)
        amax = sb("amax", [P, 4], F32)
        ctx_part = sb("ctx_part", [P, 2, B], F32)
        extremes = sb("extremes", [P, 2], F32)
        f8scale = sb("f8scale", [P, 4], F32)
        common_end = place[0]

        xTh = sb("xTh", [P, KC, B * T], F32R)
        xTl = sb("xTl", [P, KC, B * T], F32R)
        wTh = sb("wTh", [P, 6, D], F32R)
        wTl = sb("wTl", [P, 6, D], F32R)
        wstage_at = place[0]
        wstage = sb("wstage", [P, RING, D], F32)
        woTh = sb("woTh", [P, REP, D], F32R)
        woTl = sb("woTl", [P, REP, D], F32R)
        qTh = sb("qTh", [P, REP, T], F32R)
        qTl = sb("qTl", [P, REP, T], F32R)
        kTh = sb("kTh", [P, T], F32R)
        kTl = sb("kTl", [P, T], F32R)
        vh = sb("vh", [P, TB, HD], F32R)
        vl = sb("vl", [P, TB, HD], F32R)
        otmp = place[0]
        oTh = sb("oTh", [P, REP, T], F32R)
        oTl = sb("oTl", [P, REP, T], F32R)
        pTh = sb("pTh", [P, P_OFF[TB]], F32R)
        zeros = nc.alloc_sbuf_tensor_at("zeros", [P, 2, D], F32, offset=place[0])
        pTl = sb("pTl", [P, P_OFF[TB]], F32R)
        probs = sb("probs", [P, P_OFF[TB]], F32)
        xn = probs[:, 0:2 * D].rearrange("p (s d) -> p s d", s=2)
        qsq = sb("qsq", [P, T], F32)
        ksq = sb("ksq", [P, T], F32)
        kraw = sb("kraw", [P, T], F32)
        vraw = sb("vraw", [P, T], F32)
        ss = sb("ss", [P, 20], F32)
        sc = sb("sc", [P, 20], F32)
        mx = sb("mx", [P, 16], F32)
        nbias = sb("nbias", [P, 16], F32)
        rowsum = sb("rowsum", [P, 16], F32)
        rinv = sb("rinv", [P, 4], F32)
        ctx_all = nc.alloc_sbuf_tensor_at("ctx_all", [P, 2, 4, D], F32, offset=otmp)
        ctx_m = sb("ctx_m", [P, D // 2], F32)
        ctx_q = sb("ctx_q", [P, D], BF16)

        place[0] = common_end
        w13h = sb("w13h", [P, KC, W13], F32R)
        w13l = sb("w13l", [P, KC, W13], F32R)
        w13st = sb("w13st", [P, KC, W13], F32)
        w2st = sb("w2st", [P, 2, D], F32)
        assert place[0] <= wstage_at
        w2h = sb("w2h", [P, NS, D], F32R)
        w2l = sb("w2l", [P, NS, D], F32R)
        xh = sb("xh", [P, KC, T], F32R)
        xl = sb("xl", [P, KC, T], F32R)
        hh = sb("hh", [P, NS, T], F32R)
        hl = sb("hl", [P, HC, T], F32R)
        gate_act = sb("gate_act", [P, 2, T], F32)
        hid = sb("hid", [P, 2, T], F32)
        x3n = sb("x3n", [P, TB, D], F32)
        ctxq = sb("ctxq", [P, KC, D], BF16)
        tokens_q = sb("tokens_q", [P, 2, D], BF16)
        tokens_qT = sb("tokens_qT", [P, 2, KC, P], BF16)
        q_at = place[0]
        q_y = sb("q_y", [P, D], F32)
        q_m = sb("q_m", [P, D], F32)
        attended = sb("attended", [P, D], F32)
        mask_b = sb("mask_b", [P, D], F32)
        wg = sb("wg", [P, KC, NE], F32)
        wgh = sb("wgh", [P, KC, NE], F32R)
        wgl = sb("wgl", [P, KC, NE], F32R)
        tri = sb("tri", [P, P], BF16)
        ones_b = sb("ones_b", [P, P], BF16)
        expert_id = sb("expert_id", [P, NE], F32)
        lg = sb("lg", [P, TB, NE], F32)
        lt = sb("lt", [P, TB, NE], F32)
        le = sb("le", [P, TB, NE], F32)
        onehot = sb("onehot", [P, TB, NE], BF16)
        pos = sb("pos", [P, TB, NE], F32)
        carry = sb("carry", [P, NE], F32)
        r_max = sb("r_max", [P, TB], F32)
        r_idx = sb("r_idx", [P, TB], F32)
        r_sum = sb("r_sum", [P, TB], F32)
        r_sel = sb("r_sel", [P, TB], F32)
        r_keep = sb("r_keep", [P, TB], F32)
        r_t = sb("r_t", [P, TB], F32)
        slot_w = sb("slot_w", [P, TB], I32)
        slot_r = sb("slot_r", [P, NT], I32)
        gates = sb("gates", [P, NT], F32)
        expert_out = nc.alloc_sbuf_tensor_at("expert_out", [P, CAP_T, D], F32, offset=q_at)
        gathered = nc.alloc_sbuf_tensor_at("gathered", [P, NT, D], F32, offset=common_end)

        ctxq_dram = nc.dram_tensor("ctxq_dram", [B * T, D], BF16, kind="Internal").ap()
        sent = nc.dram_tensor("sent", [NE * CAP, D], F32, kind="Internal").ap()
        answered = nc.dram_tensor("answered", [NE * CAP, D], F32, kind="Internal").ap()

        x_in = [sem(f"x_in{b}") for b in range(B)]
        scales_in = sem("scales_in")
        w_in = [sem(f"w_in{r}") for r in range(RING)]
        filled = {b: sem(f"filled{b}") for b in range(4, 8)}
        freed = {b: sem(f"freed{b}") for b in range(4, 8)}
        consts = sem("consts")
        pool_step = sem("pool_step")
        ones_set = sem("ones_set")
        hi_done = sem("hi_done")
        xn_done = sem("xn_done")
        s_filled = sem("s_filled")
        exp_done = sem("exp_done")
        bias_done = sem("bias_done")
        norm_done = sem("norm_done")
        sq_done = sem("sq_done")
        norms_done = sem("norms_done")
        k_ready = sem("k_ready")
        qkl_done = sem("qkl_done")
        attn_done = sem("attn_done")
        ctx_all_in = [sem(f"ctx_all_in{i}") for i in range(2)]
        ctx_in = [sem(f"ctx_in{i}") for i in range(2)]
        ctx_read = sem("ctx_read")
        ctx_amax = sem("ctx_amax")
        ctx_amax_all = sem("ctx_amax_all")
        ctxq_done = sem("ctxq_done")
        ctxq_out = sem("ctxq_out")
        zeros_set = sem("zeros_set")
        sent_zeroed = sem("sent_zeroed")
        x_amax = sem("x_amax")
        x_amax_all = sem("x_amax_all")
        w13_in = [sem(f"w13_in{k}") for k in range(KC)]
        w2_in = [sem(f"w2_in{k}") for k in range(2)]
        w13_high = sem("w13_high")
        w13_low = sem("w13_low")
        w2_high = sem("w2_high")
        w2_low = sem("w2_low")
        ctxq_in = sem("ctxq_in")
        mask_in = sem("mask_in")
        wg_in = sem("wg_in")
        wg_high = sem("wg_high")
        wg_low = sem("wg_low")
        mask_read = sem("mask_read")
        mfull = {b: sem(f"mfull{b}") for b in range(8)}
        mfree = {b: sem(f"mfree{b}") for b in range(8)}
        quantised = sem("quantised")
        qT_done = sem("qT_done")
        x3n_done = sem("x3n_done")
        xh_done = sem("xh_done")
        act_done = sem("act_done")
        hh_done = sem("hh_done")
        hl_done = sem("hl_done")
        logits_less_max = sem("logits_less_max")
        logits_exp = sem("logits_exp")
        onehot_done = sem("onehot_done")
        slots_done = sem("slots_done")
        tokens_sent = sem("tokens_sent")
        expert_in = sem("expert_in")
        answers_out = [sem(f"answers_out{m}") for m in range(CAP_T)]
        route_consts = sem("route_consts")
        answers_in = [sem(f"answers_in{i}") for i in range(NT // TB)]
        result_done = sem("result_done")
        stored = sem("stored")

        block = stack.enter_context(nc.Block())

        FIRST, UNIT, PREP, FINAL = first_uses(), unit_uses(False, False), unit_uses(True, False), unit_uses(False, True)
        n_first, n_unit = count(FIRST), count(UNIT)
        n_prep = {b: n - n_unit[b] for b, n in count(PREP).items()}

        def banks(u, g, prep, final=False):
            return Banks(PREP if prep else FINAL if final else UNIT,
                         {b: n_first[b] + u * n_unit[b] + g * n_prep[b] for b in range(8)}, filled, freed)

        first = Banks(FIRST, {b: 0 for b in range(8)}, filled, freed)

        BEFORE, SHARED, SHARED_LAST = before_shared_uses(), shared_uses(True), shared_uses(False)
        EXPERT, EXPERT_LAST = expert_uses(True), expert_uses(False)
        n_before, n_shared, n_shared_last, n_expert = (count(u) for u in (BEFORE, SHARED, SHARED_LAST, EXPERT))
        before = Banks(BEFORE, {b: 0 for b in range(8)}, mfull, mfree)

        def shared_banks(b, ahead):
            return Banks(SHARED if ahead else SHARED_LAST,
                         {k: n_before[k] + b * n_shared[k] for k in range(8)}, mfull, mfree)

        def expert_banks(e, ahead):
            start = {k: n_before[k] + (B - 1) * n_shared[k] + n_shared_last[k] for k in range(8)}
            return Banks(EXPERT if ahead else EXPERT_LAST, {k: start[k] + e * n_expert[k] for k in range(8)},
                         mfull, mfree)

        def units(eng, body):
            with eng.Fori(0, NKV - 1) as g:
                with eng.Fori(0, B - 1) as b:
                    body(g * B + b, g, b, b + 1, False, False)
                body(g * B + B - 1, g, B - 1, 0, True, False)
            body((NKV - 1) * B, NKV - 1, 0, 1, False, False)
            with eng.Fori(1, B - 1) as b:
                body((NKV - 1) * B + b, NKV - 1, b, b + 1, False, False)
            body(UNITS - 1, NKV - 1, B - 1, None, False, True)

        SPLIT_IN_SLOT = [[], [0], [1], [2, 3]]

        HI_UNIT = {}
        for h in range(REP):
            probabilities = [f"A{h}", f"B{h}", f"C{h}"]
            for n in ([f"Q{h}"] + probabilities if h == 0 else probabilities + [f"Q{h}"]) + [f"PV{h}"]:
                HI_UNIT[n] = len(HI_UNIT)
        HI_UNIT["VT"] = len(HI_UNIT)
        HI_UNIT["KN"] = len(HI_UNIT)
        n_hi = len(HI_UNIT)
        HI_FIRST = {}
        for name, _ in FIRST:
            if name[0] in "wxQ" or name == "VT":
                HI_FIRST[name] = len(HI_FIRST)
        HI_FIRST["KN"] = len(HI_FIRST)

        def hi_at(u, g, prep, final, name):
            start = len(HI_FIRST) + u * n_hi + g * len(TILES)
            if name.startswith("w_"):
                t = TILES.index(name[2:])
                return start + t + 1 + (n_hi if t >= len(QKV_TILES) else 0)
            if prep:
                start = start + len(QKV_TILES)
            order = [n for n in HI_UNIT if n[0] in "ABCP"] if final else list(HI_UNIT)
            return start + order.index(name) + 1

        def w_src(t, g, ahead):
            if t in "kv":
                return {"k": Wk, "v": Wv}[t][bass.ds(g * P + ahead * P, P), :]
            n = int(t[1])
            if t[0] == "q":
                return Wq[bass.ds(g * REP * P + (ahead * REP + n) * P, P), :]
            return Wo[n * P:(n + 1) * P, bass.ds(g * REP * HD + ahead * REP * HD, REP * HD)]

        def w_dst(t, hi):
            if t[0] == "o":
                m = int(t[1])
                return (woTh if hi else woTl)[:, :, m * P:(m + 1) * P]
            return (wTh if hi else wTl)[:, TILES.index(t), :].rearrange("p (k n) -> p k n", k=KC)

        def blocks(bank):
            return psum[bank][:, :].rearrange("p (k n) -> p k n", k=4)

        ctx_rows = ctx_in_dram.rearrange("b k n -> (b k) n")

        @block.sync
        def _(sp):
            x_tiles = x.rearrange("b (t p) d -> b p t d", p=P)

            def load_w(g, i, ahead=0):
                sp.dma_start(wstage[:, i % RING, :], w_src(TILES[i], g, ahead)).then_inc(w_in[i % RING], 16)

            def load_x(b):
                sp.dma_start(xres[:, b * TB:(b + 1) * TB, :], x_tiles[b]).then_inc(x_in[b], 16)

            sp.dma_start(qs_col[:, 0:1], q_scale.rearrange("(p a) -> p a", a=1)).then_inc(scales_in, 16)
            sp.dma_start(qs_col[:, 1:2], k_scale.rearrange("(p a) -> p a", a=1)).then_inc(scales_in, 16)
            def transposed(bk, i):
                bank, n = bk.use(f"w_{TILES[i]}")
                sp.wait_ge(bk.filled[bank], n + 1)

            for i in range(RING):
                load_w(0, i)
            load_x(0)
            for i in range(RING, len(TILES)):
                transposed(first, i - RING)
                load_w(0, i)
                if i in (3, 5, 7):
                    load_x((i - 1) // 2)

            def replace_tiles(bk, old, g, ahead, first_tile, end_tile):
                for i in range(first_tile, end_tile):
                    transposed(bk, old + i - first_tile)
                    load_w(g, i, ahead)

            def next_group(g, ahead, bk):
                replace_tiles(bk, len(TILES) - RING, g, ahead, 0, RING)

            def rest_of_group(g, ahead):
                last = g + ahead - 1
                bk = banks(last * B + B - 1, last, True)
                replace_tiles(bk, 0, g, ahead, RING, len(TILES))
                return bk

            next_group(0, 1, first)
            with sp.Fori(0, NKV - 2) as g:
                next_group(g, 2, rest_of_group(g, 1))
            rest_of_group(NKV - 1, 0)

            for r in range(2):
                transposed(banks((NKV - 1) * B - 1, NKV - 2, True), len(TILES) - 2 + r)
                sp.dma_start(wstage[:, r, :], ctx_rows[r * P:(r + 1) * P, :]).then_inc(ctx_in[r], 16)
            with sp.Fori(1, B * KC // 2) as i:
                for r in range(2):
                    sp.wait_ge(ctxq_done, i * 2 + r - 1)
                    sp.dma_start(wstage[:, r, :], ctx_rows[bass.ds(i * 2 * P + r * P, P), :])\
                        .then_inc(ctx_in[r], 16)

            def load_w13(w1_rows, w3_rows, k, wait):
                if wait is not None:
                    sp.wait_ge(w13_low, wait)
                for dst, src in ((slice(0, H), w1_rows), (slice(W3_TAIL, W3_FULL), w3_rows[:, HC * P:H]),
                                 (slice(W3_FULL, W13), w3_rows[:, 0:HC * P])):
                    sp.dma_start(w13st[:, k, dst], src).then_inc(w13_in[k], 16)

            def load_w2(w2_rows, c, wait):
                if wait is not None:
                    sp.wait_ge(w2_low, wait)
                upper, lower = (w2_rows[0:HT, :], w2_rows[HT:P, :]) if c < HC else (w2_rows, w2_rows)
                sp.dma_start(w2st[0:HT, c % 2, :], upper).then_inc(w2_in[c % 2], 16)
                sp.dma_start(w2st[HT:P, c % 2, :], lower).then_inc(w2_in[c % 2], 16)

            def chunk_rows(c):
                return slice(c * P, min(H, (c + 1) * P))

            def expert_rows(w, e, rows):
                return w[bass.ds(e, 1), rows, :].rearrange("a p h -> (a p) h")

            def load_expert_w13(e, n):
                for k in range(KC):
                    rows = slice(k * P, (k + 1) * P)
                    load_w13(expert_rows(W1, e, rows), expert_rows(W3, e, rows), k, (n - 1) * KC + k + 1)

            def load_batch(b):
                sp.dma_start(ctxq[:, :, :], ctxq_dram[bass.ds(b * T, T), :].rearrange("(k p) n -> p k n", p=P))\
                    .then_inc(ctxq_in, 16)
                sp.dma_start(mask_b[:, :], mask_in_rows(b)).then_inc(mask_in, 16)

            def mask_in_rows(b):
                return mask_dram[bass.ds(b, 1), :, :].rearrange("a c n -> (a c n)").partition_broadcast(P)

            sp.wait_ge(norms_done, UNITS)
            for k in range(KC):
                load_w13(sw1[k * P:(k + 1) * P, :], sw3[k * P:(k + 1) * P, :], k, None)
            for c in range(2):
                load_w2(sw2[chunk_rows(c), :], c, None)
            sp.wait_ge(attn_done, 1)
            sp.wait_ge(ctxq_out, 16 * B * KC)
            sp.dma_start(wg[:, :, :], Wg.rearrange("(k p) e -> p k e", p=P)).then_inc(wg_in, 16)
            load_batch(0)
            for c in range(2, NS):
                load_w2(sw2[chunk_rows(c), :], c, c - 1)
            load_expert_w13(0, 1)
            with sp.Fori(1, B) as b:
                sp.wait_ge(mask_read, b * TB)
                load_batch(b)

            def load_tokens(e):
                sp.dma_start(x3n[:, 0:CAP_T, :], sent[bass.ds(e * CAP, CAP), :].rearrange("(t p) d -> p t d", p=P))\
                    .then_inc(expert_in, 16)

            def load_expert_w2(e, n, first_chunk, end_chunk):
                for c in range(first_chunk, end_chunk):
                    load_w2(expert_rows(W2, e, chunk_rows(c)), c, n * NS + c - 1)

            sp.wait_ge(tokens_sent, NT * 16)
            load_tokens(0)

            def tokens_transposed(bk):
                bank, n = bk.use(f"XT{CAP_T - 1}")
                sp.wait_ge(bk.filled[bank], n + 1)

            tokens_transposed(shared_banks(B - 1, False))
            load_tokens(1)
            with sp.Fori(1, NE - 1) as e:
                load_expert_w2(e - 1, e, 0, 2)
                load_expert_w13(e, e + 1)
                load_expert_w2(e - 1, e, 2, NS)
                tokens_transposed(expert_banks(e - 1, True))
                load_tokens(e + 1)
            load_expert_w2(NE - 2, NE - 1, 0, 2)
            load_expert_w13(NE - 1, NE)
            load_expert_w2(NE - 2, NE - 1, 2, NS)
            load_expert_w2(NE - 1, NE, 0, NS)
            out_tiles = out.rearrange("b (t p) d -> b p t d", p=P)
            for b in range(B):
                sp.wait_ge(result_done, b + 1)
                sp.dma_start(out_tiles[b], xres[:, b * TB:(b + 1) * TB, :]).then_inc(stored, 16)
            sp.wait_ge(stored, B * 16)

        @block.gpsimd
        def _(pool):
            nc.gpsimd.memset(ident[:], 0.0).then_inc(pool_step, 1)
            nc.gpsimd.memset(causal[:], 0.0).then_inc(pool_step, 1)
            nc.gpsimd.memset(ones[:], 1.0).then_inc(consts, 1)
            nc.gpsimd.memset(zeros[:], 0.0).then_inc(zeros_set, 1)
            pool.wait_ge(pool_step, 2)
            nc.gpsimd.affine_select(out=ident[:], in_=ident[:], compare_op=ALU.not_equal, fill=1.0, base=0,
                                    pattern=[[-1, P]], channel_multiplier=1).then_inc(pool_step, 1)
            nc.gpsimd.affine_select(out=causal[:], in_=causal[:], compare_op=ALU.is_ge, fill=MASKED, base=0,
                                    pattern=[[-1, P]], channel_multiplier=1).then_inc(consts, 1)
            pool.wait_ge(pool_step, 3)
            nc.gpsimd.tensor_copy(ident_b[:], ident[:]).then_inc(consts, 1)

            ctx_batch = ctx_in_dram.rearrange("b (k p) n -> b p k n", p=P)
            for b in range(2):
                pool.dma_start(ctx_all[:, b, :, :], ctx_batch[b]).then_inc(ctx_all_in[b], 16)
            pool.wait_ge(zeros_set, 1)
            sent_tiles = sent.rearrange("(i t p) d -> i p t d", p=P, t=2)
            for i in range(NE * CAP_T // 2):
                pool.dma_start(sent_tiles[i], zeros[:, :, :]).then_inc(sent_zeroed, 16)
            for b in range(2, B):
                pool.wait_ge(ctx_read, b - 1)
                pool.dma_start(ctx_all[:, b % 2, :, :], ctx_batch[b]).then_inc(ctx_all_in[b % 2], 16)
            pool.wait_ge(ctx_amax, 1)
            nc.gpsimd.partition_all_reduce(amax[:, 1:2], amax[:, 0:1], P, RMAX).then_inc(ctx_amax_all, 1)

            with pool.Fori(0, B * KC) as i:
                pool.wait_ge(ctxq_done, i + 1)
                pool.dma_start(ctxq_dram[bass.ds(i * P, P), :], ctx_q[:, :]).then_inc(ctxq_out, 16)
            pool.wait_ge(x_amax, 1)
            nc.gpsimd.partition_all_reduce(amax[:, 3:4], amax[:, 2:3], P, RMAX).then_inc(x_amax_all, 1)

            nc.gpsimd.memset(ones_b[:], 1.0).then_inc(route_consts, 1)
            nc.gpsimd.memset(tri[:], 1.0).then_inc(pool_step, 1)
            nc.gpsimd.memset(carry[:], 0.0).then_inc(route_consts, 1)
            nc.gpsimd.iota(expert_id[:], [[1, NE]], base=0, channel_multiplier=0,
                           allow_small_or_imprecise_dtypes=True).then_inc(route_consts, 1)
            pool.wait_ge(pool_step, 4)
            nc.gpsimd.affine_select(out=tri[:], in_=tri[:], compare_op=ALU.is_ge, fill=0.0, base=0,
                                    pattern=[[1, P]], channel_multiplier=-1).then_inc(route_consts, 1)

            pool.wait_ge(sent_zeroed, 16 * NE * CAP_T // 2)
            last_row = pool.to_reg(NE * CAP - 1)
            for b in range(B):
                pool.wait_ge(slots_done, b + 1)
                for t in range(TB):
                    pool.indirect_dma_start(
                        out=sent[:, :], out_offset=bass.IndirectOffsetOnAxis(ap=slot_w[:, t:t + 1], axis=0),
                        in_=x3n[:, t, :], in_offset=None, bounds_check=last_row,
                        oob_is_err=False).then_inc(tokens_sent, 16)

            with pool.Fori(0, NE) as e:
                for m in range(CAP_T):
                    bank, n = expert_banks(e, True).use(f"D{m}")
                    pool.wait_ge(mfree[bank], n + 1)
                    pool.dma_start(answered[bass.ds(e * CAP + m * P, P), :], expert_out[:, m, :])\
                        .then_inc(answers_out[m], 16)
            for m in range(CAP_T):
                pool.wait_ge(answers_out[m], 16 * NE)
            for i in range(NT):
                pool.indirect_dma_start(
                    out=gathered[:, i, :], out_offset=None, in_=answered[:, :],
                    in_offset=bass.IndirectOffsetOnAxis(ap=slot_r[:, i:i + 1], axis=0),
                    bounds_check=last_row, oob_is_err=False).then_inc(answers_in[i // TB], 16)

        @block.tensor
        def _(pe):
            mm = nc.tensor.matmul

            def begin(bk, name):
                bank, n = bk.use(name)
                pe.wait_ge(bk.freed[bank], n)
                return psum[bank]

            def end(bk, name, instruction):
                instruction.then_inc(bk.filled[bk.use(name)[0]], 1)

            def landed(bk, name):
                bank, n = bk.use(name)
                pe.wait_ge(bk.freed[bank], n + 1)

            def product(dst, pairs, n=None):
                last = None
                total = 3 * len(pairs)
                i = 0
                for (lh, ll), (rh, rl) in pairs:
                    for a, b_ in ((lh, rh), (ll, rh), (lh, rl)):
                        last = mm(dst, a, b_, start=(i == 0), stop=(i == total - 1))
                        i += 1
                return last

            def weight_tile(bk, g, t):
                i = TILES.index(t)
                pe.wait_ge(w_in[i % RING], (g * (len(TILES) // RING) + i // RING + 1) * 16)
                ps = begin(bk, f"w_{t}")
                for k in range(4):
                    last = nc.tensor.transpose(ps[:, k * P:(k + 1) * P], wstage[:, i % RING, k * P:(k + 1) * P],
                                               ident[:])
                end(bk, f"w_{t}", last)

            def project(bk, name, tile, b):
                ps = begin(bk, name)
                w = TILES.index(tile)
                last = product(ps[:, :], [
                    ((wTh[:, w, k * P:(k + 1) * P], wTl[:, w, k * P:(k + 1) * P]),
                     (xTh[:, k, bass.ds(b * T, T)], xTl[:, k, bass.ds(b * T, T)])) for k in range(KC)])
                end(bk, name, last)

            def scores(u, h, first_ever=False):
                for j in range(TB):
                    if not first_ever:
                        pe.wait_ge(exp_done, 16 * u + 4 * h + j - 3)
                    n = (j + 1) * P
                    qj = slice(j * P, n)
                    mm(psum[j][:, 0:n], qTh[:, h, qj], kTh[:, 0:n], start=True, stop=False)
                    mm(psum[j][:, j * P:n], ident_b[:], causal[:], start=False, stop=False,
                       skip_group_check=True)
                    mm(psum[j][:, 0:n], qTl[:, h, qj], kTh[:, 0:n], start=False, stop=False)
                    mm(psum[j][:, 0:n], qTh[:, h, qj], kTl[:, 0:n], start=False,
                       stop=True).then_inc(s_filled, 1)

            def sums_of_squares(bk, h, sq_n, with_k):
                pe.wait_ge(sq_done, sq_n)
                if with_k:
                    landed(bk, "K")
                ps = begin(bk, f"SS{h}")
                for c in range(8 if with_k else 4):
                    src = qsq if c < 4 else ksq
                    last = mm(ps[:, c:c + 1], src[:, (c % 4) * P:(c % 4 + 1) * P], ones[:, 0:1],
                              start=True, stop=True)
                end(bk, f"SS{h}", last)

            def value_blocks(bk):
                ps = begin(bk, "VT")
                for s in range(TB):
                    last = nc.tensor.transpose(ps[:, s * P:(s + 1) * P], vraw[:, s * P:(s + 1) * P], ident[:])
                end(bk, "VT", last)

            def key_scale_rows(bk):
                ps = begin(bk, "RK")
                for s in range(TB):
                    last = nc.tensor.transpose(ps[:, s * P:(s + 1) * P],
                                               sc[:, 16 + s:17 + s].to_broadcast([P, P]), ident[:])
                end(bk, "RK", last)

            pe.wait_ge(consts, 3)
            for t in TILES:
                weight_tile(first, 0, t)
            n_x = 0
            for b in range(B):
                if b == 1:
                    for t in range(TB):
                        landed(first, f"x0{t}")
                    for t in QKV_TILES:
                        landed(first, f"w_{t}")
                    project(first, "V", "v", 0)
                    project(first, "K", "k", 0)
                    for h in range(REP):
                        project(first, f"Q{h}", f"q{h}", 0)
                        sums_of_squares(first, h, h + 1, h == REP - 1)
                    value_blocks(first)
                    pe.wait_ge(norms_done, 1)
                    key_scale_rows(first)
                for t in range(TB):
                    pe.wait_ge(xn_done, n_x + 1)
                    ps = begin(first, f"x{b}{t}")
                    for k in range(KC):
                        last = nc.tensor.transpose(ps[:, k * P:(k + 1) * P], xn[:, n_x % 2, k * P:(k + 1) * P],
                                                   ident[:])
                    end(first, f"x{b}{t}", last)
                    n_x += 1
            for t in range(TB):
                landed(first, f"x{B - 1}{t}")
            landed(first, "VT")
            pe.wait_ge(k_ready, 1)
            scores(0, 0, True)

            def unit(u, g, b, b_next, prep, final):
                bk = banks(u, g, prep, final)
                if prep:
                    for t in QKV_TILES:
                        weight_tile(bk, g + 1, t)
                for h in range(REP):
                    if h == 0 and not final:
                        if prep:
                            for t in QKV_TILES:
                                landed(bk, f"w_{t}")
                        project(bk, "Q0", "q0", b_next)
                    if h < REP - 1:
                        scores(u, h + 1)
                    pe.wait_ge(norm_done, 4 * u + h + 1)
                    for c in "ABC":
                        start, _, keys = CHUNKS[c]
                        ps = begin(bk, f"{c}{h}")
                        for s in keys:
                            for t in range(s, TB):
                                col = PT_OFF[s] - start + (t - s) * P
                                src = P_OFF[t] + s * P
                                last = nc.tensor.transpose(ps[:, col:col + P], probs[:, src:src + P], ident[:])
                        end(bk, f"{c}{h}", last)
                    if not final:
                        if h:
                            project(bk, f"Q{h}", f"q{h}", b_next)
                        if h == 0:
                            project(bk, "V", "v", b_next)
                        if h == 2:
                            project(bk, "K", "k", b_next)
                    ps = begin(bk, f"PV{h}")
                    steps = 0
                    for s, c in ((0, "A"), (1, "B"), (3, "B"), (2, "C")):
                        landed(bk, f"{c}{h}")
                        n = (TB - s) * P
                        cols = slice(PT_OFF[s], PT_OFF[s] + n)
                        for a, p_ in ((vh, pTh), (vl, pTh), (vh, pTl)):
                            last = mm(ps[:, s * P:T], a[:, s, :], p_[:, cols], start=(steps == 0),
                                      stop=(steps == 11), skip_group_check=True)
                            steps += 1
                    end(bk, f"PV{h}", last)
                    if not final:
                        sums_of_squares(bk, h, REP * (u + 1) + h + 1, h == REP - 1)
                if not final:
                    value_blocks(bk)
                for m in range(TB):
                    if m == 2 and not final:
                        pe.wait_ge(norms_done, u + 2)
                        key_scale_rows(bk)
                    if m == 3 and not final:
                        landed(bk, "VT")
                        pe.wait_ge(k_ready, u + 2)
                        scores(u + 1, 0)
                    ps = begin(bk, f"O{m}")
                    if m == 0:
                        landed(bk, f"PV{REP - 1}")
                    last = product(ps[:, :], [
                        ((oTh[:, h, m * P:(m + 1) * P], oTl[:, h, m * P:(m + 1) * P]),
                         (woTh[:, h, :], woTl[:, h, :])) for h in range(REP)])
                    end(bk, f"O{m}", last)
                if prep:
                    for t in O_TILES:
                        weight_tile(bk, g + 1, t)
                    for t in O_TILES:
                        landed(bk, f"w_{t}")

            units(pe, unit)

            def token_quantised_blocks(bk, t, n):
                pe.wait_ge(quantised, n + 1)
                ps = begin(bk, f"QT{t}").bitcast(BF16)
                for k in range(KC):
                    last = nc.tensor.transpose(ps[:, k * P:(k + 1) * P], tokens_q[:, t % 2, k * P:(k + 1) * P],
                                               ident_b[:])
                end(bk, f"QT{t}", last)

            def cross_attention(bk, t, b):
                landed(bk, f"QT{t}")
                pe.wait_ge(ctxq_in, 16 * (b + 1))
                ps = begin(bk, f"XA{t}")
                for k in range(KC):
                    last = mm(ps[:, :], tokens_qT[:, t % 2, k, :], ctxq[:, k, :], start=(k == 0), stop=(k == KC - 1))
                end(bk, f"XA{t}", last)

            def token_blocks(bk, t):
                ps = begin(bk, f"XT{t}")
                for k in range(KC):
                    last = nc.tensor.transpose(ps[:, k * P:(k + 1) * P], x3n[:, t, k * P:(k + 1) * P], ident[:])
                end(bk, f"XT{t}", last)

            def router(bk):
                for t in range(TB):
                    landed(bk, f"XT{t}")
                ps = begin(bk, "RT")
                for t in range(TB):
                    for k in range(KC):
                        for i, (a, w) in enumerate(((xh, wgh), (xl, wgh), (xh, wgl))):
                            last = mm(ps[:, t * NE:(t + 1) * NE], a[:, k, t * P:(t + 1) * P], w[:, k, :],
                                      start=(t + k + i == 0), stop=(k == KC - 1 and i == 2),
                                      skip_group_check=True)
                end(bk, "RT", last)

            def count_tokens(bk, b):
                pe.wait_ge(onehot_done, b + 1)
                ps = begin(bk, "CS")
                oh = onehot[:, :, :].rearrange("p t e -> p (t e)")
                n = TB * NE
                mm(ps[:, 0:n], tri[:], oh[:, 0:n], start=True, stop=False, skip_group_check=True)
                for s in range(1, TB):
                    mm(ps[:, s * NE:n], ones_b[:], oh[:, 0:n - s * NE], start=False, stop=False,
                       skip_group_check=True)
                for t in range(TB):
                    last = mm(ps[:, n:n + NE], ones_b[:], oh[:, t * NE:(t + 1) * NE], start=False,
                              stop=(t == TB - 1), skip_group_check=True)
                end(bk, "CS", last)

            def hidden_products(bk, n_tok, n_set, between):
                def part(name, col):
                    ps = begin(bk, name)
                    steps = 0
                    for k in range(KC):
                        if name == "a0":
                            pe.wait_ge(w13_low, n_set * KC + k + 1)
                        for w, x_ in ((w13h, xh), (w13l, xh), (w13h, xl)):
                            last = mm(ps[:, 0:n_tok], w[:, k, col:col + P], x_[:, k, 0:n_tok],
                                      start=(steps == 0), stop=(steps == 3 * KC - 1))
                            steps += 1
                    end(bk, name, last)

                for c in range(HC):
                    part(f"a{c}", c * P)
                    part(f"b{c}", W3_FULL + c * P)
                    between(c)
                part("ab", HC * P)

            def down(bk, m, n_set, n_body):
                ps = begin(bk, f"D{m}")
                rows = slice(m * P, (m + 1) * P)
                if m == 0:
                    pe.wait_ge(w2_low, (n_set + 1) * NS)
                    pe.wait_ge(hl_done, n_body * NS + HC)
                for c in range(HC):
                    for i, (a, w) in enumerate(((hh, w2h), (hl, w2h), (hh, w2l))):
                        mm(ps[:, :], a[:, c, rows], w[:, c, :], start=(c + i == 0), stop=False)
                if m == 0:
                    pe.wait_ge(hl_done, n_body * NS + NS)
                mm(ps[:, :], hh[:, HC, rows], w2h[:, HC, :], start=False, stop=False)
                end(bk, f"D{m}", mm(ps[:, :], hh[:, HC, rows], w2l[:, HC, :], start=False, stop=True))

            for t in range(TB):
                token_quantised_blocks(before, t, t)
                cross_attention(before, t, 0)
            for t in range(TB):
                pe.wait_ge(x3n_done, t + 1)
                token_blocks(before, t)
            pe.wait_ge(wg_low, 1)
            router(before)
            pe.wait_ge(route_consts, 4)

            def shared(b, ahead):
                bk = shared_banks(b, ahead)

                def between(c):
                    if c == 0:
                        count_tokens(bk, b)
                    if ahead:
                        if c < TB:
                            token_quantised_blocks(bk, c, (b + 1) * TB + c)
                        if c:
                            cross_attention(bk, c - 1, b + 1)

                hidden_products(bk, T, 0, between)
                down(bk, 0, 0, b)
                down(bk, 1, 0, b)
                if not ahead:
                    pe.wait_ge(expert_in, 16)
                for t in range(TB if ahead else CAP_T):
                    if ahead:
                        pe.wait_ge(x3n_done, (b + 1) * TB + t + 1)
                    token_blocks(bk, t)
                down(bk, 2, 0, b)
                down(bk, 3, 0, b)
                if ahead:
                    router(bk)
                else:
                    for t in range(CAP_T):
                        landed(bk, f"XT{t}")

            with pe.Fori(0, B - 1) as b:
                shared(b, True)
            shared(B - 1, False)

            def expert(e, ahead):
                bk = expert_banks(e, ahead)
                hidden_products(bk, CAP, e + 1, lambda c: None)
                if ahead:
                    pe.wait_ge(expert_in, 16 * (e + 2))
                    for t in range(CAP_T):
                        token_blocks(bk, t)
                for m in range(CAP_T):
                    down(bk, m, e + 1, B + e)
                if ahead:
                    for t in range(CAP_T):
                        landed(bk, f"XT{t}")

            with pe.Fori(0, NE - 1) as e:
                expert(e, True)
            expert(NE - 1, False)

        @block.scalar
        def _(act):
            A = nc.scalar.activation

            def full(bk, name):
                bank, n = bk.use(name)
                act.wait_ge(bk.filled[bank], n + 1)
                return psum[bank]

            def high(dst, src):
                A(dst, src, ACT.Copy).then_inc(hi_done, 1)

            def weight_tile(bk, t):
                full(bk, f"w_{t}")
                high(w_dst(t, True), blocks(bk.use(f"w_{t}")[0]))

            def query_head(bk, h, ready_ss):
                ps = full(bk, f"Q{h}")
                high(qTh[:, h, :], ps[:, :])
                ready_ss()
                A(qsq[:], ps[:, :], ACT.Square).then_inc(sq_done, 1)

            def keep(bk, name, dst, sq=None):
                ps = full(bk, name)
                bank = bk.use(name)[0]
                last = A(dst[:], ps[:, :], ACT.Copy)
                if sq is not None:
                    last = A(sq[:], ps[:, :], ACT.Square)
                last.then_inc(bk.freed[bank], 1)

            def normed_keys_high(bk):
                bank, n = bk.use("RK")
                act.wait_ge(bk.freed[bank], n + 1)
                high(kTh[:], kraw[:])

            def w13_high_part(k, n):
                act.wait_ge(w13_in[k], 48 * (n + 1))
                A(w13h[:, k, :], w13st[:, k, :], ACT.Copy).then_inc(w13_high, 1)

            for name, bank in FIRST:
                if name[0] == "w":
                    weight_tile(first, name[2:])
                elif name[0] == "x":
                    b, t = int(name[1]), int(name[2])
                    full(first, name)
                    high(xTh[:, :, (b * TB + t) * P:(b * TB + t + 1) * P], blocks(bank))
                elif name == "V":
                    keep(first, "V", vraw)
                elif name == "K":
                    keep(first, "K", kraw, ksq)
                elif name[0] == "Q":
                    h = int(name[1])
                    query_head(first, h, lambda: full(first, f"SS{h - 1}") if h else None)
                elif name == "VT":
                    full(first, "VT")
                    high(vh[:, :, :], blocks(bank))
            normed_keys_high(first)

            def softmax_exp(u, h):
                for j in range(TB):
                    c = 4 * h + j
                    if j % 2 == 0:
                        act.wait_ge(bias_done, 8 * u + 2 * h + j // 2 + 1)
                    A(probs[:, P_OFF[j]:P_OFF[j + 1]], psum[j][:, 0:(j + 1) * P], ACT.Exp,
                      bias=nbias[:, c:c + 1], scale=sc[:, c:c + 1],
                      accum_out=rowsum[:, c:c + 1]).then_inc(exp_done, 1)

            def unit(u, g, b, b_next, prep, final):
                bk = banks(u, g, prep, final)
                if prep:
                    for t in QKV_TILES:
                        weight_tile(bk, t)
                for h in range(REP):
                    if h == 0 and not final:
                        query_head(bk, 0, lambda: None)
                    for c in "ABC":
                        start, n, _ = CHUNKS[c]
                        ps = full(bk, f"{c}{h}")
                        high(pTh[:, start:start + n], ps[:, 0:n])
                    if h < REP - 1:
                        softmax_exp(u, h + 1)
                    if not final:
                        if h:
                            query_head(bk, h, lambda: full(bk, f"SS{h - 1}"))
                        if h == 0:
                            keep(bk, "V", vraw)
                        if h == 2:
                            keep(bk, "K", kraw, ksq)
                    ps = full(bk, f"PV{h}")
                    high(oTh[:, h, :], ps[:, :])
                    if final:
                        for k in SPLIT_IN_SLOT[h]:
                            w13_high_part(k, 0)
                if not final:
                    full(bk, "VT")
                    high(vh[:, :, :], blocks(bk.use("VT")[0]))
                    normed_keys_high(bk)
                    softmax_exp(u + 1, 0)
                if prep:
                    for t in O_TILES:
                        weight_tile(bk, t)

            softmax_exp(0, 0)
            units(act, unit)

            def w2_high_part(c, n):
                act.wait_ge(w2_in[c % 2], 32 * (n * (NS // 2) + c // 2 + 1))
                A(w2h[:, c, :], w2st[:, c % 2, :], ACT.Copy).then_inc(w2_high, 1)

            def quantised_blocks(bk, t):
                ps = full(bk, f"QT{t}").bitcast(BF16)
                A(tokens_qT[:, t % 2, :, :], ps[:, 0:D].rearrange("p (k n) -> p k n", k=KC), ACT.Copy)\
                    .then_inc(bk.freed[bk.use(f"QT{t}")[0]], 1)

            def tokens_high(bk, t):
                full(bk, f"XT{t}")
                A(xh[:, :, t * P:(t + 1) * P], blocks(bk.use(f"XT{t}")[0]), ACT.Copy).then_inc(xh_done, 1)

            def router_exp(b):
                act.wait_ge(logits_less_max, b + 1)
                A(le[:, :, :], lt[:, :, :], ACT.Exp).then_inc(logits_exp, 1)

            def hidden_act(bk, c, n_tok):
                name, rows = (f"a{c}", P) if c < HC else ("ab", HT)
                ps = full(bk, name)
                last = A(gate_act[0:rows, c % 2, 0:n_tok], ps[0:rows, 0:n_tok], ACT.Silu)
                last.then_inc(bk.freed[bk.use(name)[0]] if c < HC else act_done, 1)

            def hidden_high(bk, c, n_tok):
                rows = P if c < HC else HT
                bank, n = bk.use(f"b{c}" if c < HC else "ab")
                act.wait_ge(bk.freed[bank], n + 1)
                A(hh[0:rows, c, 0:n_tok], hid[0:rows, c % 2, 0:n_tok], ACT.Copy).then_inc(hh_done, 1)

            act.wait_ge(attn_done, 1)
            for t in range(TB):
                w2_high_part(t, 0)
                quantised_blocks(before, t)
            act.wait_ge(wg_in, 16)
            A(wgh[:, :, :], wg[:, :, :], ACT.Copy).then_inc(wg_high, 1)
            for t in range(TB):
                tokens_high(before, t)
            for c in range(TB, NS):
                w2_high_part(c, 0)
            router_exp(0)

            def shared(b, ahead):
                bk = shared_banks(b, ahead)
                for c in range(NS):
                    hidden_act(bk, c, T)
                    if ahead and c < TB:
                        quantised_blocks(bk, c)
                    hidden_high(bk, c, T)
                if ahead:
                    for t in range(TB):
                        tokens_high(bk, t)
                    router_exp(b + 1)
                else:
                    for k in range(2):
                        w13_high_part(k, 1)
                    for t in range(CAP_T):
                        tokens_high(bk, t)
                    for k in range(2, KC):
                        w13_high_part(k, 1)

            with act.Fori(0, B - 1) as b:
                shared(b, True)
            shared(B - 1, False)

            def expert(e, ahead, first=False):
                bk = expert_banks(e, ahead)
                for c in range(NS):
                    hidden_act(bk, c, CAP)
                    w2_high_part(c, e + 1)
                    hidden_high(bk, c, CAP)
                if ahead:
                    for k in range(2):
                        w13_high_part(k, e + 2)
                    for t in range(CAP_T):
                        tokens_high(bk, t)
                for m in range(CAP_T):
                    ps = full(bk, f"D{m}")
                    if not first:
                        act.wait_ge(answers_out[m], 16 * e)
                    A(expert_out[:, m, :], ps[:, :], ACT.Copy)\
                        .then_inc(bk.freed[bk.use(f"D{m}")[0]], 1)
                    if ahead:
                        w13_high_part(m + 2, e + 2)

            expert(0, True, True)
            with act.Fori(1, NE - 1) as e:
                expert(e, True)
            expert(NE - 1, False)

        @block.vector
        def _(dve):
            V = nc.vector

            def full(bk, name):
                bank, n = bk.use(name)
                dve.wait_ge(bk.filled[bank], n + 1)
                return psum[bank]

            def low(bk, name, dst, src, hi_src, hi_count):
                dve.wait_ge(hi_done, hi_count)
                V.tensor_tensor(dst, src, hi_src.bitcast(F32), ALU.subtract)\
                    .then_inc(bk.freed[bk.use(name)[0]], 1)

            def weight_low(bk, t, n):
                bank = bk.use(f"w_{t}")[0]
                low(bk, f"w_{t}", w_dst(t, False), blocks(bank), w_dst(t, True), n)

            def flat(ap):
                return ap.rearrange("p a d -> p (a d)")

            def inverse_root(y, n, src, scale, eps):
                v, t = chain_v[:, 0:n], chain_t[:, 0:n]
                V.tensor_scalar(v, src, scale, eps, ALU.mult, ALU.add)
                dve.drain()
                V.tensor_scalar(y.bitcast(I32), v.bitcast(I32), 1, None, ALU.logical_shift_right)
                dve.drain()
                V.tensor_scalar(y.bitcast(I32), y.bitcast(I32), -1.0, float(0x5F3759DF), ALU.mult, ALU.add)
                for _ in range(4):
                    dve.drain()
                    V.tensor_tensor(t, v, y, ALU.mult)
                    dve.drain()
                    V.tensor_tensor(t, t, y, ALU.mult)
                    dve.drain()
                    V.tensor_scalar(t, t, -0.5, 1.5, ALU.mult, ALU.add)
                    dve.drain()
                    last = V.tensor_tensor(y, y, t, ALU.mult)
                dve.drain()
                return last

            def layer_norm_rows(t0):
                for t in range(TB):
                    V.bn_stats(stats[:, t, :], flat(xres[:, bass.ds(t0 + t, 1), :]))
                dve.drain()
                for t in range(TB):
                    V.bn_aggr(mv[:, t, :], stats[:, t, :])
                dve.drain()
                V.tensor_copy(mean[:, bass.ds(t0, TB)], flat(mv[:, :, 0:1]))
                inverse_root(rstd[:, bass.ds(t0, TB)], TB, flat(mv[:, :, 1:2]), 1.0, LN_EPS)

            def query_low(bk, h, n, n_sq):
                dve.wait_ge(sq_done, n_sq)
                low(bk, f"Q{h}", qTl[:, h, :], psum[bk.use(f"Q{h}")[0]][:, :], qTh[:, h, :], n)

            def take_sums(bk, h):
                ps = full(bk, f"SS{h}")
                V.tensor_copy(ss[:, 4 * h:4 * h + (8 if h == REP - 1 else 4)],
                              ps[:, 0:8 if h == REP - 1 else 4]).then_inc(bk.freed[bk.use(f"SS{h}")[0]], 1)

            def key_norms():
                dve.drain()
                inverse_root(sc[:, :], 20, ss[:, :], 1.0 / HD, QK_EPS)
                V.tensor_scalar(sc[:, 0:16], sc[:, 0:16], SCALE, None, ALU.mult).then_inc(norms_done, 1)

            def normed_keys(bk):
                ps = full(bk, "RK")
                V.scalar_tensor_tensor(out=kraw[:], in0=kraw[:], scalar=qk_scale[:, 0:1], in1=ps[:, :],
                                       op0=ALU.mult, op1=ALU.mult).then_inc(bk.freed[bk.use("RK")[0]], 1)

            def keys_low(bk, n):
                dve.wait_ge(hi_done, n)
                V.tensor_tensor(kTl[:], kraw[:], kTh[:].bitcast(F32), ALU.subtract).then_inc(k_ready, 1)

            dve.wait_ge(scales_in, 32)
            V.tensor_tensor(qk_scale[:], qs_col[:, 0:1], qs_col[:, 1:2], ALU.mult)

            def normalise(b, t):
                i = b * TB + t
                if i >= 2:
                    full(first, f"x{(i - 2) // TB}{(i - 2) % TB}")
                V.tensor_scalar(xn[:, i % 2, :], xres[:, i, :], mean[:, i:i + 1], rstd[:, i:i + 1],
                                ALU.subtract, ALU.mult).then_inc(xn_done, 1)

            def x_low(b, t):
                cols = slice((b * TB + t) * P, (b * TB + t + 1) * P)
                name = f"x{b}{t}"
                low(first, name, xTl[:, :, cols], blocks(first.use(name)[0]), xTh[:, :, cols],
                    HI_FIRST[name] + 1)

            for t in TILES:
                weight_low(first, t, HI_FIRST[f"w_{t}"] + 1)
            for b in range(B):
                dve.wait_ge(x_in[b], 16)
                layer_norm_rows(b * TB)
                if b == 1:
                    for h in range(REP):
                        query_low(first, h, HI_FIRST[f"Q{h}"] + 1, h + 1)
                        take_sums(first, h)
                    low(first, "VT", vl[:, :, :], blocks(first.use("VT")[0]), vh[:, :, :], HI_FIRST["VT"] + 1)
                    key_norms()
                    normed_keys(first)
                for t in range(TB):
                    normalise(b, t)
                    if t:
                        x_low(b, t - 1)
                x_low(b, TB - 1)
            keys_low(first, HI_FIRST["KN"] + 1)

            for b in range(B):
                dve.wait_ge(ctx_all_in[b % 2], 16 * (b // 2 + 1))
                of_batch = ctx_all[:, b % 2, :, :].rearrange("p k n -> p (k n)")
                V.tensor_reduce(ctx_part[:, 0, b:b + 1], of_batch, AX.X, ALU.max)
                V.tensor_reduce(ctx_part[:, 1, b:b + 1], of_batch, AX.X, ALU.min).then_inc(ctx_read, 1)

            def largest_magnitude(most, least, dst):
                dve.drain()
                V.tensor_reduce(extremes[:, 0:1], most, AX.X, ALU.max)
                V.tensor_reduce(extremes[:, 1:2], least, AX.X, ALU.min)
                dve.drain()
                return V.scalar_tensor_tensor(out=dst, in0=extremes[:, 1:2], scalar=-1.0, in1=extremes[:, 0:1],
                                              op0=ALU.mult, op1=ALU.max)

            largest_magnitude(ctx_part[:, 0, :], ctx_part[:, 1, :], amax[:, 0:1]).then_inc(ctx_amax, 1)

            def scale_from(src, dst):
                V.tensor_scalar(dst, src, FP8_EPS, None, ALU.max)
                dve.drain()
                V.reciprocal(dst, dst)
                dve.drain()
                V.tensor_scalar(dst, dst, FP8_MAX, None, ALU.mult)
                dve.drain()

            dve.wait_ge(ctx_amax_all, 1)
            scale_from(amax[:, 1:2], f8scale[:, 0:1])
            dve.wait_ge(sent_zeroed, 16 * NE * CAP_T // 2)

            def to_fp8(y, m, scale, dst):
                V.tensor_scalar(y, y, scale, FP8_MAX, ALU.mult, ALU.min)
                dve.drain()
                V.tensor_scalar(m.bitcast(I32), y.bitcast(I32), EXPONENT, None, ALU.bitwise_and)
                dve.drain()
                V.tensor_scalar(m, m, FP8_LEAST, ROUND_AT, ALU.max, ALU.mult)
                dve.drain()
                V.scalar_tensor_tensor(out=y, in0=y, scalar=-FP8_MAX, in1=m, op0=ALU.max, op1=ALU.add)
                dve.drain()
                return V.tensor_tensor(dst, y, m, ALU.subtract)

            def quantise_ctx(b, i):
                dve.wait_ge(ctx_in[i % 2], 16 * (b * (KC // 2) + i // 2 + 1))
                dve.wait_ge(ctxq_out, 16 * (b * KC + i))
                for half in range(2):
                    cols = slice(half * D // 2, (half + 1) * D // 2)
                    last = to_fp8(wstage[:, i % 2, cols], ctx_m[:], f8scale[:, 0:1], ctx_q[:, cols])
                last.then_inc(ctxq_done, 1)

            def row_extremes(t):
                row = xres[:, bass.ds(t, 1), :].rearrange("p a d -> p (a d)")
                V.tensor_reduce(rowmax[:, bass.ds(t, 1)], row, AX.X, ALU.max)
                V.tensor_reduce(rowmin[:, bass.ds(t, 1)], row, AX.X, ALU.min)

            def w13_low_part(k, n):
                dve.wait_ge(w13_high, n * KC + k + 1)
                V.tensor_tensor(w13l[:, k, :], w13st[:, k, :], w13h[:, k, :].bitcast(F32), ALU.subtract)\
                    .then_inc(w13_low, 1)

            def softmax_max(u, h):
                for j in range(TB):
                    c = 4 * h + j
                    dve.wait_ge(s_filled, 16 * u + c + 1)
                    V.tensor_reduce(mx[:, c:c + 1], psum[j][:, 0:(j + 1) * P], AX.X, ALU.max)
                    if j % 2:
                        dve.drain()
                        V.scalar_tensor_tensor(out=nbias[:, c - 1:c + 1], in0=mx[:, c - 1:c + 1], scalar=-1.0,
                                               in1=sc[:, c - 1:c + 1], op0=ALU.mult, op1=ALU.mult)\
                            .then_inc(bias_done, 1)

            def softmax_norm(u, h):
                dve.wait_ge(exp_done, 16 * u + 4 * h + 4)
                V.reciprocal(rinv[:, 0:4], rowsum[:, 4 * h:4 * h + 4])
                dve.drain()
                for j in range(TB):
                    cols = slice(P_OFF[j], P_OFF[j + 1])
                    last = V.tensor_scalar(probs[:, cols], probs[:, cols], rinv[:, j:j + 1], None, ALU.mult)
                last.then_inc(norm_done, 1)

            def unit(u, g, b, b_next, prep, final):
                bk = banks(u, g, prep, final)

                last_group = isinstance(g, int)
                previous_norm = last_group and not (isinstance(b, int) and b == 0)

                def hi(name):
                    return hi_at(u, g, prep, final, name)

                if prep:
                    for t in QKV_TILES:
                        weight_low(bk, t, hi(f"w_{t}"))
                for h in range(REP):
                    if h == 0 and not final:
                        query_low(bk, 0, hi("Q0"), REP * (u + 1) + 1)
                    if h < REP - 1:
                        softmax_max(u, h + 1)
                    for c in "ABC":
                        start, n, _ = CHUNKS[c]
                        low(bk, f"{c}{h}", pTl[:, start:start + n], psum[bk.use(f"{c}{h}")[0]][:, 0:n],
                            pTh[:, start:start + n], hi(f"{c}{h}"))
                    if h and not final:
                        query_low(bk, h, hi(f"Q{h}"), REP * (u + 1) + h + 1)
                    if h < REP - 1:
                        softmax_norm(u, h + 1)
                    low(bk, f"PV{h}", oTl[:, h, :], psum[bk.use(f"PV{h}")[0]][:, :], oTh[:, h, :], hi(f"PV{h}"))
                    if not final:
                        take_sums(bk, h)
                    if last_group:
                        quantise_ctx(b, h)
                        if previous_norm:
                            row_extremes((b - 1) * TB + h)
                    if final:
                        for k in SPLIT_IN_SLOT[h]:
                            w13_low_part(k, 0)
                if not final:
                    low(bk, "VT", vl[:, :, :], blocks(bk.use("VT")[0]), vh[:, :, :], hi("VT"))
                    key_norms()

                def add(m, signal=None):
                    ps = full(bk, f"O{m}")
                    row = xres[:, bass.ds(b * TB + m, 1), :].rearrange("p a d -> p (a d)")
                    V.tensor_tensor(row, row, ps[:, :], ALU.add).then_inc(signal or bk.freed[bk.use(f"O{m}")[0]], 1)

                add(0)
                add(1)
                if not final:
                    normed_keys(bk)
                    keys_low(bk, hi("KN"))
                add(2)
                if not final:
                    softmax_max(u + 1, 0)
                add(3, attn_done if final else None)
                if not final:
                    softmax_norm(u + 1, 0)
                if previous_norm:
                    layer_norm_rows((b - 1) * TB)
                if prep:
                    for t in O_TILES:
                        weight_low(bk, t, hi(f"w_{t}"))

            softmax_max(0, 0)
            softmax_norm(0, 0)
            units(dve, unit)

            dve.drain()
            for h in range(TB):
                row_extremes((B - 1) * TB + h)
            layer_norm_rows((B - 1) * TB)
            for e in (rowmax, rowmin):
                V.tensor_tensor(e[:], e[:], mean[:], ALU.subtract)
            dve.drain()
            for e in (rowmax, rowmin):
                V.tensor_tensor(e[:], e[:], rstd[:], ALU.mult)
            largest_magnitude(rowmax[:], rowmin[:], amax[:, 2:3]).then_inc(x_amax, 1)
            dve.wait_ge(x_amax_all, 1)
            scale_from(amax[:, 3:4], f8scale[:, 1:2])
            V.tensor_scalar(f8scale[:, 3:4], amax[:, 1:2], FP8_EPS, 1.0 / FP8_MAX, ALU.max, ALU.mult)
            V.tensor_scalar(f8scale[:, 2:3], amax[:, 3:4], FP8_EPS, 1.0 / FP8_MAX, ALU.max, ALU.mult)
            dve.drain()
            V.tensor_tensor(f8scale[:, 2:3], f8scale[:, 2:3], f8scale[:, 3:4], ALU.mult)
            dve.drain()

            def quantise_tokens(tile, t):
                V.tensor_scalar(q_y[:], flat(xres[:, bass.ds(tile, 1), :]),
                                mean[:, bass.ds(tile, 1)], rstd[:, bass.ds(tile, 1)],
                                ALU.subtract, ALU.mult)
                dve.drain()
                to_fp8(q_y[:], q_m[:], f8scale[:, 1:2], tokens_q[:, t % 2, :]).then_inc(quantised, 1)
                dve.drain()

            def add_cross_attention(bk, tile, t, b):
                ps = full(bk, f"XA{t}")
                dve.wait_ge(mask_read, b * TB + t)
                dve.wait_ge(mask_in, 16 * (b + 1))
                V.scalar_tensor_tensor(out=attended[:], in0=ps[:, :], scalar=f8scale[:, 2:3], in1=mask_b[:],
                                       op0=ALU.mult, op1=ALU.add).then_inc(bk.freed[bk.use(f"XA{t}")[0]], 1)
                dve.drain()
                row = flat(xres[:, bass.ds(tile, 1), :])
                V.tensor_tensor(row, row, attended[:], ALU.add).then_inc(mask_read, 1)

            def normalise_batch(b, first_batch=False):
                dve.drain()
                layer_norm_rows(b * TB)
                if not first_batch:
                    dve.wait_ge(tokens_sent, 16 * TB * b)
                for t in range(TB):
                    tile = b * TB + t
                    V.tensor_scalar(x3n[:, t, :], flat(xres[:, bass.ds(tile, 1), :]),
                                    mean[:, bass.ds(tile, 1)], rstd[:, bass.ds(tile, 1)],
                                    ALU.subtract, ALU.mult).then_inc(x3n_done, 1)

            def tokens_low(bk, t, n):
                dve.wait_ge(xh_done, n)
                name = f"XT{t}"
                cols = slice(t * P, (t + 1) * P)
                V.tensor_tensor(xl[:, :, cols], blocks(bk.use(name)[0]), xh[:, :, cols].bitcast(F32),
                                ALU.subtract).then_inc(bk.freed[bk.use(name)[0]], 1)

            def over_experts(ap):
                return ap.rearrange("p (t a) -> p t a", a=1).to_broadcast([P, TB, NE])

            def over_tiles(ap):
                return ap.rearrange("p (a e) -> p a e", a=1).to_broadcast([P, TB, NE])

            def choose_expert(bk, b):
                ps = full(bk, "RT")
                V.tensor_copy(lg[:].rearrange("p t e -> p (t e)"), ps[:, 0:TB * NE])\
                    .then_inc(bk.freed[bk.use("RT")[0]], 1)
                dve.drain()
                V.tensor_reduce(r_max[:], lg[:], AX.X, ALU.max)
                dve.drain()
                V.tensor_tensor(lt[:], lg[:], over_experts(r_max[:]), ALU.subtract).then_inc(logits_less_max, 1)
                dve.drain()
                V.tensor_scalar(pos[:], lt[:], 0.0, float(NE), ALU.is_lt, ALU.mult)
                dve.drain()
                V.tensor_tensor(pos[:], pos[:], over_tiles(expert_id[:]), ALU.add)
                dve.drain()
                V.tensor_reduce(r_idx[:], pos[:], AX.X, ALU.min)
                dve.drain()
                V.tensor_tensor(onehot[:], over_tiles(expert_id[:]), over_experts(r_idx[:]), ALU.is_equal)\
                    .then_inc(onehot_done, 1)
                dve.wait_ge(logits_exp, b + 1)
                V.tensor_reduce(r_sum[:], le[:], AX.X, ALU.add)
                dve.drain()
                V.reciprocal(gates[:, bass.ds(b * TB, TB)], r_sum[:])

            def place_tokens(bk, b):
                ps = full(bk, "CS")
                n = TB * NE
                V.tensor_tensor(pos[:], ps[:, 0:n].rearrange("p (t e) -> p t e", e=NE), over_tiles(carry[:]),
                                ALU.add)
                dve.drain()
                V.tensor_tensor(carry[:], ps[:, n:n + NE], carry[:], ALU.add)\
                    .then_inc(bk.freed[bk.use("CS")[0]], 1)
                dve.drain()
                V.tensor_tensor(pos[:], pos[:], onehot[:], ALU.mult)
                dve.drain()
                V.tensor_reduce(r_sel[:], pos[:], AX.X, ALU.add)
                V.tensor_scalar(r_t[:], r_idx[:], float(CAP), -1.0, ALU.mult, ALU.add)
                dve.drain()
                V.tensor_scalar(r_keep[:], r_sel[:], CAP + 0.5, None, ALU.is_lt)
                V.tensor_tensor(r_t[:], r_t[:], r_sel[:], ALU.add)
                dve.drain()
                g = gates[:, bass.ds(b * TB, TB)]
                V.tensor_tensor(g, g, r_keep[:], ALU.mult)
                for dst, away in ((slot_r[:, bass.ds(b * TB, TB)], float(NE * CAP - 1)),
                                  (slot_w[:, :], float(2 * NE * CAP))):
                    V.tensor_scalar(r_sum[:], r_t[:], away, None, ALU.subtract)
                    dve.drain()
                    V.tensor_tensor(r_sum[:], r_sum[:], r_keep[:], ALU.mult)
                    dve.drain()
                    last = V.tensor_scalar(dst, r_sum[:], away, None, ALU.add)
                    if away == NE * CAP - 1:
                        dve.drain()
                last.then_inc(slots_done, 1)
                dve.drain()

            def w2_low_part(c, n):
                dve.wait_ge(w2_high, n * NS + c + 1)
                V.tensor_tensor(w2l[:, c, :], w2st[:, c % 2, :], w2h[:, c, :].bitcast(F32), ALU.subtract)\
                    .then_inc(w2_low, 1)

            def hidden(bk, c, n_tok, n_body):
                if c < HC:
                    ps = full(bk, f"b{c}")
                    bank, n = bk.use(f"a{c}")
                    dve.wait_ge(bk.freed[bank], n + 1)
                    V.tensor_tensor(hid[:, c % 2, 0:n_tok], gate_act[:, c % 2, 0:n_tok], ps[:, 0:n_tok], ALU.mult)\
                        .then_inc(bk.freed[bk.use(f"b{c}")[0]], 1)
                    dve.wait_ge(hh_done, n_body * NS + c + 1)
                    V.tensor_tensor(hl[:, c, 0:n_tok], hid[:, c % 2, 0:n_tok], hh[:, c, 0:n_tok].bitcast(F32),
                                    ALU.subtract).then_inc(hl_done, 1)
                else:
                    ps = full(bk, "ab")
                    dve.wait_ge(act_done, n_body + 1)
                    V.tensor_tensor(hid[0:HT, c % 2, 0:n_tok], gate_act[0:HT, c % 2, 0:n_tok], ps[HT:P, 0:n_tok],
                                    ALU.mult).then_inc(bk.freed[bk.use("ab")[0]], 1)
                    dve.wait_ge(hh_done, n_body * NS + c + 1)
                    V.tensor_tensor(hh[HT:P, c, 0:n_tok], hid[0:HT, c % 2, 0:n_tok],
                                    hh[0:HT, c, 0:n_tok].bitcast(F32), ALU.subtract).then_inc(hl_done, 1)

            def add_shared(bk, tile, m):
                ps = full(bk, f"D{m}")
                row = flat(xres[:, bass.ds(tile, 1), :])
                V.tensor_tensor(row, row, ps[:, :], ALU.add).then_inc(bk.freed[bk.use(f"D{m}")[0]], 1)

            for t in range(TB):
                if t >= 2:
                    full(before, f"QT{t - 2}")
                quantise_tokens(t, t)
                w2_low_part(t, 0)
                if t:
                    add_cross_attention(before, t - 1, t - 1, 0)
            add_cross_attention(before, TB - 1, TB - 1, 0)
            normalise_batch(0, True)
            dve.wait_ge(wg_high, 1)
            V.tensor_tensor(wgl[:, :, :], wg[:, :, :], wgh[:, :, :].bitcast(F32), ALU.subtract).then_inc(wg_low, 1)
            for t in range(TB):
                tokens_low(before, t, t + 1)
            for c in range(TB, NS):
                w2_low_part(c, 0)
            dve.wait_ge(route_consts, 4)
            choose_expert(before, 0)

            def shared(b, ahead):
                bk = shared_banks(b, ahead)
                next_tile = (b + 1) * TB
                for c in range(NS):
                    if ahead and c < TB:
                        if c >= 2:
                            full(bk, f"QT{c - 2}")
                        quantise_tokens(next_tile + c, c)
                    hidden(bk, c, T, b)
                    if c == 1:
                        place_tokens(bk, b)
                    if ahead and 1 <= c <= TB:
                        add_cross_attention(bk, next_tile + c - 1, c - 1, b + 1)
                if ahead:
                    normalise_batch(b + 1)
                add_shared(bk, b * TB, 0)
                add_shared(bk, b * TB + 1, 1)
                n_x = (b + 1) * TB
                if ahead:
                    for t in range(TB):
                        tokens_low(bk, t, n_x + t + 1)
                else:
                    for k in range(2):
                        w13_low_part(k, 1)
                    for t in range(CAP_T):
                        tokens_low(bk, t, n_x + t + 1)
                add_shared(bk, b * TB + 2, 2)
                add_shared(bk, b * TB + 3, 3)
                if ahead:
                    choose_expert(bk, b + 1)
                else:
                    for k in range(2, KC):
                        w13_low_part(k, 1)

            with dve.Fori(0, B - 1) as b:
                shared(b, True)
            shared(B - 1, False)

            def expert(e, ahead):
                bk = expert_banks(e, ahead)
                for c in range(NS):
                    hidden(bk, c, CAP, B + e)
                    w2_low_part(c, e + 1)
                if ahead:
                    for k in range(2):
                        w13_low_part(k, e + 2)
                    for t in range(CAP_T):
                        tokens_low(bk, t, NT + e * CAP_T + CAP_T + t + 1)
                    for k in range(2, KC):
                        w13_low_part(k, e + 2)

            with dve.Fori(0, NE - 1) as e:
                expert(e, True)
            expert(NE - 1, False)

            for i in range(NT):
                dve.wait_ge(answers_in[i // TB], 16 * TB)
                last = V.scalar_tensor_tensor(out=xres[:, i, :], in0=gathered[:, i, :], scalar=gates[:, i:i + 1],
                                              in1=xres[:, i, :], op0=ALU.mult, op1=ALU.add)
                if i % TB == TB - 1:
                    last.then_inc(result_done, 1)


_INS = ['x', 'ctx_2048', 'mask_Bx1xS2_ff0', 'L0_attn_Wq', 'L0_attn_Wk', 'L0_attn_Wv', 'L0_attn_Wo',
        'L0_attn_q_scale', 'L0_attn_k_scale', 'L0_ffn_Wg', 'L0_ffn_W1', 'L0_ffn_W3', 'L0_ffn_W2',
        'L0_ffn_sw1', 'L0_ffn_sw3', 'L0_ffn_sw2']
_OUTS = [((B, T, D), 'float32')]


def kernel(**inputs):
    import numpy as _np
    import concourse.bacc as _bacc
    from concourse import mybir as _mybir
    from concourse.bass_utils import run_bass_kernel_spmd as _run

    nc = _bacc.Bacc("TRN2", target_bir_lowering=False, num_devices=1)
    arrays, args = {}, []
    for name in _INS:
        a = _np.ascontiguousarray(inputs[name])
        arrays[f"in_{name}_dram"] = a
        args.append(nc.dram_tensor(f"in_{name}_dram", a.shape, _mybir.dt.from_np(a.dtype), kind="ExternalInput").ap())
    for i, (shape, dtype) in enumerate(_OUTS):
        dt = _mybir.dt.from_np(_np.dtype(dtype))
        args.append(nc.dram_tensor(f"out_{i}_dram", shape, dt, kind="ExternalOutput").ap())
    decoder(nc, *args)
    r = _run(nc, [arrays], core_ids=[0])
    got = tuple(r.results[0][f"out_{i}_dram"] for i in range(len(_OUTS)))
    return got[0]
```

```python
from contextlib import ExitStack

import concourse.bass as bass
from concourse import mybir

P = 128
B, T, D = 4, 512, 512
NH, NKV, HD = 16, 4, 128
REP = NH // NKV
KC = D // P
TB = T // P
NT = B * TB
UNITS = NKV * B
LN_EPS = 1e-5
QK_EPS = 1e-6
SCALE = float(HD) ** -0.5
MASKED = -1e30
FP8_MAX = 448.0
FP8_EPS = 1e-12
FP8_LEAST = 2.0 ** -6
ROUND_AT = 1.5 * 2.0 ** 20
EXPONENT = 0x7F800000
NE, H = 8, 704
CAP = B * T // NE
CAP_T = CAP // P
HC = H // P
HT = H - HC * P
W13 = 2 * H
NS = HC + 1

ALU = mybir.AluOpType
ACT = mybir.ActivationFunctionType
AX = mybir.AxisListType
F32 = mybir.dt.float32
F32R = mybir.dt.float32r
BF16 = mybir.dt.bfloat16
I32 = mybir.dt.int32
RMAX = bass.bass_isa.ReduceOp.max

P_OFF = [P * (j * (j + 1) // 2) for j in range(TB + 1)]
PT_OFF = {0: 0, 1: 512, 3: 896, 2: 1024}
CHUNKS = {"A": (0, 512, [0]), "B": (512, 512, [1, 3]), "C": (1024, 256, [2])}

TILES = ["q0", "v", "q1", "q2", "k", "q3", "o0", "o1", "o2", "o3"]
QKV_TILES, O_TILES = TILES[:6], TILES[6:]
PREP_START = [("q0", 5), ("v", 6)]
PREP_IN_SLOT = [[("q1", 6)], [("q2", 6), ("k", 5)], [("q3", 5)], []]
RING = 2
EARLY_TILES = 4
FIRST_STAGE = len(TILES) - RING


class Banks:

    def __init__(self, uses, base, filled, freed):
        self.filled, self.freed = filled, freed
        self.at, seen = {}, {}
        for name, bank in uses:
            self.at[name] = (bank, seen.get(bank, 0))
            seen[bank] = seen.get(bank, 0) + 1
        self.base = base

    def use(self, name):
        bank, n = self.at[name]
        return bank, self.base[bank] + n


def count(uses, of=range(8)):
    return {b: sum(1 for _, bank in uses if bank == b) for b in of}


def unit_uses(prep, final):
    uses = [(f"w_{t}", bank) for t, bank in PREP_START] if prep else []
    for h in range(REP):
        uses += [(f"Q{h}", 7), (f"A{h}", 4), (f"B{h}", 5), (f"C{h}", 6)]
        uses += [("V", 7)] if h == 0 else [("K", 6)] if h == 2 else []
        uses += [(f"w_{t}", bank) for t, bank in PREP_IN_SLOT[h]] if prep else []
        uses += [(f"PV{h}", 4), (f"SS{h}", 5)]
    uses += [("VT", 6), ("O0", 7), ("O1", 4), ("RK", 5), ("O2", 6), ("O3", 4)]
    if prep:
        uses += [(f"w_{t}", 4 + i % 4) for i, t in enumerate(O_TILES)]
    if final:
        uses = [u for u in uses if u[0][0] in "ABCPO"]
    return uses


def shared_uses(ahead):
    uses = []
    for c in range(HC):
        uses += [(f"a{c}", 2 * (c % 2)), (f"b{c}", 2 * (c % 2) + 1)]
        uses += [("RT", 6)] if c == 0 else [("CS", 7)] if c == 1 else []
        if ahead:
            uses += [(f"QT{c}", 4)] if c < TB else []
            uses += [(f"XA{c - 1}", 5)] if c else []
    uses += [("ab", 2), ("D0", 6), ("D1", 7), ("D2", 0)]
    uses += [(f"XT{t}", (4, 5, 3, 2)[t]) for t in range(TB if ahead else CAP_T)]
    return uses + [("D3", 1)]


def expert_uses(ahead):
    uses = []
    for c in range(HC):
        uses += [(f"a{c}", 2 * (c % 2)), (f"b{c}", 2 * (c % 2) + 1)]
    uses += [("ab", 2)]
    uses += [(f"XT{t}", 4 + t) for t in range(CAP_T)] if ahead else []
    return uses + [("D0", 6), ("D1", 7)]


def before_shared_uses():
    uses = []
    for t in range(TB):
        uses += [(f"QT{t}", 6 + t % 2), (f"XA{t}", 5)]
    return uses + [(f"XT{t}", t) for t in range(TB)]


def first_uses():
    w = [(f"w_{t}", 4 + i % 4) for i, t in enumerate(TILES)]
    tokens = [[(f"x{b}{t}", 4 + t) for t in range(TB)] for b in range(B)]
    uses = w[:EARLY_TILES] + tokens[0] + w[EARLY_TILES:] + [("V", 6), ("K", 7)]
    for h in range(REP):
        uses += [(f"Q{h}", 4 + h % 2)] + ([(f"SS{h - 1}", 6)] if h else [])
    uses += [(f"SS{REP - 1}", 6), ("VT", 7)] + tokens[1] + [("RK", 6)]
    return uses + tokens[2] + tokens[3]


def decoder(nc, x, ctx_in_dram, mask_dram, Wq, Wk, Wv, Wo, q_scale, k_scale, Wg, W1, W3, W2, sw1, sw3, sw2, out):
    nc_stack = ExitStack()
    with nc_stack as stack:

        def sem(name):
            return stack.enter_context(nc.semaphore(name))

        base = nc.sbuf_base + (-nc.sbuf_base) % 32
        room = nc.sbuf_usable_end - 64 - base
        slab = stack.enter_context(nc.sbuf_tensor("slab", [P, (room - 64) // 4], F32))
        place = [base + 32]

        def sb(name, shape, dtype):
            n = 1
            for s in shape[1:]:
                n *= s
            size = n * (2 if dtype == BF16 else 4)
            t = nc.alloc_sbuf_tensor_at(name, shape, dtype, offset=place[0])
            place[0] += size + (-size) % 32
            assert place[0] <= base + room, (name, place[0] - base - room)
            return t

        psum = [stack.enter_context(nc.psum_tensor(f"bank{i}", [P, 512], F32)) for i in range(8)]

        xres = sb("xres", [P, NT, D], F32)
        ident = sb("ident", [P, P], F32)
        ident_b = sb("ident_b", [P, P], BF16)
        causal = sb("causal", [P, P], BF16)
        ones = sb("ones", [P, 2], F32)
        qs_col = sb("qs_col", [P, 2], F32)
        qk_scale = sb("qk_scale", [P, 1], F32)
        stats = sb("stats", [P, TB, 6], F32)
        mv = sb("mv", [P, TB, 2], F32)
        mean = sb("mean", [P, NT], F32)
        rstd = sb("rstd", [P, NT], F32)
        chain_v = sb("chain_v", [P, 20], F32)
        chain_t = sb("chain_t", [P, 20], F32)
        shift = nc.alloc_sbuf_tensor_at("shift", [P, NT], F32, offset=place[0])
        rowmax = sb("rowmax", [P, NT], F32)
        rowmin = sb("rowmin", [P, NT], F32)
        amax = sb("amax", [P, 4], F32)
        ctx_part = sb("ctx_part", [P, B * KC // 2], F32)
        extremes = sb("extremes", [P, 2], F32)
        f8scale = sb("f8scale", [P, 4], F32)
        common_end = place[0]

        xTh = sb("xTh", [P, KC, B * T], F32R)
        xTl = sb("xTl", [P, KC, B * T], F32R)
        wTh = sb("wTh", [P, 6, D], F32R)
        wTl = sb("wTl", [P, 6, D], F32R)
        wstage_at = place[0]
        wstage = sb("wstage", [P, RING, D], F32)
        woTh = sb("woTh", [P, REP, D], F32R)
        woTl = sb("woTl", [P, REP, D], F32R)
        qTh = sb("qTh", [P, REP, T], F32R)
        qTl = sb("qTl", [P, REP, T], F32R)
        kTh = sb("kTh", [P, T], F32R)
        kTl = sb("kTl", [P, T], F32R)
        vh = sb("vh", [P, TB, HD], F32R)
        vl = sb("vl", [P, TB, HD], F32R)
        otmp = place[0]
        oTh = sb("oTh", [P, REP, T], F32R)
        oTl = sb("oTl", [P, REP, T], F32R)
        xn = nc.alloc_sbuf_tensor_at("xn", [P, 2, D], F32, offset=place[0])
        pTh = sb("pTh", [P, P_OFF[TB]], F32R)
        pTl = sb("pTl", [P, P_OFF[TB]], F32R)
        probs = sb("probs", [P, P_OFF[TB]], F32)
        qsq = sb("qsq", [P, T], F32)
        ctx_m = nc.alloc_sbuf_tensor_at("ctx_m", [P, D // 2], F32, offset=place[0])
        ctx_q = nc.alloc_sbuf_tensor_at("ctx_q", [P, D], BF16, offset=place[0] + D // 2 * 4)
        ksq = sb("ksq", [P, T], F32)
        kraw = sb("kraw", [P, T], F32)
        vraw = sb("vraw", [P, T], F32)
        ss = sb("ss", [P, 20], F32)
        sc = sb("sc", [P, 20], F32)
        mx = sb("mx", [P, 16], F32)
        nbias = sb("nbias", [P, 16], F32)
        rowsum = sb("rowsum", [P, 16], F32)
        rinv = sb("rinv", [P, 4], F32)
        ctx_all = nc.alloc_sbuf_tensor_at("ctx_all", [P, 4, 2, D], F32, offset=otmp)
        first_w = nc.alloc_sbuf_tensor_at("first_w", [P, FIRST_STAGE, D], F32, offset=otmp)
        first_stats = nc.alloc_sbuf_tensor_at("first_stats", [P, NT, 6], F32, offset=place[0])
        first_mv = nc.alloc_sbuf_tensor_at("first_mv", [P, NT, 2], F32, offset=place[0] + NT * 6 * 4)
        ctx_stage = sb("ctx_stage", [P, D], F32)
        zeros = sb("zeros", [P, P], F32)

        place[0] = common_end
        w13h = sb("w13h", [P, KC * W13], F32R)
        w13l = sb("w13l", [P, KC * W13], F32R)
        w13st = sb("w13st", [P, KC * W13], F32)
        w2st = sb("w2st", [P, 2, D], F32)
        assert place[0] <= wstage_at
        w2h = sb("w2h", [P, NS, D], F32R)
        w2l = sb("w2l", [P, NS, D], F32R)
        xh = sb("xh", [P, KC, T], F32R)
        xl = sb("xl", [P, KC, T], F32R)
        hh = sb("hh", [P, NS, T], F32R)
        hl = sb("hl", [P, HC, T], F32R)
        gate_act = sb("gate_act", [P, 2, T], F32)
        hid = sb("hid", [P, 2, T], F32)
        x3n = sb("x3n", [P, TB, D], F32)
        ctxq = sb("ctxq", [P, KC, D], BF16)
        tokens_q = sb("tokens_q", [P, 2, D], BF16)
        tokens_qT = sb("tokens_qT", [P, 2, KC, P], BF16)
        q_at = place[0]
        q_y = sb("q_y", [P, D], F32)
        q_m = sb("q_m", [P, D], F32)
        attended = sb("attended", [P, D], F32)
        mask_b = sb("mask_b", [P, D], F32)
        wg = sb("wg", [P, KC, NE], F32)
        wgh = sb("wgh", [P, KC, NE], F32R)
        wgl = sb("wgl", [P, KC, NE], F32R)
        tri = sb("tri", [P, P], BF16)
        ones_b = sb("ones_b", [P, P], BF16)
        expert_id = sb("expert_id", [P, NE], F32)
        lg = sb("lg", [P, TB, NE], F32)
        lt = sb("lt", [P, TB, NE], F32)
        le = sb("le", [P, TB, NE], F32)
        onehot = sb("onehot", [P, TB, NE], BF16)
        pos = sb("pos", [P, TB, NE], F32)
        carry = sb("carry", [P, NE], F32)
        r_max = sb("r_max", [P, TB], F32)
        r_idx = sb("r_idx", [P, TB], F32)
        r_sum = sb("r_sum", [P, TB], F32)
        r_sel = sb("r_sel", [P, TB], F32)
        r_keep = sb("r_keep", [P, TB], F32)
        r_t = sb("r_t", [P, TB], F32)
        slot_w = sb("slot_w", [P, TB], I32)
        slot_r = sb("slot_r", [P, NT], I32)
        gates = sb("gates", [P, NT], F32)
        expert_out = nc.alloc_sbuf_tensor_at("expert_out", [P, CAP_T, D], F32, offset=q_at)
        gathered = nc.alloc_sbuf_tensor_at("gathered", [P, NT, D], F32, offset=common_end)

        ctxq_dram = nc.dram_tensor("ctxq_dram", [B * T, D], BF16, kind="Internal").ap()
        sent = nc.dram_tensor("sent", [NE * CAP, D], F32, kind="Internal").ap()
        answered = nc.dram_tensor("answered", [NE * CAP, D], F32, kind="Internal").ap()

        x_in = [sem(f"x_in{b}") for b in range(B)]
        scales_in = sem("scales_in")
        w_in = [sem(f"w_in{r}") for r in range(RING)]
        filled = {b: sem(f"filled{b}") for b in range(4, 8)}
        freed = {b: sem(f"freed{b}") for b in range(4, 8)}
        consts = sem("consts")
        pool_step = sem("pool_step")
        ones_set = sem("ones_set")
        hi_done = sem("hi_done")
        mean_done = sem("mean_done")
        xn_done = sem("xn_done")
        s_filled = sem("s_filled")
        exp_done = sem("exp_done")
        bias_done = sem("bias_done")
        norm_done = sem("norm_done")
        sq_done = sem("sq_done")
        norms_done = sem("norms_done")
        k_ready = sem("k_ready")
        qkl_done = sem("qkl_done")
        attn_done = sem("attn_done")
        ctx_all_in = [sem(f"ctx_all_in{i}") for i in range(4)]
        ctx_in = sem("ctx_in")
        ctx_abs = sem("ctx_abs")
        first_w_in = [sem(f"first_w_in{i}") for i in range(FIRST_STAGE // 2)]
        ctx_read = sem("ctx_read")
        ctx_amax = sem("ctx_amax")
        ctx_amax_all = sem("ctx_amax_all")
        ctxq_done = sem("ctxq_done")
        ctxq_out = sem("ctxq_out")
        zeros_set = sem("zeros_set")
        sent_zeroed = sem("sent_zeroed")
        x_amax = sem("x_amax")
        x_amax_all = sem("x_amax_all")
        w13_in = [sem(f"w13_in{c}") for c in range(NS)]
        w2_in = [sem(f"w2_in{k}") for k in range(2)]
        w13_high = sem("w13_high")
        w13_low = sem("w13_low")
        w2_high = sem("w2_high")
        w2_low = sem("w2_low")
        ctxq_in = sem("ctxq_in")
        mask_in = sem("mask_in")
        wg_in = sem("wg_in")
        wg_high = sem("wg_high")
        wg_low = sem("wg_low")
        mask_read = sem("mask_read")
        mfull = {b: sem(f"mfull{b}") for b in range(8)}
        mfree = {b: sem(f"mfree{b}") for b in range(8)}
        quantised = sem("quantised")
        qT_done = sem("qT_done")
        x3n_done = sem("x3n_done")
        xh_done = sem("xh_done")
        act_done = sem("act_done")
        hh_done = sem("hh_done")
        hl_done = sem("hl_done")
        logits_less_max = sem("logits_less_max")
        logits_exp = sem("logits_exp")
        onehot_done = sem("onehot_done")
        slots_done = sem("slots_done")
        tokens_sent = sem("tokens_sent")
        expert_in = sem("expert_in")
        answers_out = [sem(f"answers_out{m}") for m in range(CAP_T)]
        route_consts = sem("route_consts")
        answers_in = [sem(f"answers_in{i}") for i in range(NT // TB)]
        result_done = sem("result_done")
        stored = sem("stored")

        block = stack.enter_context(nc.Block())

        FIRST, UNIT, PREP, FINAL = first_uses(), unit_uses(False, False), unit_uses(True, False), unit_uses(False, True)
        n_first, n_unit = count(FIRST), count(UNIT)
        n_prep = {b: n - n_unit[b] for b, n in count(PREP).items()}

        def banks(u, g, prep, final=False):
            return Banks(PREP if prep else FINAL if final else UNIT,
                         {b: n_first[b] + u * n_unit[b] + g * n_prep[b] for b in range(8)}, filled, freed)

        first = Banks(FIRST, {b: 0 for b in range(8)}, filled, freed)

        BEFORE, SHARED, SHARED_LAST = before_shared_uses(), shared_uses(True), shared_uses(False)
        EXPERT, EXPERT_LAST = expert_uses(True), expert_uses(False)
        n_before, n_shared, n_shared_last, n_expert = (count(u) for u in (BEFORE, SHARED, SHARED_LAST, EXPERT))
        before = Banks(BEFORE, {b: 0 for b in range(8)}, mfull, mfree)

        def shared_banks(b, ahead):
            return Banks(SHARED if ahead else SHARED_LAST,
                         {k: n_before[k] + b * n_shared[k] for k in range(8)}, mfull, mfree)

        def expert_banks(e, ahead):
            start = {k: n_before[k] + (B - 1) * n_shared[k] + n_shared_last[k] for k in range(8)}
            return Banks(EXPERT if ahead else EXPERT_LAST, {k: start[k] + e * n_expert[k] for k in range(8)},
                         mfull, mfree)

        def units(eng, body):
            with eng.Fori(0, NKV - 1) as g:
                with eng.Fori(0, B - 1) as b:
                    body(g * B + b, g, b, b + 1, False, False)
                body(g * B + B - 1, g, B - 1, 0, True, False)
            body((NKV - 1) * B, NKV - 1, 0, 1, False, False)
            with eng.Fori(1, B - 1) as b:
                body((NKV - 1) * B + b, NKV - 1, b, b + 1, False, False)
            body(UNITS - 1, NKV - 1, B - 1, None, False, True)

        SPLIT_IN_SLOT = [[], [0, 1], [2, 3], [4, 5]]

        def high_parts(prep, final):
            names = [f"w_{t}" for t, _ in PREP_START] if prep else []
            for h in range(REP):
                probabilities = [f"A{h}", f"B{h}", f"C{h}"]
                if not final:
                    probabilities = [f"Q{h}"] + probabilities if h == 0 else probabilities + [f"Q{h}"]
                names += probabilities + ([f"w_{t}" for t, _ in PREP_IN_SLOT[h]] if prep else []) + [f"PV{h}"]
            return names + ([] if final else ["VT", "KN"]) + ([f"w_{t}" for t in O_TILES] if prep else [])

        n_hi = len(high_parts(False, False))
        HI_FIRST = {}
        for name, _ in FIRST:
            if name[0] in "wxQ" or name in ("VT", "RK"):
                HI_FIRST[name] = len(HI_FIRST)

        def hi_at(u, g, prep, final, name):
            return len(HI_FIRST) + u * n_hi + g * len(TILES) + high_parts(prep, final).index(name) + 1

        def w_src(t, g, ahead):
            if t in "kv":
                return {"k": Wk, "v": Wv}[t][bass.ds(g * P + ahead * P, P), :]
            n = int(t[1])
            if t[0] == "q":
                return Wq[bass.ds(g * REP * P + (ahead * REP + n) * P, P), :]
            return Wo[n * P:(n + 1) * P, bass.ds(g * REP * HD + ahead * REP * HD, REP * HD)]

        def w_dst(t, hi):
            if t[0] == "o":
                m = int(t[1])
                return (woTh if hi else woTl)[:, :, m * P:(m + 1) * P]
            return (wTh if hi else wTl)[:, TILES.index(t), :].rearrange("p (k n) -> p k n", k=KC)

        def w13_chunk(w, c):
            n = P if c < HC else HT
            return w[:, c * KC * 2 * P:(c * 2 * P + 2 * n) * KC].rearrange("p (k n) -> p k n", k=KC)

        def blocks(bank):
            return psum[bank][:, :].rearrange("p (k n) -> p k n", k=4)

        ctx_rows = ctx_in_dram.rearrange("b k n -> (b k) n")

        @block.sync
        def _(sp):
            x_tiles = x.rearrange("b (t p) d -> b p t d", p=P)

            def load_w(g, i, ahead=0):
                sp.dma_start(wstage[:, i % RING, :], w_src(TILES[i], g, ahead)).then_inc(w_in[i % RING], 16)

            def load_x(b):
                sp.dma_start(xres[:, b * TB:(b + 1) * TB, :], x_tiles[b]).then_inc(x_in[b], 16)

            sp.dma_start(qs_col[:, 0:1], q_scale.rearrange("(p a) -> p a", a=1)).then_inc(scales_in, 16)
            sp.dma_start(qs_col[:, 1:2], k_scale.rearrange("(p a) -> p a", a=1)).then_inc(scales_in, 16)
            def transposed(bk, i):
                bank, n = bk.use(f"w_{TILES[i]}")
                sp.wait_ge(bk.filled[bank], n + 1)

            for b in range(B):
                load_x(b)
                if b == 0:
                    for i in range(FIRST_STAGE):
                        sp.dma_start(first_w[:, i, :], w_src(TILES[i], 0, 0)).then_inc(first_w_in[i // 2], 16)
                    for i in range(FIRST_STAGE, len(TILES)):
                        load_w(0, i)

            def replace_tiles(bk, old, g, ahead, first_tile, end_tile):
                for i in range(first_tile, end_tile):
                    transposed(bk, old + i - first_tile)
                    load_w(g, i, ahead)

            def next_group(g, ahead, bk):
                replace_tiles(bk, len(TILES) - RING, g, ahead, 0, RING)

            def rest_of_group(g, ahead):
                last = g + ahead - 1
                bk = banks(last * B + B - 1, last, True)
                replace_tiles(bk, 0, g, ahead, RING, len(TILES))
                return bk

            next_group(0, 1, first)
            with sp.Fori(0, NKV - 2) as g:
                next_group(g, 2, rest_of_group(g, 1))
            rest_of_group(NKV - 1, 0)

            def load_w13(w1, w3, c, wait):
                if wait is not None:
                    sp.wait_ge(w13_low, wait)
                n = P if c < HC else HT
                dst = w13_chunk(w13st, c)
                for i, w in enumerate((w1, w3)):
                    sp.dma_start(dst[:, :, i * n:(i + 1) * n],
                                 w[:, c * P:c * P + n].rearrange("(k p) h -> p k h", p=P)).then_inc(w13_in[c], 16)

            def load_w2(w2_rows, c, wait):
                if wait is not None:
                    sp.wait_ge(w2_low, wait)
                upper, lower = (w2_rows[0:HT, :], w2_rows[HT:P, :]) if c < HC else (w2_rows, w2_rows)
                sp.dma_start(w2st[0:HT, c % 2, :], upper).then_inc(w2_in[c % 2], 16)
                sp.dma_start(w2st[HT:P, c % 2, :], lower).then_inc(w2_in[c % 2], 16)

            def chunk_rows(c):
                return slice(c * P, min(H, (c + 1) * P))

            def expert_rows(w, e, rows):
                return w[bass.ds(e, 1), rows, :].rearrange("a p h -> (a p) h")

            def load_expert_w13(e, n, c):
                w1, w3 = (w[bass.ds(e, 1), :, :].rearrange("a d h -> (a d) h") for w in (W1, W3))
                load_w13(w1, w3, c, (n - 1) * NS + c + 1)

            def load_batch(b):
                sp.dma_start(ctxq[:, :, :], ctxq_dram[bass.ds(b * T, T), :].rearrange("(k p) n -> p k n", p=P))\
                    .then_inc(ctxq_in, 16)
                sp.dma_start(mask_b[:, :], mask_in_rows(b)).then_inc(mask_in, 16)

            def mask_in_rows(b):
                return mask_dram[bass.ds(b, 1), :, :].rearrange("a c n -> (a c n)").partition_broadcast(P)

            sp.wait_ge(norms_done, UNITS)
            for c in range(NS):
                load_w13(sw1, sw3, c, None)
            for c in range(2):
                load_w2(sw2[chunk_rows(c), :], c, None)
            sp.wait_ge(attn_done, 1)
            sp.wait_ge(ctxq_out, 16 * B * KC)
            sp.dma_start(wg[:, :, :], Wg.rearrange("(k p) e -> p k e", p=P)).then_inc(wg_in, 16)
            load_batch(0)
            for c in range(2, NS):
                load_w2(sw2[chunk_rows(c), :], c, c - 1)
            for c in range(NS):
                load_expert_w13(0, 1, c)
            with sp.Fori(1, B) as b:
                sp.wait_ge(mask_read, b * TB)
                load_batch(b)

            def load_tokens(e):
                sp.dma_start(x3n[:, 0:CAP_T, :], sent[bass.ds(e * CAP, CAP), :].rearrange("(t p) d -> p t d", p=P))\
                    .then_inc(expert_in, 16)

            def load_expert_w2(e, n, c):
                load_w2(expert_rows(W2, e, chunk_rows(c)), c, n * NS + c - 1)

            def load_sets(e, with_next=True):
                for c in range(NS):
                    load_expert_w2(e - 1, e, c)
                    if with_next:
                        load_expert_w13(e, e + 1, c)

            sp.wait_ge(tokens_sent, NT * 16)
            load_tokens(0)

            def tokens_transposed(bk):
                bank, n = bk.use(f"XT{CAP_T - 1}")
                sp.wait_ge(bk.filled[bank], n + 1)

            tokens_transposed(shared_banks(B - 1, False))
            load_tokens(1)
            with sp.Fori(1, NE - 1) as e:
                load_sets(e)
                tokens_transposed(expert_banks(e - 1, True))
                load_tokens(e + 1)
            load_sets(NE - 1)
            load_sets(NE, False)
            out_tiles = out.rearrange("b (t p) d -> b p t d", p=P)
            for b in range(B):
                sp.wait_ge(result_done, b + 1)
                sp.dma_start(out_tiles[b], xres[:, b * TB:(b + 1) * TB, :]).then_inc(stored, 16)
            sp.wait_ge(stored, B * 16)

        @block.gpsimd
        def _(pool):
            nc.gpsimd.memset(ident[:], 0.0).then_inc(pool_step, 1)
            nc.gpsimd.memset(causal[:], 0.0).then_inc(pool_step, 1)
            nc.gpsimd.memset(ones[:], 1.0).then_inc(consts, 1)
            nc.gpsimd.memset(zeros[:], 0.0).then_inc(zeros_set, 1)
            pool.wait_ge(pool_step, 2)
            nc.gpsimd.affine_select(out=ident[:], in_=ident[:], compare_op=ALU.not_equal, fill=1.0, base=0,
                                    pattern=[[-1, P]], channel_multiplier=1).then_inc(pool_step, 1)
            nc.gpsimd.affine_select(out=causal[:], in_=causal[:], compare_op=ALU.is_ge, fill=MASKED, base=0,
                                    pattern=[[-1, P]], channel_multiplier=1).then_inc(consts, 1)
            pool.wait_ge(pool_step, 3)
            nc.gpsimd.tensor_copy(ident_b[:], ident[:]).then_inc(consts, 1)

            ctx_pairs = ctx_in_dram.rearrange("b (i t p) n -> (b i) p t n", p=P, t=2)
            pool.wait_ge(x_in[B - 1], 16)
            bank, n = first.use(f"w_{TILES[-1]}")
            pool.wait_ge(filled[bank], n + 1)
            for i in range(B * KC // 2):
                if i >= 4:
                    pool.wait_ge(ctx_read, i - 3)
                pool.dma_start(ctx_all[:, i % 4, :, :], ctx_pairs[i]).then_inc(ctx_all_in[i % 4], 16)
            pool.wait_ge(ctx_amax, 1)
            nc.gpsimd.partition_all_reduce(amax[:, 1:2], amax[:, 0:1], P, RMAX).then_inc(ctx_amax_all, 1)

            zero_row = zeros[:, :].rearrange("p (a n) -> p a n", a=1).to_broadcast([P, D // P, P])

            def ctx_tile_out(i):
                pool.wait_ge(ctxq_done, i + 1)
                pool.dma_start(ctxq_dram[bass.ds(i * P, P), :], ctx_q[:, :]).then_inc(ctxq_out, 16)
                pool.dma_start(sent[bass.ds(i * P, P), :].rearrange("p (a n) -> p a n", a=D // P), zero_row)\
                    .then_inc(sent_zeroed, 16)
                pool.wait_ge(ctxq_out, (i + 1) * 16)

            pool.wait_ge(zeros_set, 1)
            pool.dma_start(ctx_stage[:, :], ctx_rows[0:P, :]).then_inc(ctx_in, 16)
            with pool.Fori(0, UNITS - 1) as i:
                ctx_tile_out(i)
                pool.dma_start(ctx_stage[:, :], ctx_rows[bass.ds((i + 1) * P, P), :]).then_inc(ctx_in, 16)
            ctx_tile_out(UNITS - 1)
            pool.wait_ge(x_amax, 1)
            nc.gpsimd.partition_all_reduce(amax[:, 3:4], amax[:, 2:3], P, RMAX).then_inc(x_amax_all, 1)

            nc.gpsimd.memset(ones_b[:], 1.0).then_inc(route_consts, 1)
            nc.gpsimd.memset(tri[:], 1.0).then_inc(pool_step, 1)
            nc.gpsimd.memset(carry[:], 0.0).then_inc(route_consts, 1)
            nc.gpsimd.iota(expert_id[:], [[1, NE]], base=0, channel_multiplier=0,
                           allow_small_or_imprecise_dtypes=True).then_inc(route_consts, 1)
            pool.wait_ge(pool_step, 4)
            nc.gpsimd.affine_select(out=tri[:], in_=tri[:], compare_op=ALU.is_ge, fill=0.0, base=0,
                                    pattern=[[1, P]], channel_multiplier=-1).then_inc(route_consts, 1)

            pool.wait_ge(sent_zeroed, 16 * UNITS)
            last_row = pool.to_reg(NE * CAP - 1)
            for b in range(B):
                pool.wait_ge(slots_done, b + 1)
                for t in range(TB):
                    pool.indirect_dma_start(
                        out=sent[:, :], out_offset=bass.IndirectOffsetOnAxis(ap=slot_w[:, t:t + 1], axis=0),
                        in_=x3n[:, t, :], in_offset=None, bounds_check=last_row,
                        oob_is_err=False).then_inc(tokens_sent, 16)

            with pool.Fori(0, NE) as e:
                for m in range(CAP_T):
                    bank, n = expert_banks(e, True).use(f"D{m}")
                    pool.wait_ge(mfree[bank], n + 1)
                    pool.dma_start(answered[bass.ds(e * CAP + m * P, P), :], expert_out[:, m, :])\
                        .then_inc(answers_out[m], 16)
            for m in range(CAP_T):
                pool.wait_ge(answers_out[m], 16 * NE)
            for i in range(NT):
                pool.indirect_dma_start(
                    out=gathered[:, i, :], out_offset=None, in_=answered[:, :],
                    in_offset=bass.IndirectOffsetOnAxis(ap=slot_r[:, i:i + 1], axis=0),
                    bounds_check=last_row, oob_is_err=False).then_inc(answers_in[i // TB], 16)

        @block.tensor
        def _(pe):
            mm = nc.tensor.matmul

            def begin(bk, name):
                bank, n = bk.use(name)
                pe.wait_ge(bk.freed[bank], n)
                return psum[bank]

            def end(bk, name, instruction):
                instruction.then_inc(bk.filled[bk.use(name)[0]], 1)

            def landed(bk, name):
                bank, n = bk.use(name)
                pe.wait_ge(bk.freed[bank], n + 1)

            def product(dst, pairs, n=None):
                last = None
                total = 3 * len(pairs)
                i = 0
                for (lh, ll), (rh, rl) in pairs:
                    for a, b_ in ((lh, rh), (ll, rh), (lh, rl)):
                        last = mm(dst, a, b_, start=(i == 0), stop=(i == total - 1))
                        i += 1
                return last

            def weight_tile(bk, g, t, own_place=False):
                i = TILES.index(t)
                if own_place:
                    pe.wait_ge(first_w_in[i // 2], 32)
                    src = first_w[:, i, :]
                else:
                    pe.wait_ge(w_in[i % RING], (g * (len(TILES) // RING) + (i - FIRST_STAGE) // RING + 1) * 16)
                    src = wstage[:, i % RING, :]
                ps = begin(bk, f"w_{t}")
                for k in range(4):
                    last = nc.tensor.transpose(ps[:, k * P:(k + 1) * P], src[:, k * P:(k + 1) * P], ident[:])
                end(bk, f"w_{t}", last)

            def project(bk, name, tile, b, prep=False):
                if prep:
                    landed(bk, f"w_{tile}")
                ps = begin(bk, name)
                w = TILES.index(tile)
                last = product(ps[:, :], [
                    ((wTh[:, w, k * P:(k + 1) * P], wTl[:, w, k * P:(k + 1) * P]),
                     (xTh[:, k, bass.ds(b * T, T)], xTl[:, k, bass.ds(b * T, T)])) for k in range(KC)])
                end(bk, name, last)

            def scores(u, h, first_ever=False):
                for j in range(TB):
                    if not first_ever:
                        pe.wait_ge(exp_done, 16 * u + 4 * h + j - 3)
                    n = (j + 1) * P
                    qj = slice(j * P, n)
                    mm(psum[j][:, 0:n], qTh[:, h, qj], kTh[:, 0:n], start=True, stop=False)
                    mm(psum[j][:, j * P:n], ident_b[:], causal[:], start=False, stop=False,
                       skip_group_check=True)
                    mm(psum[j][:, 0:n], qTl[:, h, qj], kTh[:, 0:n], start=False, stop=False)
                    mm(psum[j][:, 0:n], qTh[:, h, qj], kTl[:, 0:n], start=False,
                       stop=True).then_inc(s_filled, 1)

            def sums_of_squares(bk, h, sq_n, with_k):
                pe.wait_ge(sq_done, sq_n)
                if with_k:
                    landed(bk, "K")
                ps = begin(bk, f"SS{h}")
                for c in range(8 if with_k else 4):
                    src = qsq if c < 4 else ksq
                    last = mm(ps[:, c:c + 1], src[:, (c % 4) * P:(c % 4 + 1) * P], ones[:, 0:1],
                              start=True, stop=True)
                end(bk, f"SS{h}", last)

            def value_blocks(bk):
                ps = begin(bk, "VT")
                for s in range(TB):
                    last = nc.tensor.transpose(ps[:, s * P:(s + 1) * P], vraw[:, s * P:(s + 1) * P], ident[:])
                end(bk, "VT", last)

            def key_scale_rows(bk):
                ps = begin(bk, "RK")
                for s in range(TB):
                    last = nc.tensor.transpose(ps[:, s * P:(s + 1) * P],
                                               sc[:, 16 + s:17 + s].to_broadcast([P, P]), ident[:])
                end(bk, "RK", last)

            pe.wait_ge(consts, 3)
            def token_tile(b, t):
                n = b * TB + t
                pe.wait_ge(xn_done, n + 1)
                ps = begin(first, f"x{b}{t}")
                for k in range(KC):
                    last = nc.tensor.transpose(ps[:, k * P:(k + 1) * P], xn[:, n % 2, k * P:(k + 1) * P], ident[:])
                end(first, f"x{b}{t}", last)

            for i, t in enumerate(TILES):
                if i == EARLY_TILES:
                    for n in range(TB):
                        token_tile(0, n)
                weight_tile(first, 0, t, own_place=(i < FIRST_STAGE))
            for t in range(TB):
                landed(first, f"x0{t}")
            for t in QKV_TILES:
                landed(first, f"w_{t}")
            project(first, "V", "v", 0)
            project(first, "K", "k", 0)
            for h in range(REP):
                project(first, f"Q{h}", f"q{h}", 0)
                if h:
                    sums_of_squares(first, h - 1, h, False)
            sums_of_squares(first, REP - 1, REP, True)
            value_blocks(first)
            for t in range(TB):
                token_tile(1, t)
            pe.wait_ge(norms_done, 1)
            key_scale_rows(first)
            landed(first, "VT")
            pe.wait_ge(k_ready, 1)
            scores(0, 0, True)
            for b in range(2, B):
                for t in range(TB):
                    token_tile(b, t)
            for t in range(TB):
                landed(first, f"x{B - 1}{t}")

            def unit(u, g, b, b_next, prep, final):
                bk = banks(u, g, prep, final)
                if prep:
                    for t, _ in PREP_START:
                        weight_tile(bk, g + 1, t)
                for h in range(REP):
                    if h == 0 and not final:
                        project(bk, "Q0", "q0", b_next, prep)
                    if h < REP - 1:
                        scores(u, h + 1)
                    pe.wait_ge(norm_done, 4 * u + h + 1)
                    for c in "ABC":
                        start, _, keys = CHUNKS[c]
                        ps = begin(bk, f"{c}{h}")
                        for s in keys:
                            for t in range(s, TB):
                                col = PT_OFF[s] - start + (t - s) * P
                                src = P_OFF[t] + s * P
                                last = nc.tensor.transpose(ps[:, col:col + P], probs[:, src:src + P], ident[:])
                        end(bk, f"{c}{h}", last)
                    if not final:
                        if h:
                            project(bk, f"Q{h}", f"q{h}", b_next, prep)
                        if h == 0:
                            project(bk, "V", "v", b_next, prep)
                        if h == 2:
                            project(bk, "K", "k", b_next, prep)
                    if prep:
                        for t, _ in PREP_IN_SLOT[h]:
                            weight_tile(bk, g + 1, t)
                    ps = begin(bk, f"PV{h}")
                    steps = 0
                    for s, c in ((0, "A"), (1, "B"), (3, "B"), (2, "C")):
                        landed(bk, f"{c}{h}")
                        n = (TB - s) * P
                        cols = slice(PT_OFF[s], PT_OFF[s] + n)
                        for a, p_ in ((vh, pTh), (vl, pTh), (vh, pTl)):
                            last = mm(ps[:, s * P:T], a[:, s, :], p_[:, cols], start=(steps == 0),
                                      stop=(steps == 11), skip_group_check=True)
                            steps += 1
                    end(bk, f"PV{h}", last)
                    if not final:
                        sums_of_squares(bk, h, REP * (u + 1) + h + 1, h == REP - 1)
                if not final:
                    value_blocks(bk)
                for m in range(TB):
                    if m == 2 and not final:
                        pe.wait_ge(norms_done, u + 2)
                        key_scale_rows(bk)
                    if m == 3 and not final:
                        landed(bk, "VT")
                        pe.wait_ge(k_ready, u + 2)
                        scores(u + 1, 0)
                    ps = begin(bk, f"O{m}")
                    if m == 0:
                        landed(bk, f"PV{REP - 1}")
                    last = product(ps[:, :], [
                        ((oTh[:, h, m * P:(m + 1) * P], oTl[:, h, m * P:(m + 1) * P]),
                         (woTh[:, h, :], woTl[:, h, :])) for h in range(REP)])
                    end(bk, f"O{m}", last)
                if prep:
                    for t in O_TILES:
                        weight_tile(bk, g + 1, t)

            units(pe, unit)

            def token_quantised_blocks(bk, t, n):
                pe.wait_ge(quantised, n + 1)
                ps = begin(bk, f"QT{t}").bitcast(BF16)
                for k in range(KC):
                    last = nc.tensor.transpose(ps[:, k * P:(k + 1) * P], tokens_q[:, t % 2, k * P:(k + 1) * P],
                                               ident_b[:])
                end(bk, f"QT{t}", last)

            def cross_attention(bk, t, b):
                landed(bk, f"QT{t}")
                pe.wait_ge(ctxq_in, 16 * (b + 1))
                ps = begin(bk, f"XA{t}")
                for k in range(KC):
                    last = mm(ps[:, :], tokens_qT[:, t % 2, k, :], ctxq[:, k, :], start=(k == 0), stop=(k == KC - 1))
                end(bk, f"XA{t}", last)

            def token_blocks(bk, t):
                ps = begin(bk, f"XT{t}")
                for k in range(KC):
                    last = nc.tensor.transpose(ps[:, k * P:(k + 1) * P], x3n[:, t, k * P:(k + 1) * P], ident[:])
                end(bk, f"XT{t}", last)

            def router(bk):
                ps = begin(bk, "RT")
                for t in range(TB):
                    for k in range(KC):
                        for i, (a, w) in enumerate(((xh, wgh), (xl, wgh), (xh, wgl))):
                            last = mm(ps[:, t * NE:(t + 1) * NE], a[:, k, t * P:(t + 1) * P], w[:, k, :],
                                      start=(t + k + i == 0), stop=(k == KC - 1 and i == 2),
                                      skip_group_check=True)
                end(bk, "RT", last)

            def count_tokens(bk, b):
                pe.wait_ge(onehot_done, b + 1)
                ps = begin(bk, "CS")
                oh = onehot[:, :, :].rearrange("p t e -> p (t e)")
                n = TB * NE
                mm(ps[:, 0:n], tri[:], oh[:, 0:n], start=True, stop=False, skip_group_check=True)
                for s in range(1, TB):
                    mm(ps[:, s * NE:n], ones_b[:], oh[:, 0:n - s * NE], start=False, stop=False,
                       skip_group_check=True)
                for t in range(TB):
                    last = mm(ps[:, n:n + NE], ones_b[:], oh[:, t * NE:(t + 1) * NE], start=False,
                              stop=(t == TB - 1), skip_group_check=True)
                end(bk, "CS", last)

            def hidden_products(bk, n_tok, n_set, between):
                def part(name, c, cols):
                    ps = begin(bk, name)
                    pe.wait_ge(w13_low, n_set * NS + c + 1)
                    high, low = w13_chunk(w13h, c), w13_chunk(w13l, c)
                    steps = 0
                    for k in range(KC):
                        for w, x_ in ((high, xh), (low, xh), (high, xl)):
                            last = mm(ps[:, 0:n_tok], w[:, k, cols], x_[:, k, 0:n_tok],
                                      start=(steps == 0), stop=(steps == 3 * KC - 1))
                            steps += 1
                    end(bk, name, last)

                for c in range(HC):
                    part(f"a{c}", c, slice(0, P))
                    part(f"b{c}", c, slice(P, 2 * P))
                    between(c)
                part("ab", HC, slice(0, P))

            def down(bk, m, n_set, n_body):
                ps = begin(bk, f"D{m}")
                rows = slice(m * P, (m + 1) * P)
                for c in range(HC):
                    if m == 0:
                        pe.wait_ge(w2_low, n_set * NS + c + 1)
                        pe.wait_ge(hl_done, n_body * NS + c + 1)
                    for i, (a, w) in enumerate(((hh, w2h), (hl, w2h), (hh, w2l))):
                        mm(ps[:, :], a[:, c, rows], w[:, c, :], start=(c + i == 0), stop=False)
                if m == 0:
                    pe.wait_ge(w2_low, (n_set + 1) * NS)
                    pe.wait_ge(hl_done, n_body * NS + NS)
                mm(ps[:, :], hh[:, HC, rows], w2h[:, HC, :], start=False, stop=False)
                end(bk, f"D{m}", mm(ps[:, :], hh[:, HC, rows], w2l[:, HC, :], start=False, stop=True))

            for t in range(TB):
                token_quantised_blocks(before, t, t)
                cross_attention(before, t, 0)
            for t in range(TB):
                pe.wait_ge(x3n_done, t + 1)
                token_blocks(before, t)
            for t in range(TB):
                landed(before, f"XT{t}")
            pe.wait_ge(wg_low, 1)
            pe.wait_ge(route_consts, 4)

            def shared(b, ahead):
                bk = shared_banks(b, ahead)

                def between(c):
                    if c == 0:
                        router(bk)
                    if c == 1:
                        count_tokens(bk, b)
                    if ahead:
                        if c < TB:
                            token_quantised_blocks(bk, c, (b + 1) * TB + c)
                        if c:
                            cross_attention(bk, c - 1, b + 1)

                hidden_products(bk, T, 0, between)
                down(bk, 0, 0, b)
                down(bk, 1, 0, b)
                down(bk, 2, 0, b)
                if not ahead:
                    pe.wait_ge(expert_in, 16)
                for t in range(TB if ahead else CAP_T):
                    if ahead:
                        pe.wait_ge(x3n_done, (b + 1) * TB + t + 1)
                    token_blocks(bk, t)
                down(bk, 3, 0, b)
                for t in range(TB if ahead else CAP_T):
                    landed(bk, f"XT{t}")

            with pe.Fori(0, B - 1) as b:
                shared(b, True)
            shared(B - 1, False)

            def expert(e, ahead):
                bk = expert_banks(e, ahead)
                hidden_products(bk, CAP, e + 1, lambda c: None)
                if ahead:
                    pe.wait_ge(expert_in, 16 * (e + 2))
                    for t in range(CAP_T):
                        token_blocks(bk, t)
                for m in range(CAP_T):
                    down(bk, m, e + 1, B + e)
                if ahead:
                    for t in range(CAP_T):
                        landed(bk, f"XT{t}")

            with pe.Fori(0, NE - 1) as e:
                expert(e, True)
            expert(NE - 1, False)

        @block.scalar
        def _(act):
            A = nc.scalar.activation

            def full(bk, name):
                bank, n = bk.use(name)
                act.wait_ge(bk.filled[bank], n + 1)
                return psum[bank]

            def high(dst, src):
                A(dst, src, ACT.Copy).then_inc(hi_done, 1)

            def weight_tile(bk, t):
                full(bk, f"w_{t}")
                high(w_dst(t, True), blocks(bk.use(f"w_{t}")[0]))

            def query_head(bk, h, ready_ss):
                ps = full(bk, f"Q{h}")
                high(qTh[:, h, :], ps[:, :])
                ready_ss()
                A(qsq[:], ps[:, :], ACT.Square).then_inc(sq_done, 1)

            def keep(bk, name, dst, sq=None):
                ps = full(bk, name)
                bank = bk.use(name)[0]
                last = A(dst[:], ps[:, :], ACT.Copy)
                if sq is not None:
                    last = A(sq[:], ps[:, :], ACT.Square)
                last.then_inc(bk.freed[bank], 1)

            def normed_keys_high(bk):
                bank, n = bk.use("RK")
                act.wait_ge(bk.freed[bank], n + 1)
                high(kTh[:], kraw[:])

            def w13_high_part(c, n):
                act.wait_ge(w13_in[c], 32 * (n + 1))
                A(w13_chunk(w13h, c), w13_chunk(w13st, c), ACT.Copy).then_inc(w13_high, 1)

            def softmax_exp(u, h):
                for j in range(TB):
                    c = 4 * h + j
                    if j % 2 == 0:
                        act.wait_ge(bias_done, 8 * u + 2 * h + j // 2 + 1)
                    A(probs[:, P_OFF[j]:P_OFF[j + 1]], psum[j][:, 0:(j + 1) * P], ACT.Exp,
                      bias=nbias[:, c:c + 1], scale=sc[:, c:c + 1],
                      accum_out=rowsum[:, c:c + 1]).then_inc(exp_done, 1)

            def normalise(b, t):
                i = b * TB + t
                act.wait_ge(mean_done, b + 1)
                if i >= 2:
                    full(first, f"x{(i - 2) // TB}{(i - 2) % TB}")
                A(xn[:, i % 2, :], xres[:, i, :], ACT.Identity, bias=shift[:, i:i + 1],
                  scale=rstd[:, i:i + 1]).then_inc(xn_done, 1)

            def ctx_magnitudes(i):
                act.wait_ge(ctx_all_in[i % 4], 16 * (i // 4 + 1))
                A(ctx_all[:, i % 4, :, :], ctx_all[:, i % 4, :, :], ACT.Abs).then_inc(ctx_abs, 1)

            for name, bank in FIRST:
                if name[0] == "w":
                    weight_tile(first, name[2:])
                elif name[0] == "x":
                    b, t = int(name[1]), int(name[2])
                    if t == 0:
                        if b == 2:
                            softmax_exp(0, 0)
                        normalise(b, 0)
                    if t + 1 < TB:
                        normalise(b, t + 1)
                    full(first, name)
                    high(xTh[:, :, (b * TB + t) * P:(b * TB + t + 1) * P], blocks(bank))
                    if b == 3:
                        ctx_magnitudes(4 + t)
                elif name == "V":
                    keep(first, "V", vraw)
                elif name == "K":
                    keep(first, "K", kraw, ksq)
                elif name[0] == "Q":
                    h = int(name[1])
                    query_head(first, h, lambda: full(first, f"SS{h - 1}") if h else None)
                    ctx_magnitudes(h)
                elif name == "VT":
                    full(first, "VT")
                    high(vh[:, :, :], blocks(bank))
                elif name == "RK":
                    normed_keys_high(first)
            act.wait_ge(ctx_read, B * KC // 2)

            def unit(u, g, b, b_next, prep, final):
                bk = banks(u, g, prep, final)
                if prep:
                    for t, _ in PREP_START:
                        weight_tile(bk, t)
                for h in range(REP):
                    if h == 0 and not final:
                        query_head(bk, 0, lambda: None)
                    for c in "ABC":
                        start, n, _ = CHUNKS[c]
                        ps = full(bk, f"{c}{h}")
                        high(pTh[:, start:start + n], ps[:, 0:n])
                    if h < REP - 1:
                        softmax_exp(u, h + 1)
                    if not final:
                        if h:
                            query_head(bk, h, lambda: full(bk, f"SS{h - 1}"))
                        if h == 0:
                            keep(bk, "V", vraw)
                        if h == 2:
                            act.wait_ge(ctxq_out, (u + 1) * 16)
                            keep(bk, "K", kraw, ksq)
                    if prep:
                        for t, _ in PREP_IN_SLOT[h]:
                            weight_tile(bk, t)
                    ps = full(bk, f"PV{h}")
                    high(oTh[:, h, :], ps[:, :])
                    if final:
                        for c in SPLIT_IN_SLOT[h]:
                            w13_high_part(c, 0)
                if not final:
                    full(bk, "VT")
                    high(vh[:, :, :], blocks(bk.use("VT")[0]))
                    normed_keys_high(bk)
                    softmax_exp(u + 1, 0)
                if prep:
                    for t in O_TILES:
                        weight_tile(bk, t)

            units(act, unit)

            def w2_high_part(c, n):
                act.wait_ge(w2_in[c % 2], 32 * (n * (NS // 2) + c // 2 + 1))
                A(w2h[:, c, :], w2st[:, c % 2, :], ACT.Copy).then_inc(w2_high, 1)

            def quantised_blocks(bk, t):
                ps = full(bk, f"QT{t}").bitcast(BF16)
                A(tokens_qT[:, t % 2, :, :], ps[:, 0:D].rearrange("p (k n) -> p k n", k=KC), ACT.Copy)\
                    .then_inc(bk.freed[bk.use(f"QT{t}")[0]], 1)

            def tokens_high(bk, t):
                full(bk, f"XT{t}")
                A(xh[:, :, t * P:(t + 1) * P], blocks(bk.use(f"XT{t}")[0]), ACT.Copy).then_inc(xh_done, 1)

            def router_exp(b):
                act.wait_ge(logits_less_max, b + 1)
                A(le[:, :, :], lt[:, :, :], ACT.Exp).then_inc(logits_exp, 1)

            def hidden_act(bk, c, n_tok):
                name, rows = (f"a{c}", P) if c < HC else ("ab", HT)
                ps = full(bk, name)
                last = A(gate_act[0:rows, c % 2, 0:n_tok], ps[0:rows, 0:n_tok], ACT.Silu)
                last.then_inc(bk.freed[bk.use(name)[0]] if c < HC else act_done, 1)

            def hidden_high(bk, c, n_tok):
                rows = P if c < HC else HT
                bank, n = bk.use(f"b{c}" if c < HC else "ab")
                act.wait_ge(bk.freed[bank], n + 1)
                A(hh[0:rows, c, 0:n_tok], hid[0:rows, c % 2, 0:n_tok], ACT.Copy).then_inc(hh_done, 1)

            act.wait_ge(attn_done, 1)
            for t in range(TB):
                w2_high_part(t, 0)
                quantised_blocks(before, t)
            act.wait_ge(wg_in, 16)
            A(wgh[:, :, :], wg[:, :, :], ACT.Copy).then_inc(wg_high, 1)
            for t in range(TB):
                tokens_high(before, t)
            for c in range(TB, NS):
                w2_high_part(c, 0)

            def shared(b, ahead):
                bk = shared_banks(b, ahead)
                for c in range(NS):
                    hidden_act(bk, c, T)
                    if ahead and c < TB:
                        quantised_blocks(bk, c)
                    hidden_high(bk, c, T)
                    if c == 0:
                        router_exp(b)
                    if not ahead and c:
                        w13_high_part(c - 1, 1)
                if ahead:
                    for t in range(TB):
                        tokens_high(bk, t)
                else:
                    w13_high_part(HC, 1)
                    for t in range(CAP_T):
                        tokens_high(bk, t)

            with act.Fori(0, B - 1) as b:
                shared(b, True)
            shared(B - 1, False)

            def expert(e, ahead, first=False):
                bk = expert_banks(e, ahead)
                for c in range(NS):
                    hidden_act(bk, c, CAP)
                    w2_high_part(c, e + 1)
                    hidden_high(bk, c, CAP)
                    if ahead and c:
                        w13_high_part(c - 1, e + 2)
                if ahead:
                    w13_high_part(HC, e + 2)
                    for t in range(CAP_T):
                        tokens_high(bk, t)
                for m in range(CAP_T):
                    ps = full(bk, f"D{m}")
                    if not first:
                        act.wait_ge(answers_out[m], 16 * e)
                    A(expert_out[:, m, :], ps[:, :], ACT.Copy)\
                        .then_inc(bk.freed[bk.use(f"D{m}")[0]], 1)

            expert(0, True, True)
            with act.Fori(1, NE - 1) as e:
                expert(e, True)
            expert(NE - 1, False)

        @block.vector
        def _(dve):
            V = nc.vector

            def full(bk, name):
                bank, n = bk.use(name)
                dve.wait_ge(bk.filled[bank], n + 1)
                return psum[bank]

            def low(bk, name, dst, src, hi_src, hi_count):
                dve.wait_ge(hi_done, hi_count)
                V.tensor_tensor(dst, src, hi_src.bitcast(F32), ALU.subtract)\
                    .then_inc(bk.freed[bk.use(name)[0]], 1)

            def weight_low(bk, t, n):
                bank = bk.use(f"w_{t}")[0]
                low(bk, f"w_{t}", w_dst(t, False), blocks(bank), w_dst(t, True), n)

            def flat(ap):
                return ap.rearrange("p a d -> p (a d)")

            def inverse_root(y, n, src, scale, eps):
                v, t = chain_v[:, 0:n], chain_t[:, 0:n]
                V.tensor_scalar(v, src, scale, eps, ALU.mult, ALU.add)
                dve.drain()
                V.tensor_scalar(y.bitcast(I32), v.bitcast(I32), 1, None, ALU.logical_shift_right)
                dve.drain()
                V.tensor_scalar(y.bitcast(I32), y.bitcast(I32), -1.0, float(0x5F3759DF), ALU.mult, ALU.add)
                for _ in range(3):
                    dve.drain()
                    V.tensor_tensor(t, v, y, ALU.mult)
                    dve.drain()
                    V.tensor_tensor(t, t, y, ALU.mult)
                    dve.drain()
                    V.tensor_scalar(t, t, -0.5, 1.5, ALU.mult, ALU.add)
                    dve.drain()
                    last = V.tensor_tensor(y, y, t, ALU.mult)
                dve.drain()
                return last

            def tile_stats(tile, t, stats=stats):
                V.bn_stats(stats[:, t, :], flat(xres[:, bass.ds(tile, 1), :]))

            def finish_norm(t0, n=TB, stats=stats, mv=mv):
                dve.drain()
                for t in range(n):
                    V.bn_aggr(mv[:, t, :], stats[:, t, :])
                dve.drain()
                V.tensor_copy(mean[:, bass.ds(t0, n)], flat(mv[:, 0:n, 0:1]))
                inverse_root(rstd[:, bass.ds(t0, n)], n, flat(mv[:, 0:n, 1:2]), 1.0, LN_EPS)

            def layer_norm_rows(t0):
                for t in range(TB):
                    tile_stats(t0 + t, t)
                finish_norm(t0)

            def query_low(bk, h, n, n_sq):
                dve.wait_ge(sq_done, n_sq)
                low(bk, f"Q{h}", qTl[:, h, :], psum[bk.use(f"Q{h}")[0]][:, :], qTh[:, h, :], n)

            def take_sums(bk, h):
                ps = full(bk, f"SS{h}")
                V.tensor_copy(ss[:, 4 * h:4 * h + (8 if h == REP - 1 else 4)],
                              ps[:, 0:8 if h == REP - 1 else 4]).then_inc(bk.freed[bk.use(f"SS{h}")[0]], 1)

            def key_norms():
                dve.drain()
                inverse_root(sc[:, :], 20, ss[:, :], 1.0 / HD, QK_EPS)
                V.tensor_scalar(sc[:, 0:16], sc[:, 0:16], SCALE, None, ALU.mult).then_inc(norms_done, 1)

            def normed_keys(bk):
                ps = full(bk, "RK")
                V.scalar_tensor_tensor(out=kraw[:], in0=kraw[:], scalar=qk_scale[:, 0:1], in1=ps[:, :],
                                       op0=ALU.mult, op1=ALU.mult).then_inc(bk.freed[bk.use("RK")[0]], 1)

            def keys_low(bk, n):
                dve.wait_ge(hi_done, n)
                V.tensor_tensor(kTl[:], kraw[:], kTh[:].bitcast(F32), ALU.subtract).then_inc(k_ready, 1)

            def softmax_max(u, h):
                for j in range(TB):
                    c = 4 * h + j
                    dve.wait_ge(s_filled, 16 * u + c + 1)
                    V.tensor_reduce(mx[:, c:c + 1], psum[j][:, 0:(j + 1) * P], AX.X, ALU.max)
                    if j % 2:
                        dve.drain()
                        V.scalar_tensor_tensor(out=nbias[:, c - 1:c + 1], in0=mx[:, c - 1:c + 1], scalar=-1.0,
                                               in1=sc[:, c - 1:c + 1], op0=ALU.mult, op1=ALU.mult)\
                            .then_inc(bias_done, 1)

            def softmax_norm(u, h):
                dve.wait_ge(exp_done, 16 * u + 4 * h + 4)
                V.reciprocal(rinv[:, 0:4], rowsum[:, 4 * h:4 * h + 4])
                dve.drain()
                for j in range(TB):
                    cols = slice(P_OFF[j], P_OFF[j + 1])
                    last = V.tensor_scalar(probs[:, cols], probs[:, cols], rinv[:, j:j + 1], None, ALU.mult)
                last.then_inc(norm_done, 1)

            dve.wait_ge(scales_in, 32)
            V.tensor_tensor(qk_scale[:], qs_col[:, 0:1], qs_col[:, 1:2], ALU.mult)

            def x_low(b, t):
                cols = slice((b * TB + t) * P, (b * TB + t + 1) * P)
                name = f"x{b}{t}"
                low(first, name, xTl[:, :, cols], blocks(first.use(name)[0]), xTh[:, :, cols],
                    HI_FIRST[name] + 1)

            def shift_of(t0, n):
                V.scalar_tensor_tensor(out=shift[:, t0:t0 + n], in0=mean[:, t0:t0 + n], scalar=-1.0,
                                       in1=rstd[:, t0:t0 + n], op0=ALU.mult, op1=ALU.mult)\
                    .then_inc(mean_done, n // TB)

            dve.wait_ge(x_in[0], 16)
            layer_norm_rows(0)
            shift_of(0, TB)
            for i, t in enumerate(TILES):
                if i == EARLY_TILES:
                    for n in range(TB):
                        x_low(0, n)
                weight_low(first, t, HI_FIRST[f"w_{t}"] + 1)
            for h in range(REP):
                query_low(first, h, HI_FIRST[f"Q{h}"] + 1, h + 1)
                if h:
                    take_sums(first, h - 1)
                if h < B - 1:
                    dve.wait_ge(x_in[h + 1], 16)
                    for t in range(TB):
                        tile_stats((h + 1) * TB + t, h * TB + t, first_stats)
            finish_norm(TB, NT - TB, first_stats, first_mv)
            shift_of(TB, NT - TB)
            take_sums(first, REP - 1)
            key_norms()
            low(first, "VT", vl[:, :, :], blocks(first.use("VT")[0]), vh[:, :, :], HI_FIRST["VT"] + 1)
            for t in range(TB):
                x_low(1, t)
            normed_keys(first)
            keys_low(first, HI_FIRST["RK"] + 1)
            softmax_max(0, 0)
            softmax_norm(0, 0)

            for i in range(2 * TB):
                x_low(2 + i // TB, i % TB)
                dve.wait_ge(ctx_abs, i + 1)
                V.tensor_reduce(ctx_part[:, i:i + 1], ctx_all[:, i % 4, :, :].rearrange("p k n -> p (k n)"),
                                AX.X, ALU.max).then_inc(ctx_read, 1)
            dve.drain()
            V.tensor_reduce(amax[:, 0:1], ctx_part[:, 0:B * KC // 2], AX.X, ALU.max).then_inc(ctx_amax, 1)

            def largest_magnitude(most, least, dst):
                dve.drain()
                V.tensor_reduce(extremes[:, 0:1], most, AX.X, ALU.max)
                V.tensor_reduce(extremes[:, 1:2], least, AX.X, ALU.min)
                dve.drain()
                return V.scalar_tensor_tensor(out=dst, in0=extremes[:, 1:2], scalar=-1.0, in1=extremes[:, 0:1],
                                              op0=ALU.mult, op1=ALU.max)

            def scale_from(src, dst):
                V.tensor_scalar(dst, src, FP8_EPS, None, ALU.max)
                dve.drain()
                V.reciprocal(dst, dst)
                dve.drain()
                V.tensor_scalar(dst, dst, FP8_MAX, None, ALU.mult)
                dve.drain()

            dve.wait_ge(ctx_amax_all, 1)
            scale_from(amax[:, 1:2], f8scale[:, 0:1])

            def to_fp8(y, m, scale, dst):
                V.tensor_scalar(y, y, scale, FP8_MAX, ALU.mult, ALU.min)
                dve.drain()
                V.tensor_scalar(m.bitcast(I32), y.bitcast(I32), EXPONENT, None, ALU.bitwise_and)
                dve.drain()
                V.tensor_scalar(m, m, FP8_LEAST, ROUND_AT, ALU.max, ALU.mult)
                dve.drain()
                V.scalar_tensor_tensor(out=y, in0=y, scalar=-FP8_MAX, in1=m, op0=ALU.max, op1=ALU.add)
                dve.drain()
                return V.tensor_tensor(dst, y, m, ALU.subtract)

            def quantise_ctx(u, half):
                if half == 0:
                    dve.wait_ge(ctx_in, (u + 1) * 16)
                cols = slice(half * D // 2, (half + 1) * D // 2)
                last = to_fp8(ctx_stage[:, cols], ctx_m[:], f8scale[:, 0:1], ctx_q[:, cols])
                if half == 1:
                    last.then_inc(ctxq_done, 1)

            def row_extremes(t):
                row = xres[:, bass.ds(t, 1), :].rearrange("p a d -> p (a d)")
                V.tensor_reduce(rowmax[:, bass.ds(t, 1)], row, AX.X, ALU.max)
                V.tensor_reduce(rowmin[:, bass.ds(t, 1)], row, AX.X, ALU.min)

            def w13_low_part(c, n):
                dve.wait_ge(w13_high, n * NS + c + 1)
                V.tensor_tensor(w13_chunk(w13l, c), w13_chunk(w13st, c), w13_chunk(w13h, c).bitcast(F32),
                                ALU.subtract).then_inc(w13_low, 1)

            def unit(u, g, b, b_next, prep, final):
                bk = banks(u, g, prep, final)

                last_group = isinstance(g, int)
                previous_norm = last_group and not (isinstance(b, int) and b == 0)

                def hi(name):
                    return hi_at(u, g, prep, final, name)

                if prep:
                    for t, _ in PREP_START:
                        weight_low(bk, t, hi(f"w_{t}"))
                for h in range(REP):
                    if h == 0 and not final:
                        query_low(bk, 0, hi("Q0"), REP * (u + 1) + 1)
                    if h < REP - 1:
                        softmax_max(u, h + 1)
                    for c in "ABC":
                        start, n, _ = CHUNKS[c]
                        low(bk, f"{c}{h}", pTl[:, start:start + n], psum[bk.use(f"{c}{h}")[0]][:, 0:n],
                            pTh[:, start:start + n], hi(f"{c}{h}"))
                    if h and not final:
                        query_low(bk, h, hi(f"Q{h}"), REP * (u + 1) + h + 1)
                    if h < REP - 1:
                        softmax_norm(u, h + 1)
                    if prep:
                        for t, _ in PREP_IN_SLOT[h]:
                            weight_low(bk, t, hi(f"w_{t}"))
                    low(bk, f"PV{h}", oTl[:, h, :], psum[bk.use(f"PV{h}")[0]][:, :], oTh[:, h, :], hi(f"PV{h}"))
                    if not final:
                        take_sums(bk, h)
                    if h < 2:
                        quantise_ctx(u, h)
                    if previous_norm:
                        row_extremes((b - 1) * TB + h)
                    if final and h >= 2:
                        for t in (2 * h - 4, 2 * h - 3):
                            tile_stats((b - 1) * TB + t, t, first_stats)
                    if final:
                        for c in SPLIT_IN_SLOT[h]:
                            w13_low_part(c, 0)
                if not final:
                    low(bk, "VT", vl[:, :, :], blocks(bk.use("VT")[0]), vh[:, :, :], hi("VT"))
                    key_norms()

                def add(m, signal=None):
                    ps = full(bk, f"O{m}")
                    row = xres[:, bass.ds(b * TB + m, 1), :].rearrange("p a d -> p (a d)")
                    V.tensor_tensor(row, row, ps[:, :], ALU.add).then_inc(signal or bk.freed[bk.use(f"O{m}")[0]], 1)

                if final:
                    for m in range(TB):
                        add(m, attn_done if m == TB - 1 else None)
                        dve.drain()
                        row_extremes(b * TB + m)
                        tile_stats(b * TB + m, TB + m, first_stats)
                    return
                add(0)
                add(1)
                normed_keys(bk)
                keys_low(bk, hi("KN"))
                add(2)
                softmax_max(u + 1, 0)
                add(3)
                softmax_norm(u + 1, 0)
                if previous_norm:
                    layer_norm_rows((b - 1) * TB)
                if prep:
                    for t in O_TILES:
                        weight_low(bk, t, hi(f"w_{t}"))

            units(dve, unit)

            finish_norm((B - 2) * TB, 2 * TB, first_stats, first_mv)
            for e in (rowmax, rowmin):
                V.tensor_tensor(e[:], e[:], mean[:], ALU.subtract)
            dve.drain()
            for e in (rowmax, rowmin):
                V.tensor_tensor(e[:], e[:], rstd[:], ALU.mult)
            largest_magnitude(rowmax[:], rowmin[:], amax[:, 2:3]).then_inc(x_amax, 1)
            dve.wait_ge(x_amax_all, 1)
            scale_from(amax[:, 3:4], f8scale[:, 1:2])
            V.tensor_scalar(f8scale[:, 3:4], amax[:, 1:2], FP8_EPS, 1.0 / FP8_MAX, ALU.max, ALU.mult)
            V.tensor_scalar(f8scale[:, 2:3], amax[:, 3:4], FP8_EPS, 1.0 / FP8_MAX, ALU.max, ALU.mult)
            dve.drain()
            V.tensor_tensor(f8scale[:, 2:3], f8scale[:, 2:3], f8scale[:, 3:4], ALU.mult)
            dve.drain()

            def quantise_tokens(tile, t):
                V.tensor_scalar(q_y[:], flat(xres[:, bass.ds(tile, 1), :]),
                                mean[:, bass.ds(tile, 1)], rstd[:, bass.ds(tile, 1)],
                                ALU.subtract, ALU.mult)
                dve.drain()
                to_fp8(q_y[:], q_m[:], f8scale[:, 1:2], tokens_q[:, t % 2, :]).then_inc(quantised, 1)
                dve.drain()

            def add_cross_attention(bk, tile, t, b):
                ps = full(bk, f"XA{t}")
                dve.wait_ge(mask_read, b * TB + t)
                dve.wait_ge(mask_in, 16 * (b + 1))
                V.scalar_tensor_tensor(out=attended[:], in0=ps[:, :], scalar=f8scale[:, 2:3], in1=mask_b[:],
                                       op0=ALU.mult, op1=ALU.add).then_inc(bk.freed[bk.use(f"XA{t}")[0]], 1)
                dve.drain()
                row = flat(xres[:, bass.ds(tile, 1), :])
                V.tensor_tensor(row, row, attended[:], ALU.add).then_inc(mask_read, 1)

            def normalise_batch(b, first_batch=False):
                dve.drain()
                layer_norm_rows(b * TB)
                if not first_batch:
                    dve.wait_ge(tokens_sent, 16 * TB * b)
                for t in range(TB):
                    tile = b * TB + t
                    V.tensor_scalar(x3n[:, t, :], flat(xres[:, bass.ds(tile, 1), :]),
                                    mean[:, bass.ds(tile, 1)], rstd[:, bass.ds(tile, 1)],
                                    ALU.subtract, ALU.mult).then_inc(x3n_done, 1)

            def tokens_low(bk, t, n):
                dve.wait_ge(xh_done, n)
                name = f"XT{t}"
                cols = slice(t * P, (t + 1) * P)
                V.tensor_tensor(xl[:, :, cols], blocks(bk.use(name)[0]), xh[:, :, cols].bitcast(F32),
                                ALU.subtract).then_inc(bk.freed[bk.use(name)[0]], 1)

            def over_experts(ap):
                return ap.rearrange("p (t a) -> p t a", a=1).to_broadcast([P, TB, NE])

            def over_tiles(ap):
                return ap.rearrange("p (a e) -> p a e", a=1).to_broadcast([P, TB, NE])

            def choose_expert(bk, b):
                ps = full(bk, "RT")
                V.tensor_copy(lg[:].rearrange("p t e -> p (t e)"), ps[:, 0:TB * NE])\
                    .then_inc(bk.freed[bk.use("RT")[0]], 1)
                dve.drain()
                V.tensor_reduce(r_max[:], lg[:], AX.X, ALU.max)
                dve.drain()
                V.tensor_tensor(lt[:], lg[:], over_experts(r_max[:]), ALU.subtract).then_inc(logits_less_max, 1)
                dve.drain()
                V.tensor_scalar(pos[:], lt[:], 0.0, float(NE), ALU.is_lt, ALU.mult)
                dve.drain()
                V.tensor_tensor(pos[:], pos[:], over_tiles(expert_id[:]), ALU.add)
                dve.drain()
                V.tensor_reduce(r_idx[:], pos[:], AX.X, ALU.min)
                dve.drain()
                V.tensor_tensor(onehot[:], over_tiles(expert_id[:]), over_experts(r_idx[:]), ALU.is_equal)\
                    .then_inc(onehot_done, 1)
                dve.wait_ge(logits_exp, b + 1)
                V.tensor_reduce(r_sum[:], le[:], AX.X, ALU.add)
                dve.drain()
                V.reciprocal(gates[:, bass.ds(b * TB, TB)], r_sum[:])

            def place_tokens(bk, b):
                ps = full(bk, "CS")
                n = TB * NE
                V.tensor_tensor(pos[:], ps[:, 0:n].rearrange("p (t e) -> p t e", e=NE), over_tiles(carry[:]),
                                ALU.add)
                dve.drain()
                V.tensor_tensor(carry[:], ps[:, n:n + NE], carry[:], ALU.add)\
                    .then_inc(bk.freed[bk.use("CS")[0]], 1)
                dve.drain()
                V.tensor_tensor(pos[:], pos[:], onehot[:], ALU.mult)
                dve.drain()
                V.tensor_reduce(r_sel[:], pos[:], AX.X, ALU.add)
                V.tensor_scalar(r_t[:], r_idx[:], float(CAP), -1.0, ALU.mult, ALU.add)
                dve.drain()
                V.tensor_scalar(r_keep[:], r_sel[:], CAP + 0.5, None, ALU.is_lt)
                V.tensor_tensor(r_t[:], r_t[:], r_sel[:], ALU.add)
                dve.drain()
                g = gates[:, bass.ds(b * TB, TB)]
                V.tensor_tensor(g, g, r_keep[:], ALU.mult)
                for dst, away in ((slot_r[:, bass.ds(b * TB, TB)], float(NE * CAP - 1)),
                                  (slot_w[:, :], float(2 * NE * CAP))):
                    V.tensor_scalar(r_sum[:], r_t[:], away, None, ALU.subtract)
                    dve.drain()
                    V.tensor_tensor(r_sum[:], r_sum[:], r_keep[:], ALU.mult)
                    dve.drain()
                    last = V.tensor_scalar(dst, r_sum[:], away, None, ALU.add)
                    if away == NE * CAP - 1:
                        dve.drain()
                last.then_inc(slots_done, 1)
                dve.drain()

            def w2_low_part(c, n):
                dve.wait_ge(w2_high, n * NS + c + 1)
                V.tensor_tensor(w2l[:, c, :], w2st[:, c % 2, :], w2h[:, c, :].bitcast(F32), ALU.subtract)\
                    .then_inc(w2_low, 1)

            def hidden(bk, c, n_tok, n_body):
                if c < HC:
                    ps = full(bk, f"b{c}")
                    bank, n = bk.use(f"a{c}")
                    dve.wait_ge(bk.freed[bank], n + 1)
                    V.tensor_tensor(hid[:, c % 2, 0:n_tok], gate_act[:, c % 2, 0:n_tok], ps[:, 0:n_tok], ALU.mult)\
                        .then_inc(bk.freed[bk.use(f"b{c}")[0]], 1)
                    dve.wait_ge(hh_done, n_body * NS + c + 1)
                    V.tensor_tensor(hl[:, c, 0:n_tok], hid[:, c % 2, 0:n_tok], hh[:, c, 0:n_tok].bitcast(F32),
                                    ALU.subtract).then_inc(hl_done, 1)
                else:
                    ps = full(bk, "ab")
                    dve.wait_ge(act_done, n_body + 1)
                    V.tensor_tensor(hid[0:HT, c % 2, 0:n_tok], gate_act[0:HT, c % 2, 0:n_tok], ps[HT:P, 0:n_tok],
                                    ALU.mult).then_inc(bk.freed[bk.use("ab")[0]], 1)
                    dve.wait_ge(hh_done, n_body * NS + c + 1)
                    V.tensor_tensor(hh[HT:P, c, 0:n_tok], hid[0:HT, c % 2, 0:n_tok],
                                    hh[0:HT, c, 0:n_tok].bitcast(F32), ALU.subtract).then_inc(hl_done, 1)

            def add_shared(bk, tile, m):
                ps = full(bk, f"D{m}")
                row = flat(xres[:, bass.ds(tile, 1), :])
                V.tensor_tensor(row, row, ps[:, :], ALU.add).then_inc(bk.freed[bk.use(f"D{m}")[0]], 1)

            for t in range(TB):
                if t >= 2:
                    full(before, f"QT{t - 2}")
                quantise_tokens(t, t)
                w2_low_part(t, 0)
                if t:
                    add_cross_attention(before, t - 1, t - 1, 0)
            add_cross_attention(before, TB - 1, TB - 1, 0)
            normalise_batch(0, True)
            dve.wait_ge(wg_high, 1)
            V.tensor_tensor(wgl[:, :, :], wg[:, :, :], wgh[:, :, :].bitcast(F32), ALU.subtract).then_inc(wg_low, 1)
            for t in range(TB):
                tokens_low(before, t, t + 1)
            for c in range(TB, NS):
                w2_low_part(c, 0)
            dve.wait_ge(route_consts, 4)

            def shared(b, ahead):
                bk = shared_banks(b, ahead)
                next_tile = (b + 1) * TB
                for c in range(NS):
                    if ahead and c < TB:
                        if c >= 2:
                            full(bk, f"QT{c - 2}")
                        quantise_tokens(next_tile + c, c)
                    hidden(bk, c, T, b)
                    if not ahead and c:
                        w13_low_part(c - 1, 1)
                    if c == 0:
                        choose_expert(bk, b)
                    if c == 3:
                        place_tokens(bk, b)
                    if ahead and 1 <= c <= TB:
                        add_cross_attention(bk, next_tile + c - 1, c - 1, b + 1)
                if ahead:
                    normalise_batch(b + 1)
                add_shared(bk, b * TB, 0)
                add_shared(bk, b * TB + 1, 1)
                if not ahead:
                    w13_low_part(HC, 1)
                add_shared(bk, b * TB + 2, 2)
                for t in range(TB if ahead else CAP_T):
                    tokens_low(bk, t, (b + 1) * TB + t + 1)
                add_shared(bk, b * TB + 3, 3)

            with dve.Fori(0, B - 1) as b:
                shared(b, True)
            shared(B - 1, False)

            def expert(e, ahead):
                bk = expert_banks(e, ahead)
                for c in range(NS):
                    hidden(bk, c, CAP, B + e)
                    w2_low_part(c, e + 1)
                    if ahead and c:
                        w13_low_part(c - 1, e + 2)
                if ahead:
                    w13_low_part(HC, e + 2)
                    for t in range(CAP_T):
                        tokens_low(bk, t, NT + e * CAP_T + CAP_T + t + 1)

            with dve.Fori(0, NE - 1) as e:
                expert(e, True)
            expert(NE - 1, False)

            for i in range(NT):
                dve.wait_ge(answers_in[i // TB], 16 * TB)
                last = V.scalar_tensor_tensor(out=xres[:, i, :], in0=gathered[:, i, :], scalar=gates[:, i:i + 1],
                                              in1=xres[:, i, :], op0=ALU.mult, op1=ALU.add)
                if i % TB == TB - 1:
                    last.then_inc(result_done, 1)


_INS = ['x', 'ctx_2048', 'mask_Bx1xS2_ff0', 'L0_attn_Wq', 'L0_attn_Wk', 'L0_attn_Wv', 'L0_attn_Wo',
        'L0_attn_q_scale', 'L0_attn_k_scale', 'L0_ffn_Wg', 'L0_ffn_W1', 'L0_ffn_W3', 'L0_ffn_W2',
        'L0_ffn_sw1', 'L0_ffn_sw3', 'L0_ffn_sw2']
_OUTS = [((B, T, D), 'float32')]


def kernel(**inputs):
    import numpy as _np
    import concourse.bacc as _bacc
    from concourse import mybir as _mybir
    from concourse.bass_utils import run_bass_kernel_spmd as _run

    nc = _bacc.Bacc("TRN2", target_bir_lowering=False, num_devices=1)
    arrays, args = {}, []
    for name in _INS:
        a = _np.ascontiguousarray(inputs[name])
        arrays[f"in_{name}_dram"] = a
        args.append(nc.dram_tensor(f"in_{name}_dram", a.shape, _mybir.dt.from_np(a.dtype), kind="ExternalInput").ap())
    for i, (shape, dtype) in enumerate(_OUTS):
        dt = _mybir.dt.from_np(_np.dtype(dtype))
        args.append(nc.dram_tensor(f"out_{i}_dram", shape, dt, kind="ExternalOutput").ap())
    decoder(nc, *args)
    r = _run(nc, [arrays], core_ids=[0])
    got = tuple(r.results[0][f"out_{i}_dram"] for i in range(len(_OUTS)))
    return got[0]
```

```python
from contextlib import ExitStack

import concourse.bass as bass
from concourse import mybir

P = 128
B, T, D = 4, 512, 512
NH, NKV, HD = 16, 4, 128
REP = NH // NKV
KC = D // P
TB = T // P
NT = B * TB
UNITS = NKV * B
LN_EPS = 1e-5
QK_EPS = 1e-6
SCALE = float(HD) ** -0.5
MASKED = -1e30
FP8_MAX = 448.0
FP8_EPS = 1e-12
FP8_LEAST = 2.0 ** -6
ROUND_AT = 1.5 * 2.0 ** 20
EXPONENT = 0x7F800000
NE, H = 8, 704
CAP = B * T // NE
CAP_T = CAP // P
NOBODY = 2 * B * T
HC = H // P
HT = H - HC * P
W13 = 2 * H
NS = HC + 1

ALU = mybir.AluOpType
ACT = mybir.ActivationFunctionType
AX = mybir.AxisListType
F32 = mybir.dt.float32
F32R = mybir.dt.float32r
BF16 = mybir.dt.bfloat16
I32 = mybir.dt.int32
RMAX = bass.bass_isa.ReduceOp.max

P_OFF = [P * (j * (j + 1) // 2) for j in range(TB + 1)]
PT_OFF = {0: 0, 1: 512, 3: 896, 2: 1024}
CHUNKS = {"A": (0, 512, [0]), "B": (512, 512, [1, 3]), "C": (1024, 256, [2])}

TILES = ["q0", "v", "q1", "q2", "k", "q3", "o0", "o1", "o2", "o3"]
QKV_TILES, O_TILES = TILES[:6], TILES[6:]
PREP_START = [("q0", 5), ("v", 6)]
PREP_IN_SLOT = [[("q1", 6)], [("q2", 6), ("k", 7)], [("q3", 7)], []]
RING = 2
IN_RING = 8
EARLY_TILES = 4
FIRST_STAGE = IN_RING


class Banks:

    def __init__(self, uses, base, filled, freed):
        self.filled, self.freed = filled, freed
        self.at, seen = {}, {}
        for name, bank in uses:
            self.at[name] = (bank, seen.get(bank, 0))
            seen[bank] = seen.get(bank, 0) + 1
        self.base = base

    def use(self, name):
        bank, n = self.at[name]
        return bank, self.base[bank] + n


def count(uses, of=range(8)):
    return {b: sum(1 for _, bank in uses if bank == b) for b in of}


def unit_uses(prep, final):
    uses = [(f"w_{t}", bank) for t, bank in PREP_START] if prep else []
    for h in range(REP):
        uses += [(f"Q{h}", 7), (f"A{h}", 4), (f"B{h}", 5), (f"C{h}", 6)]
        uses += [("V", 7)] if h == 0 else [("K", 6)] if h == 2 else []
        uses += [(f"w_{t}", bank) for t, bank in PREP_IN_SLOT[h]] if prep else []
        uses += [(f"PV{h}", 4), (f"SS{h}", 5)]
    uses += [("VT", 6), ("O0", 7), ("O1", 4), ("RK", 5), ("O2", 6), ("O3", 4)]
    if prep:
        uses += [(f"w_{t}", 4 + i % 4) for i, t in enumerate(O_TILES)]
    if final:
        uses = [u for u in uses if u[0][0] in "ABCPO"]
    return uses


def shared_uses(ahead):
    uses = []
    for c in range(HC):
        uses += [(f"a{c}", 2 * (c % 2)), (f"b{c}", 2 * (c % 2) + 1)]
        uses += [("RT", 6)] if c == 0 else [("LT", 7)] if c == 1 else [("CS", 7)] if c == 3 else []
        if ahead:
            uses += [(f"QT{c}", 4)] if c < TB else []
            uses += [(f"XA{c - 1}", 5)] if c else []
    uses += [("ab", 2), ("D0", 6), ("D1", 7), ("D2", 0)]
    uses += [(f"XT{t}", (4, 5, 3, 2)[t]) for t in range(TB if ahead else CAP_T)]
    return uses + [("D3", 1)]


def expert_uses(ahead):
    uses = []
    for c in range(HC):
        uses += [(f"a{c}", 2 * (c % 2)), (f"b{c}", 2 * (c % 2) + 1)]
    uses += [("ab", 2)]
    uses += [(f"XT{t}", 4 + t) for t in range(CAP_T)] if ahead else []
    return uses + [("D0", 6), ("D1", 7)]


def before_shared_uses():
    uses = []
    for t in range(TB):
        uses += [(f"QT{t}", 6 + t % 2), (f"XA{t}", 4 + t % 2)]
    return uses + [(f"XT{t}", t) for t in range(TB)]


def first_uses():
    w = [(f"w_{t}", 4 + i % 4) for i, t in enumerate(TILES)]
    tokens = [[(f"x{b}{t}", 4 + t) for t in range(TB)] for b in range(B)]
    uses = w[:EARLY_TILES] + tokens[0] + w[EARLY_TILES:] + [("V", 6), ("K", 7)]
    for h in range(REP):
        uses += [(f"Q{h}", 4 + h % 2)] + ([(f"SS{h - 1}", 6)] if h else [])
    uses += [(f"SS{REP - 1}", 6), ("VT", 7)] + tokens[1] + [("RK", 6)]
    return uses + tokens[2] + tokens[3]


def decoder(nc, x, ctx_in_dram, mask_dram, Wq, Wk, Wv, Wo, q_scale, k_scale, Wg, W1, W3, W2, sw1, sw3, sw2, out):
    nc_stack = ExitStack()
    with nc_stack as stack:

        def sem(name):
            return stack.enter_context(nc.semaphore(name))

        base = nc.sbuf_base + (-nc.sbuf_base) % 32
        room = nc.sbuf_usable_end - 64 - base
        slab = stack.enter_context(nc.sbuf_tensor("slab", [P, (room - 64) // 4], F32))
        place = [base + 32]

        def sb(name, shape, dtype):
            n = 1
            for s in shape[1:]:
                n *= s
            size = n * (2 if dtype == BF16 else 4)
            t = nc.alloc_sbuf_tensor_at(name, shape, dtype, offset=place[0])
            place[0] += size + (-size) % 32
            assert place[0] <= base + room, (name, place[0] - base - room)
            return t

        psum = [stack.enter_context(nc.psum_tensor(f"bank{i}", [P, 512], F32)) for i in range(8)]

        xres = sb("xres", [P, NT, D], F32)
        ident = sb("ident", [P, P], F32)
        ident_b = sb("ident_b", [P, P], BF16)
        causal = sb("causal", [P, P], BF16)
        ones = sb("ones", [P, 2], F32)
        qs_col = sb("qs_col", [P, 2], F32)
        qk_scale = sb("qk_scale", [P, 1], F32)
        stats = sb("stats", [P, TB, 6], F32)
        mv = sb("mv", [P, TB, 2], F32)
        mean = sb("mean", [P, NT], F32)
        rstd = sb("rstd", [P, NT], F32)
        chain_v = sb("chain_v", [P, 20], F32)
        chain_t = sb("chain_t", [P, 20], F32)
        shift = nc.alloc_sbuf_tensor_at("shift", [P, NT], F32, offset=place[0])
        rowmax = sb("rowmax", [P, NT], F32)
        rowmin = sb("rowmin", [P, NT], F32)
        amax = sb("amax", [P, 4], F32)
        ctx_part = sb("ctx_part", [P, B * KC // 2], F32)
        extremes = sb("extremes", [P, 2], F32)
        f8scale = sb("f8scale", [P, 4], F32)
        common_end = place[0]

        xTh = sb("xTh", [P, KC, B * T], F32R)
        xTl = sb("xTl", [P, KC, B * T], F32R)
        wTh = sb("wTh", [P, 6, D], F32R)
        wTl = sb("wTl", [P, 6, D], F32R)
        wstage_at = place[0]
        wstage = sb("wstage", [P, RING, D], F32)
        woTh = sb("woTh", [P, REP, D], F32R)
        woTl = sb("woTl", [P, REP, D], F32R)
        qTh = sb("qTh", [P, REP, T], F32R)
        qTl = sb("qTl", [P, REP, T], F32R)
        kTh = sb("kTh", [P, T], F32R)
        kTl = sb("kTl", [P, T], F32R)
        vh = sb("vh", [P, TB, HD], F32R)
        vl = sb("vl", [P, TB, HD], F32R)
        otmp = place[0]
        oTh = sb("oTh", [P, REP, T], F32R)
        oTl = sb("oTl", [P, REP, T], F32R)
        xn = nc.alloc_sbuf_tensor_at("xn", [P, 2, D], F32, offset=place[0])
        pTh = sb("pTh", [P, P_OFF[TB]], F32R)
        pTl = sb("pTl", [P, P_OFF[TB]], F32R)
        probs = sb("probs", [P, P_OFF[TB]], F32)
        qsq = sb("qsq", [P, T], F32)
        ctx_m = nc.alloc_sbuf_tensor_at("ctx_m", [P, D // 2], F32, offset=place[0])
        ctx_q = nc.alloc_sbuf_tensor_at("ctx_q", [P, D], BF16, offset=place[0] + D // 2 * 4)
        ksq = sb("ksq", [P, T], F32)
        kraw = sb("kraw", [P, T], F32)
        vraw = sb("vraw", [P, T], F32)
        ss = sb("ss", [P, 20], F32)
        sc = sb("sc", [P, 20], F32)
        mx = sb("mx", [P, 16], F32)
        nbias = sb("nbias", [P, 16], F32)
        rowsum = sb("rowsum", [P, 16], F32)
        rinv = sb("rinv", [P, 4], F32)
        ctx_all = nc.alloc_sbuf_tensor_at("ctx_all", [P, 4, 2, D], F32, offset=otmp)
        first_w = nc.alloc_sbuf_tensor_at("first_w", [P, FIRST_STAGE, D], F32, offset=otmp)
        first_stats = nc.alloc_sbuf_tensor_at("first_stats", [P, NT, 6], F32, offset=place[0])
        first_mv = nc.alloc_sbuf_tensor_at("first_mv", [P, NT, 2], F32, offset=place[0] + NT * 6 * 4)
        ctx_stage = sb("ctx_stage", [P, D], F32)
        zeros = sb("zeros", [P, P], F32)

        place[0] = common_end
        w13h = sb("w13h", [P, KC * W13], F32R)
        w13l = sb("w13l", [P, KC * W13], F32R)
        w13st = sb("w13st", [P, KC * W13], F32)
        w2st = sb("w2st", [P, 2, D], F32)
        assert place[0] <= wstage_at
        w2h = sb("w2h", [P, NS, D], F32R)
        w2l = sb("w2l", [P, NS, D], F32R)
        xh = sb("xh", [P, KC, T], F32R)
        xl = sb("xl", [P, KC, T], F32R)
        hh = sb("hh", [P, NS, T], F32R)
        hl = sb("hl", [P, HC, T], F32R)
        gate_act = sb("gate_act", [P, 2, T], F32)
        hid = sb("hid", [P, 2, T], F32)
        x3n = sb("x3n", [P, TB, D], F32)
        ctxq = sb("ctxq", [P, KC, D], BF16)
        tokens_q = sb("tokens_q", [P, 2, D], BF16)
        tokens_qT = sb("tokens_qT", [P, 2, KC, P], BF16)
        q_at = place[0]
        q_y = sb("q_y", [P, 2, D], F32)
        q_m = sb("q_m", [P, D], F32)
        attended = sb("attended", [P, D], F32)
        mask_b = sb("mask_b", [P, D], F32)
        wg = sb("wg", [P, KC, NE], F32)
        wgh = sb("wgh", [P, KC, NE], F32R)
        wgl = sb("wgl", [P, KC, NE], F32R)
        tri = sb("tri", [P, P], BF16)
        ones_b = sb("ones_b", [P, P], BF16)
        expert_id = sb("expert_id", [P, NE], F32)
        lgT = sb("lgT", [P, T], F32)
        lg = sb("lg", [P, TB, NE], F32)
        lt = sb("lt", [P, TB, NE], F32)
        le = sb("le", [P, TB, NE], F32)
        onehot = sb("onehot", [P, TB, NE], BF16)
        pos = sb("pos", [P, TB, NE], F32)
        carry = sb("carry", [P, NE], F32)
        r_max = sb("r_max", [P, TB], F32)
        r_idx = sb("r_idx", [P, TB], F32)
        r_sum = sb("r_sum", [P, TB], F32)
        r_sel = sb("r_sel", [P, TB], F32)
        r_keep = sb("r_keep", [P, TB], F32)
        r_t = sb("r_t", [P, TB], F32)
        slot_w = sb("slot_w", [P, TB], I32)
        token_code = sb("token_code", [P, TB], F32)
        meta = sb("meta", [P, TB, 2], F32)
        slot_meta = sb("slot_meta", [P, NE * CAP_T, 2], F32)
        slot_token = sb("slot_token", [P, NE * CAP_T], F32)
        row_to = sb("row_to", [P, NE * CAP_T], I32)
        row_from = sb("row_from", [P, NE * CAP_T], I32)
        expert_out = nc.alloc_sbuf_tensor_at("expert_out", [P, CAP_T, D], F32, offset=q_at)
        slot_x = nc.alloc_sbuf_tensor_at("slot_x", [P, CAP_T, D], F32, offset=q_at + CAP_T * D * 4)

        ctxq_dram = nc.dram_tensor("ctxq_dram", [B * T, D], BF16, kind="Internal").ap()
        sent = nc.dram_tensor("sent", [NE * CAP, D], F32, kind="Internal").ap()
        sent_meta = nc.dram_tensor("sent_meta", [NE * CAP, 2], F32, kind="Internal").ap()
        x_shared = nc.dram_tensor("x_shared", [B * T, D], F32, kind="Internal").ap()

        x_in = [sem(f"x_in{b}") for b in range(B)]
        scales_in = sem("scales_in")
        w_in = [sem(f"w_in{r}") for r in range(RING + 2)]
        filled = {b: sem(f"filled{b}") for b in range(4, 8)}
        freed = {b: sem(f"freed{b}") for b in range(4, 8)}
        consts = sem("consts")
        pool_step = sem("pool_step")
        hi_done = sem("hi_done")
        mean_done = sem("mean_done")
        xn_done = sem("xn_done")
        s_filled = sem("s_filled")
        exp_done = sem("exp_done")
        bias_done = sem("bias_done")
        norm_done = sem("norm_done")
        sq_done = sem("sq_done")
        norms_done = sem("norms_done")
        k_ready = sem("k_ready")
        attn_done = sem("attn_done")
        ctx_all_in = [sem(f"ctx_all_in{i}") for i in range(4)]
        ctx_in = sem("ctx_in")
        ctx_abs = sem("ctx_abs")
        first_w_in = [sem(f"first_w_in{i}") for i in range(FIRST_STAGE // 2)]
        ctx_read = sem("ctx_read")
        ctx_amax = sem("ctx_amax")
        ctx_amax_all = sem("ctx_amax_all")
        ctxq_done = sem("ctxq_done")
        ctxq_out = sem("ctxq_out")
        zeros_set = sem("zeros_set")
        sent_zeroed = sem("sent_zeroed")
        x_amax = sem("x_amax")
        x_amax_all = sem("x_amax_all")
        w13_in = [sem(f"w13_in{c}") for c in range(NS)]
        w2_in = [sem(f"w2_in{k}") for k in range(2)]
        w13_high = sem("w13_high")
        w13_low = sem("w13_low")
        w2_high = sem("w2_high")
        w2_low = sem("w2_low")
        ctxq_in = sem("ctxq_in")
        mask_in = sem("mask_in")
        wg_in = sem("wg_in")
        wg_high = sem("wg_high")
        wg_low = sem("wg_low")
        mask_read = sem("mask_read")
        mfull = {b: sem(f"mfull{b}") for b in range(8)}
        mfree = {b: sem(f"mfree{b}") for b in range(8)}
        y_done = sem("y_done")
        shifts_done = sem("shifts_done")
        quantised = sem("quantised")
        x3n_done = sem("x3n_done")
        xh_done = sem("xh_done")
        act_done = sem("act_done")
        hh_done = sem("hh_done")
        hl_done = sem("hl_done")
        logits_less_max = sem("logits_less_max")
        logits_exp = sem("logits_exp")
        onehot_done = sem("onehot_done")
        slots_done = sem("slots_done")
        tokens_sent = sem("tokens_sent")
        expert_in = sem("expert_in")
        meta_zeroed = sem("meta_zeroed")
        meta_sent = sem("meta_sent")
        slot_meta_in = sem("slot_meta_in")
        rows_known = sem("rows_known")
        slot_x_in = [sem(f"slot_x_in{m}") for m in range(CAP_T)]
        route_consts = sem("route_consts")
        x_stored = sem("x_stored")
        answers_out = [sem(f"answers_out{m}") for m in range(CAP_T)]

        block = stack.enter_context(nc.Block())

        FIRST, UNIT, PREP, FINAL = first_uses(), unit_uses(False, False), unit_uses(True, False), unit_uses(False, True)
        n_first, n_unit = count(FIRST), count(UNIT)
        n_prep = {b: n - n_unit[b] for b, n in count(PREP).items()}

        def banks(u, g, prep, final=False):
            return Banks(PREP if prep else FINAL if final else UNIT,
                         {b: n_first[b] + u * n_unit[b] + g * n_prep[b] for b in range(8)}, filled, freed)

        first = Banks(FIRST, {b: 0 for b in range(8)}, filled, freed)

        BEFORE, SHARED, SHARED_LAST = before_shared_uses(), shared_uses(True), shared_uses(False)
        EXPERT, EXPERT_LAST = expert_uses(True), expert_uses(False)
        n_before, n_shared, n_shared_last, n_expert = (count(u) for u in (BEFORE, SHARED, SHARED_LAST, EXPERT))
        assert min(n_before.values()) > 0 and min(n_first[k] for k in range(4, 8)) > 0
        before = Banks(BEFORE, {b: 0 for b in range(8)}, mfull, mfree)

        def shared_banks(b, ahead):
            return Banks(SHARED if ahead else SHARED_LAST,
                         {k: n_before[k] + b * n_shared[k] for k in range(8)}, mfull, mfree)

        def expert_banks(e, ahead):
            start = {k: n_before[k] + (B - 1) * n_shared[k] + n_shared_last[k] for k in range(8)}
            return Banks(EXPERT if ahead else EXPERT_LAST, {k: start[k] + e * n_expert[k] for k in range(8)},
                         mfull, mfree)

        def units(eng, body):
            with eng.Fori(0, NKV - 1) as g:
                with eng.Fori(0, B - 1) as b:
                    body(g * B + b, g, b, b + 1, False, False)
                body(g * B + B - 1, g, B - 1, 0, True, False)
            body((NKV - 1) * B, NKV - 1, 0, 1, False, False)
            with eng.Fori(1, B - 1) as b:
                body((NKV - 1) * B + b, NKV - 1, b, b + 1, False, False)
            body(UNITS - 1, NKV - 1, B - 1, None, False, True)

        SPLIT_IN_SLOT = [[], [0, 1], [2, 3], [4, 5]]

        def high_parts(prep, final):
            names = [f"w_{t}" for t, _ in PREP_START] if prep else []
            for h in range(REP):
                probabilities = [f"A{h}", f"B{h}", f"C{h}"]
                if not final:
                    probabilities = [f"Q{h}"] + probabilities if h == 0 else probabilities + [f"Q{h}"]
                names += probabilities + ([f"w_{t}" for t, _ in PREP_IN_SLOT[h]] if prep else []) + [f"PV{h}"]
            return names + ([] if final else ["VT", "KN"]) + ([f"w_{t}" for t in O_TILES] if prep else [])

        n_hi = len(high_parts(False, False))
        HI_FIRST = {}
        for name, _ in FIRST:
            if name[0] in "wxQ" or name in ("VT", "RK"):
                HI_FIRST[name] = len(HI_FIRST)

        def hi_at(u, g, prep, final, name):
            return len(HI_FIRST) + u * n_hi + g * len(TILES) + high_parts(prep, final).index(name) + 1

        def w_place(i):
            if i < IN_RING:
                return i % RING, wstage[:, i % RING, :]
            return RING + i - IN_RING, (vraw, qsq)[i - IN_RING][:, :]

        def w_src(t, g, ahead):
            if t in "kv":
                return {"k": Wk, "v": Wv}[t][bass.ds(g * P + ahead * P, P), :]
            n = int(t[1])
            if t[0] == "q":
                return Wq[bass.ds(g * REP * P + (ahead * REP + n) * P, P), :]
            return Wo[n * P:(n + 1) * P, bass.ds(g * REP * HD + ahead * REP * HD, REP * HD)]

        def w_dst(t, hi):
            if t[0] == "o":
                m = int(t[1])
                return (woTh if hi else woTl)[:, :, m * P:(m + 1) * P]
            return (wTh if hi else wTl)[:, TILES.index(t), :].rearrange("p (k n) -> p k n", k=KC)

        def w13_chunk(w, c):
            n = P if c < HC else HT
            return w[:, c * KC * 2 * P:(c * 2 * P + 2 * n) * KC].rearrange("p (k n) -> p k n", k=KC)

        def blocks(bank):
            return psum[bank][:, :].rearrange("p (k n) -> p k n", k=4)

        out_rows = out.rearrange("b t d -> (b t) d")
        ctx_rows = ctx_in_dram.rearrange("b k n -> (b k) n")

        @block.sync
        def _(sp):
            x_tiles = x.rearrange("b (t p) d -> b p t d", p=P)

            def load_w(g, i, ahead=0):
                place, dst = w_place(i)
                sp.dma_start(dst, w_src(TILES[i], g, ahead)).then_inc(w_in[place], 16)

            def load_x(b):
                sp.dma_start(xres[:, b * TB:(b + 1) * TB, :], x_tiles[b]).then_inc(x_in[b], 16)

            sp.dma_start(qs_col[:, 0:1], q_scale.rearrange("(p a) -> p a", a=1)).then_inc(scales_in, 16)
            sp.dma_start(qs_col[:, 1:2], k_scale.rearrange("(p a) -> p a", a=1)).then_inc(scales_in, 16)
            def transposed(bk, i):
                bank, n = bk.use(f"w_{TILES[i]}")
                sp.wait_ge(bk.filled[bank], n + 1)

            for b in range(B):
                load_x(b)
                if b == 0:
                    for i in range(FIRST_STAGE):
                        sp.dma_start(first_w[:, i, :], w_src(TILES[i], 0, 0)).then_inc(first_w_in[i // 2], 16)
                    for i in range(FIRST_STAGE, len(TILES)):
                        load_w(0, i)

            def next_group(g, ahead, bk=None):
                for i in range(RING):
                    if bk is not None:
                        transposed(bk, IN_RING - RING + i)
                    load_w(g, i, ahead)

            def rest_of_group(g, ahead):
                last = g + ahead - 1
                bk = banks(last * B + B - 1, last, True)
                for i in range(RING, IN_RING):
                    transposed(bk, i - RING)
                    load_w(g, i, ahead)
                for i, read_by in ((IN_RING + 1, f"SS{REP - 1}"), (IN_RING, "VT")):
                    bank, n = bk.use(read_by)
                    sp.wait_ge(bk.filled[bank], n + 1)
                    load_w(g, i, ahead)
                return bk

            next_group(0, 1)
            with sp.Fori(0, NKV - 2) as g:
                next_group(g, 2, rest_of_group(g, 1))
            rest_of_group(NKV - 1, 0)

            def load_w13(w1, w3, c, wait):
                if wait is not None:
                    sp.wait_ge(w13_low, wait)
                n = P if c < HC else HT
                dst = w13_chunk(w13st, c)
                for i, w in enumerate((w1, w3)):
                    sp.dma_start(dst[:, :, i * n:(i + 1) * n],
                                 w[:, c * P:c * P + n].rearrange("(k p) h -> p k h", p=P)).then_inc(w13_in[c], 16)

            def load_w2(w2_rows, c, wait):
                if wait is not None:
                    sp.wait_ge(w2_low, wait)
                upper, lower = (w2_rows[0:HT, :], w2_rows[HT:P, :]) if c < HC else (w2_rows, w2_rows)
                sp.dma_start(w2st[0:HT, c % 2, :], upper).then_inc(w2_in[c % 2], 16)
                sp.dma_start(w2st[HT:P, c % 2, :], lower).then_inc(w2_in[c % 2], 16)

            def chunk_rows(c):
                return slice(c * P, min(H, (c + 1) * P))

            def expert_rows(w, e, rows):
                return w[bass.ds(e, 1), rows, :].rearrange("a p h -> (a p) h")

            def load_expert_w13(e, n, c):
                w1, w3 = (w[bass.ds(e, 1), :, :].rearrange("a d h -> (a d) h") for w in (W1, W3))
                load_w13(w1, w3, c, (n - 1) * NS + c + 1)

            def load_batch(b):
                sp.dma_start(ctxq[:, :, :], ctxq_dram[bass.ds(b * T, T), :].rearrange("(k p) n -> p k n", p=P))\
                    .then_inc(ctxq_in, 16)
                sp.dma_start(mask_b[:, :], mask_in_rows(b)).then_inc(mask_in, 16)

            def mask_in_rows(b):
                return mask_dram[bass.ds(b, 1), :, :].rearrange("a c n -> (a c n)").partition_broadcast(P)

            sp.wait_ge(norms_done, UNITS)
            for c in range(NS):
                load_w13(sw1, sw3, c, None)
            for c in range(2):
                load_w2(sw2[chunk_rows(c), :], c, None)
            sp.wait_ge(attn_done, 1)
            sp.wait_ge(ctxq_out, 16 * B * KC)
            sp.dma_start(wg[:, :, :], Wg.rearrange("(k p) e -> p k e", p=P)).then_inc(wg_in, 16)
            load_batch(0)
            for c in range(2, NS):
                load_w2(sw2[chunk_rows(c), :], c, c - 1)
            for c in range(NS):
                load_expert_w13(0, 1, c)
            def store_batch(b):
                bank, n = shared_banks(b, True).use(f"D{TB - 1}")
                sp.wait_ge(mfree[bank], n + 1)
                for dst in (out_rows, x_shared):
                    sp.dma_start(dst[bass.ds(b * T, T), :].rearrange("(t p) d -> p t d", p=P),
                                 xres[:, bass.ds(b * TB, TB), :]).then_inc(x_stored, 16)

            def load_expert_w2(e, n, c):
                load_w2(expert_rows(W2, e, chunk_rows(c)), c, n * NS + c - 1)

            for c in range(2):
                load_expert_w2(0, 1, c)
            with sp.Fori(1, B) as b:
                sp.wait_ge(mask_read, b * TB)
                load_batch(b)
                store_batch(b - 1)

            def load_tokens(e):
                sp.dma_start(x3n[:, 0:CAP_T, :], sent[bass.ds(e * CAP, CAP), :].rearrange("(t p) d -> p t d", p=P))\
                    .then_inc(expert_in, 16)

            def load_sets(e, first_w2=0, with_next=True):
                for c in range(NS):
                    if c >= first_w2:
                        load_expert_w2(e - 1, e, c)
                    if with_next:
                        load_expert_w13(e, e + 1, c)

            sp.wait_ge(tokens_sent, NT * 16)
            load_tokens(0)
            sp.wait_ge(meta_sent, NT * 16)
            sp.dma_start(slot_meta[:, :, :], sent_meta.rearrange("(s p) c -> p s c", p=P)).then_inc(slot_meta_in, 16)

            def tokens_transposed(bk):
                bank, n = bk.use(f"XT{CAP_T - 1}")
                sp.wait_ge(bk.filled[bank], n + 1)

            tokens_transposed(shared_banks(B - 1, False))
            load_tokens(1)
            store_batch(B - 1)
            load_sets(1, first_w2=2)
            with sp.Fori(2, NE) as e:
                tokens_transposed(expert_banks(e - 2, True))
                load_tokens(e)
                load_sets(e)
            load_sets(NE, with_next=False)

        @block.gpsimd
        def _(pool):
            nc.gpsimd.memset(ident[:], 0.0).then_inc(pool_step, 1)
            nc.gpsimd.memset(causal[:], 0.0).then_inc(pool_step, 1)
            nc.gpsimd.memset(ones[:], 1.0).then_inc(consts, 1)
            nc.gpsimd.memset(zeros[:], 0.0).then_inc(zeros_set, 1)
            pool.wait_ge(pool_step, 2)
            nc.gpsimd.affine_select(out=ident[:], in_=ident[:], compare_op=ALU.not_equal, fill=1.0, base=0,
                                    pattern=[[-1, P]], channel_multiplier=1).then_inc(pool_step, 1)
            nc.gpsimd.affine_select(out=causal[:], in_=causal[:], compare_op=ALU.is_ge, fill=MASKED, base=0,
                                    pattern=[[-1, P]], channel_multiplier=1).then_inc(consts, 1)
            pool.wait_ge(pool_step, 3)
            nc.gpsimd.tensor_copy(ident_b[:], ident[:]).then_inc(consts, 1)

            ctx_pairs = ctx_in_dram.rearrange("b (i t p) n -> (b i) p t n", p=P, t=2)
            pool.wait_ge(x_in[B - 1], 16)
            bank, n = first.use(f"w_{TILES[-1]}")
            pool.wait_ge(filled[bank], n + 1)
            for i in range(B * KC // 2):
                if i >= 4:
                    pool.wait_ge(ctx_read, i - 3)
                pool.dma_start(ctx_all[:, i % 4, :, :], ctx_pairs[i]).then_inc(ctx_all_in[i % 4], 16)
            pool.wait_ge(ctx_amax, 1)
            nc.gpsimd.partition_all_reduce(amax[:, 1:2], amax[:, 0:1], P, RMAX).then_inc(ctx_amax_all, 1)

            zero_row = zeros[:, :].rearrange("p (a n) -> p a n", a=1).to_broadcast([P, D // P, P])

            def ctx_tile_out(i):
                pool.wait_ge(ctxq_done, i + 1)
                pool.dma_start(ctxq_dram[bass.ds(i * P, P), :], ctx_q[:, :]).then_inc(ctxq_out, 16)
                pool.dma_start(sent[bass.ds(i * P, P), :].rearrange("p (a n) -> p a n", a=D // P), zero_row)\
                    .then_inc(sent_zeroed, 16)
                pool.wait_ge(ctxq_out, (i + 1) * 16)

            pool.wait_ge(zeros_set, 1)
            pool.dma_start(sent_meta.rearrange("(p s) c -> p (s c)", p=P), zeros[:, 0:2 * NT]).then_inc(meta_zeroed, 16)
            pool.dma_start(ctx_stage[:, :], ctx_rows[0:P, :]).then_inc(ctx_in, 16)
            with pool.Fori(0, UNITS - 1) as i:
                ctx_tile_out(i)
                pool.dma_start(ctx_stage[:, :], ctx_rows[bass.ds((i + 1) * P, P), :]).then_inc(ctx_in, 16)
            ctx_tile_out(UNITS - 1)
            for c in range(NS):
                pool.wait_ge(w13_high, c + 1)
                nc.gpsimd.tensor_tensor(w13_chunk(w13l, c), w13_chunk(w13st, c), w13_chunk(w13h, c).bitcast(F32),
                                        ALU.subtract).then_inc(w13_low, 1)
            pool.wait_ge(x_amax, 1)
            nc.gpsimd.partition_all_reduce(amax[:, 3:4], amax[:, 2:3], P, RMAX).then_inc(x_amax_all, 1)

            nc.gpsimd.memset(ones_b[:], 1.0).then_inc(route_consts, 1)
            nc.gpsimd.memset(tri[:], 1.0).then_inc(pool_step, 1)
            nc.gpsimd.memset(carry[:], 0.0).then_inc(route_consts, 1)
            nc.gpsimd.memset(lgT[:], 0.0).then_inc(route_consts, 1)
            nc.gpsimd.iota(expert_id[:], [[1, NE]], base=0, channel_multiplier=0,
                           allow_small_or_imprecise_dtypes=True).then_inc(route_consts, 1)
            nc.gpsimd.iota(token_code[:], [[-P, TB]], base=NOBODY, channel_multiplier=-1,
                           allow_small_or_imprecise_dtypes=True).then_inc(route_consts, 1)
            pool.wait_ge(pool_step, 4)
            nc.gpsimd.affine_select(out=tri[:], in_=tri[:], compare_op=ALU.is_ge, fill=0.0, base=0,
                                    pattern=[[1, P]], channel_multiplier=-1).then_inc(route_consts, 1)

            pool.wait_ge(sent_zeroed, 16 * UNITS)
            pool.wait_ge(meta_zeroed, 16)
            last_row = pool.to_reg(NE * CAP - 1)
            for b in range(B):
                pool.wait_ge(slots_done, b + 1)
                for t in range(TB):
                    place = bass.IndirectOffsetOnAxis(ap=slot_w[:, t:t + 1], axis=0)
                    pool.indirect_dma_start(out=sent[:, :], out_offset=place, in_=x3n[:, t, :], in_offset=None,
                                            bounds_check=last_row, oob_is_err=False).then_inc(tokens_sent, 16)
                    pool.indirect_dma_start(out=sent_meta[:, :], out_offset=place, in_=meta[:, t, :],
                                            in_offset=None, bounds_check=last_row,
                                            oob_is_err=False).then_inc(meta_sent, 16)

            pool.wait_ge(rows_known, 1)
            pool.wait_ge(x_stored, 2 * B * 16)
            last_token = pool.to_reg(B * T - 1)
            for e in range(NE):
                for m in range(CAP_T):
                    s = e * CAP_T + m
                    pool.indirect_dma_start(out=slot_x[:, m, :], out_offset=None, in_=x_shared[:, :],
                                            in_offset=bass.IndirectOffsetOnAxis(ap=row_from[:, s:s + 1], axis=0),
                                            bounds_check=last_token, oob_is_err=False).then_inc(slot_x_in[m], 16)
                for m in range(CAP_T):
                    s = e * CAP_T + m
                    bank, n = expert_banks(e, True).use(f"D{m}")
                    pool.wait_ge(mfree[bank], n + 1)
                    pool.indirect_dma_start(out=out_rows[:, :], in_=expert_out[:, m, :], in_offset=None,
                                            out_offset=bass.IndirectOffsetOnAxis(ap=row_to[:, s:s + 1], axis=0),
                                            bounds_check=last_token, oob_is_err=False).then_inc(answers_out[m], 16)
            for m in range(CAP_T):
                pool.wait_ge(answers_out[m], NE * 16)

        @block.tensor
        def _(pe):
            mm = nc.tensor.matmul

            def begin(bk, name):
                bank, n = bk.use(name)
                pe.wait_ge(bk.freed[bank], n)
                return psum[bank]

            def end(bk, name, instruction):
                instruction.then_inc(bk.filled[bk.use(name)[0]], 1)

            def landed(bk, name):
                bank, n = bk.use(name)
                pe.wait_ge(bk.freed[bank], n + 1)

            def product(dst, pairs, n=None):
                last = None
                total = 3 * len(pairs)
                i = 0
                for (lh, ll), (rh, rl) in pairs:
                    for a, b_ in ((lh, rh), (ll, rh), (lh, rl)):
                        last = mm(dst, a, b_, start=(i == 0), stop=(i == total - 1))
                        i += 1
                return last

            def weight_tile(bk, g, t, own_place=False):
                i = TILES.index(t)
                if own_place:
                    pe.wait_ge(first_w_in[i // 2], 32)
                    src = first_w[:, i, :]
                else:
                    place, src = w_place(i)
                    n_before = (g - 1) * (IN_RING // RING) + i // RING if i < IN_RING else g
                    pe.wait_ge(w_in[place], (n_before + 1) * 16)
                ps = begin(bk, f"w_{t}")
                for k in range(4):
                    last = nc.tensor.transpose(ps[:, k * P:(k + 1) * P], src[:, k * P:(k + 1) * P], ident[:])
                end(bk, f"w_{t}", last)

            def project(bk, name, tile, b, prep=False):
                if prep:
                    landed(bk, f"w_{tile}")
                ps = begin(bk, name)
                w = TILES.index(tile)
                last = product(ps[:, :], [
                    ((wTh[:, w, k * P:(k + 1) * P], wTl[:, w, k * P:(k + 1) * P]),
                     (xTh[:, k, bass.ds(b * T, T)], xTl[:, k, bass.ds(b * T, T)])) for k in range(KC)])
                end(bk, name, last)

            def scores(u, h, first_ever=False):
                for j in range(TB):
                    if not first_ever:
                        pe.wait_ge(exp_done, 16 * u + 4 * h + j - 3)
                    n = (j + 1) * P
                    qj = slice(j * P, n)
                    mm(psum[j][:, 0:n], qTh[:, h, qj], kTh[:, 0:n], start=True, stop=False)
                    mm(psum[j][:, j * P:n], ident_b[:], causal[:], start=False, stop=False,
                       skip_group_check=True)
                    mm(psum[j][:, 0:n], qTl[:, h, qj], kTh[:, 0:n], start=False, stop=False)
                    mm(psum[j][:, 0:n], qTh[:, h, qj], kTl[:, 0:n], start=False,
                       stop=True).then_inc(s_filled, 1)

            def sums_of_squares(bk, h, sq_n, with_k):
                pe.wait_ge(sq_done, sq_n)
                if with_k:
                    landed(bk, "K")
                ps = begin(bk, f"SS{h}")
                for c in range(8 if with_k else 4):
                    src = qsq if c < 4 else ksq
                    last = mm(ps[:, c:c + 1], src[:, (c % 4) * P:(c % 4 + 1) * P], ones[:, 0:1],
                              start=True, stop=True)
                end(bk, f"SS{h}", last)

            def value_blocks(bk):
                ps = begin(bk, "VT")
                for s in range(TB):
                    last = nc.tensor.transpose(ps[:, s * P:(s + 1) * P], vraw[:, s * P:(s + 1) * P], ident[:])
                end(bk, "VT", last)

            def key_scale_rows(bk):
                ps = begin(bk, "RK")
                for s in range(TB):
                    last = nc.tensor.transpose(ps[:, s * P:(s + 1) * P],
                                               sc[:, 16 + s:17 + s].to_broadcast([P, P]), ident[:])
                end(bk, "RK", last)

            pe.wait_ge(consts, 3)
            def token_tile(b, t):
                n = b * TB + t
                pe.wait_ge(xn_done, n + 1)
                ps = begin(first, f"x{b}{t}")
                for k in range(KC):
                    last = nc.tensor.transpose(ps[:, k * P:(k + 1) * P], xn[:, n % 2, k * P:(k + 1) * P], ident[:])
                end(first, f"x{b}{t}", last)

            for i, t in enumerate(TILES):
                if i == EARLY_TILES:
                    for n in range(TB):
                        token_tile(0, n)
                weight_tile(first, 0, t, own_place=(i < FIRST_STAGE))
            for t in range(TB):
                landed(first, f"x0{t}")
            for t in QKV_TILES:
                landed(first, f"w_{t}")
            project(first, "V", "v", 0)
            project(first, "K", "k", 0)
            for h in range(REP):
                project(first, f"Q{h}", f"q{h}", 0)
                if h:
                    sums_of_squares(first, h - 1, h, False)
            sums_of_squares(first, REP - 1, REP, True)
            value_blocks(first)
            for t in range(TB):
                token_tile(1, t)
            pe.wait_ge(norms_done, 1)
            key_scale_rows(first)
            landed(first, "VT")
            pe.wait_ge(k_ready, 1)
            scores(0, 0, True)
            for b in range(2, B):
                for t in range(TB):
                    token_tile(b, t)
            for t in range(TB):
                landed(first, f"x{B - 1}{t}")

            def unit(u, g, b, b_next, prep, final):
                bk = banks(u, g, prep, final)
                if prep:
                    for t, _ in PREP_START:
                        weight_tile(bk, g + 1, t)
                for h in range(REP):
                    if prep and h == 0:
                        scores(u, 1)
                    if h == 0 and not final:
                        project(bk, "Q0", "q0", b_next, prep)
                    if h < REP - 1 and not (prep and h == 0):
                        scores(u, h + 1)
                    pe.wait_ge(norm_done, 4 * u + h + 1)
                    for c in "ABC":
                        start, _, keys = CHUNKS[c]
                        ps = begin(bk, f"{c}{h}")
                        for s in keys:
                            for t in range(s, TB):
                                col = PT_OFF[s] - start + (t - s) * P
                                src = P_OFF[t] + s * P
                                last = nc.tensor.transpose(ps[:, col:col + P], probs[:, src:src + P], ident[:])
                        end(bk, f"{c}{h}", last)
                    if not final:
                        if h:
                            project(bk, f"Q{h}", f"q{h}", b_next, prep)
                        if h == 0:
                            project(bk, "V", "v", b_next, prep)
                        if h == 2:
                            project(bk, "K", "k", b_next, prep)
                    if prep:
                        for t, _ in PREP_IN_SLOT[h]:
                            weight_tile(bk, g + 1, t)
                    ps = begin(bk, f"PV{h}")
                    steps = 0
                    for s, c in ((0, "A"), (1, "B"), (3, "B"), (2, "C")):
                        landed(bk, f"{c}{h}")
                        n = (TB - s) * P
                        cols = slice(PT_OFF[s], PT_OFF[s] + n)
                        for a, p_ in ((vh, pTh), (vl, pTh), (vh, pTl)):
                            last = mm(ps[:, s * P:T], a[:, s, :], p_[:, cols], start=(steps == 0),
                                      stop=(steps == 11), skip_group_check=True)
                            steps += 1
                    end(bk, f"PV{h}", last)
                    if not final:
                        sums_of_squares(bk, h, REP * (u + 1) + h + 1, h == REP - 1)
                if not final:
                    value_blocks(bk)
                for m in range(TB):
                    if m == 2 and not final:
                        pe.wait_ge(norms_done, u + 2)
                        key_scale_rows(bk)
                    if m == 3 and not final:
                        landed(bk, "VT")
                        pe.wait_ge(k_ready, u + 2)
                        scores(u + 1, 0)
                    ps = begin(bk, f"O{m}")
                    if m == 0:
                        landed(bk, f"PV{REP - 1}")
                    last = product(ps[:, :], [
                        ((oTh[:, h, m * P:(m + 1) * P], oTl[:, h, m * P:(m + 1) * P]),
                         (woTh[:, h, :], woTl[:, h, :])) for h in range(REP)])
                    end(bk, f"O{m}", last)
                if prep:
                    for t in O_TILES:
                        weight_tile(bk, g + 1, t)

            units(pe, unit)

            def token_quantised_blocks(bk, t, n):
                pe.wait_ge(quantised, n + 1)
                ps = begin(bk, f"QT{t}").bitcast(BF16)
                for k in range(KC):
                    last = nc.tensor.transpose(ps[:, k * P:(k + 1) * P], tokens_q[:, t % 2, k * P:(k + 1) * P],
                                               ident_b[:])
                end(bk, f"QT{t}", last)

            def cross_attention(bk, t, b):
                landed(bk, f"QT{t}")
                pe.wait_ge(ctxq_in, 16 * (b + 1))
                ps = begin(bk, f"XA{t}")
                for k in range(KC):
                    last = mm(ps[:, :], tokens_qT[:, t % 2, k, :], ctxq[:, k, :], start=(k == 0), stop=(k == KC - 1))
                end(bk, f"XA{t}", last)

            def token_blocks(bk, t):
                ps = begin(bk, f"XT{t}")
                for k in range(KC):
                    last = nc.tensor.transpose(ps[:, k * P:(k + 1) * P], x3n[:, t, k * P:(k + 1) * P], ident[:])
                end(bk, f"XT{t}", last)

            def router(bk):
                ps = begin(bk, "RT")
                end(bk, "RT", product(ps[0:NE, :], [
                    ((wgh[:, k, :], wgl[:, k, :]), (xh[:, k, :], xl[:, k, :])) for k in range(KC)]))

            def logit_blocks(bk):
                landed(bk, "RT")
                ps = begin(bk, "LT")
                for t in range(TB):
                    last = nc.tensor.transpose(ps[:, t * P:(t + 1) * P], lgT[:, t * P:(t + 1) * P], ident[:])
                end(bk, "LT", last)

            def count_tokens(bk, b):
                pe.wait_ge(onehot_done, b + 1)
                ps = begin(bk, "CS")
                oh = onehot[:, :, :].rearrange("p t e -> p (t e)")
                n = TB * NE
                mm(ps[:, 0:n], tri[:], oh[:, 0:n], start=True, stop=False, skip_group_check=True)
                for s in range(1, TB):
                    mm(ps[:, s * NE:n], ones_b[:], oh[:, 0:n - s * NE], start=False, stop=False,
                       skip_group_check=True)
                for t in range(TB):
                    last = mm(ps[:, n:n + NE], ones_b[:], oh[:, t * NE:(t + 1) * NE], start=False,
                              stop=(t == TB - 1), skip_group_check=True)
                end(bk, "CS", last)

            def hidden_products(bk, n_tok, n_set, between):
                def part(name, c, cols):
                    ps = begin(bk, name)
                    pe.wait_ge(w13_low, n_set * NS + c + 1)
                    high, low = w13_chunk(w13h, c), w13_chunk(w13l, c)
                    steps = 0
                    for k in range(KC):
                        for w, x_ in ((high, xh), (low, xh), (high, xl)):
                            last = mm(ps[:, 0:n_tok], w[:, k, cols], x_[:, k, 0:n_tok],
                                      start=(steps == 0), stop=(steps == 3 * KC - 1))
                            steps += 1
                    end(bk, name, last)

                for c in range(HC):
                    part(f"a{c}", c, slice(0, P))
                    part(f"b{c}", c, slice(P, 2 * P))
                    between(c)
                part("ab", HC, slice(0, P))

            def down(bk, ms, n_set, n_body, first=False):
                for m in ms:
                    ps = begin(bk, f"D{m}")
                    rows = slice(m * P, (m + 1) * P)
                    for c in range(HC):
                        if first and m == ms[0]:
                            pe.wait_ge(w2_low, n_set * NS + c + 1)
                            pe.wait_ge(hl_done, n_body * NS + c + 1)
                        for i, (a, w) in enumerate(((hh, w2h), (hl, w2h), (hh, w2l))):
                            mm(ps[:, :], a[:, c, rows], w[:, c, :], start=(c + i == 0), stop=False,
                               skip_group_check=True)
                if first:
                    pe.wait_ge(w2_low, (n_set + 1) * NS)
                    pe.wait_ge(hl_done, n_body * NS + NS)
                for m in ms:
                    ps = psum[bk.use(f"D{m}")[0]]
                    rows = slice(m * P, (m + 1) * P)
                    mm(ps[:, :], hh[:, HC, rows], w2h[:, HC, :], start=False, stop=False, skip_group_check=True)
                    end(bk, f"D{m}", mm(ps[:, :], hh[:, HC, rows], w2l[:, HC, :], start=False, stop=True,
                                        skip_group_check=True))

            for t in range(TB):
                token_quantised_blocks(before, t, t)
                cross_attention(before, t, 0)
            for t in range(TB):
                pe.wait_ge(x3n_done, t + 1)
                token_blocks(before, t)
            for t in range(TB):
                landed(before, f"XT{t}")
            pe.wait_ge(wg_low, 1)
            pe.wait_ge(route_consts, 6)

            def shared(b, ahead, next_two):
                bk = shared_banks(b, ahead)

                def between(c):
                    if c == 0:
                        router(bk)
                    if c == 1:
                        logit_blocks(bk)
                    if c == 3:
                        count_tokens(bk, b)
                    if ahead:
                        if c < TB:
                            token_quantised_blocks(bk, c, (b + 1) * TB + c)
                        if c:
                            cross_attention(bk, c - 1, b + 1)

                hidden_products(bk, T, 0, between)
                down(bk, (0, 1), 0, b, True)
                down(bk, (2,), 0, b)
                if not ahead:
                    pe.wait_ge(expert_in, 16)
                for t in range(TB if ahead else CAP_T):
                    if ahead:
                        pe.wait_ge(x3n_done, (b + 1) * TB + t + 1)
                    token_blocks(bk, t)
                down(bk, (3,), 0, b)
                for t in range(TB if ahead else CAP_T):
                    landed(bk, f"XT{t}")

            with pe.Fori(0, B - 2) as b:
                shared(b, True, True)
            shared(B - 2, True, False)
            shared(B - 1, False, False)

            def expert(e, ahead):
                bk = expert_banks(e, ahead)
                hidden_products(bk, CAP, e + 1, lambda c: None)
                if ahead:
                    pe.wait_ge(expert_in, 16 * (e + 2))
                    for t in range(CAP_T):
                        token_blocks(bk, t)
                down(bk, range(CAP_T), e + 1, B + e, True)
                if ahead:
                    for t in range(CAP_T):
                        landed(bk, f"XT{t}")

            with pe.Fori(0, NE - 1) as e:
                expert(e, True)
            expert(NE - 1, False)

        @block.scalar
        def _(act):
            A = nc.scalar.activation

            def full(bk, name):
                bank, n = bk.use(name)
                act.wait_ge(bk.filled[bank], n + 1)
                return psum[bank]

            def high(dst, src):
                A(dst, src, ACT.Copy).then_inc(hi_done, 1)

            def weight_tile(bk, t):
                full(bk, f"w_{t}")
                high(w_dst(t, True), blocks(bk.use(f"w_{t}")[0]))

            def query_head(bk, h, ready_ss):
                ps = full(bk, f"Q{h}")
                high(qTh[:, h, :], ps[:, :])
                ready_ss()
                A(qsq[:], ps[:, :], ACT.Square).then_inc(sq_done, 1)

            def keep(bk, name, dst, sq=None):
                ps = full(bk, name)
                bank = bk.use(name)[0]
                last = A(dst[:], ps[:, :], ACT.Copy)
                if sq is not None:
                    last = A(sq[:], ps[:, :], ACT.Square)
                last.then_inc(bk.freed[bank], 1)

            def normed_keys_high(bk):
                bank, n = bk.use("RK")
                act.wait_ge(bk.freed[bank], n + 1)
                high(kTh[:], kraw[:])

            def w13_high_part(c, n):
                act.wait_ge(w13_in[c], 32 * (n + 1))
                A(w13_chunk(w13h, c), w13_chunk(w13st, c), ACT.Copy).then_inc(w13_high, 1)

            def softmax_exp(u, h):
                for j in range(TB):
                    c = 4 * h + j
                    if j % 2 == 0:
                        act.wait_ge(bias_done, 8 * u + 2 * h + j // 2 + 1)
                    A(probs[:, P_OFF[j]:P_OFF[j + 1]], psum[j][:, 0:(j + 1) * P], ACT.Exp,
                      bias=nbias[:, c:c + 1], scale=sc[:, c:c + 1],
                      accum_out=rowsum[:, c:c + 1]).then_inc(exp_done, 1)

            def normalise(b, t):
                i = b * TB + t
                act.wait_ge(mean_done, b + 1)
                if i >= 2:
                    full(first, f"x{(i - 2) // TB}{(i - 2) % TB}")
                A(xn[:, i % 2, :], xres[:, i, :], ACT.Identity, bias=shift[:, i:i + 1],
                  scale=rstd[:, i:i + 1]).then_inc(xn_done, 1)

            def ctx_magnitudes(i):
                act.wait_ge(ctx_all_in[i % 4], 16 * (i // 4 + 1))
                A(ctx_all[:, i % 4, :, :], ctx_all[:, i % 4, :, :], ACT.Abs).then_inc(ctx_abs, 1)

            for name, bank in FIRST:
                if name[0] == "w":
                    weight_tile(first, name[2:])
                elif name[0] == "x":
                    b, t = int(name[1]), int(name[2])
                    if t == 0:
                        if b == 2:
                            softmax_exp(0, 0)
                        normalise(b, 0)
                    if t + 1 < TB:
                        normalise(b, t + 1)
                    full(first, name)
                    high(xTh[:, :, (b * TB + t) * P:(b * TB + t + 1) * P], blocks(bank))
                    if b == 3:
                        ctx_magnitudes(4 + t)
                elif name == "V":
                    keep(first, "V", vraw)
                elif name == "K":
                    keep(first, "K", kraw, ksq)
                elif name[0] == "Q":
                    h = int(name[1])
                    query_head(first, h, lambda: full(first, f"SS{h - 1}") if h else None)
                    ctx_magnitudes(h)
                elif name == "VT":
                    full(first, "VT")
                    high(vh[:, :, :], blocks(bank))
                elif name == "RK":
                    normed_keys_high(first)
            act.wait_ge(ctx_read, B * KC // 2)

            def unit(u, g, b, b_next, prep, final):
                bk = banks(u, g, prep, final)
                if prep:
                    for t, _ in PREP_START:
                        weight_tile(bk, t)
                for h in range(REP):
                    if h == 0 and not final:
                        query_head(bk, 0, lambda: None)
                    for c in "ABC":
                        start, n, _ = CHUNKS[c]
                        ps = full(bk, f"{c}{h}")
                        high(pTh[:, start:start + n], ps[:, 0:n])
                    if h < REP - 1:
                        softmax_exp(u, h + 1)
                    if not final:
                        if h:
                            query_head(bk, h, lambda: full(bk, f"SS{h - 1}"))
                        if h == 0:
                            keep(bk, "V", vraw)
                        if h == 2:
                            act.wait_ge(ctxq_out, (u + 1) * 16)
                            keep(bk, "K", kraw, ksq)
                    if prep:
                        for t, _ in PREP_IN_SLOT[h]:
                            weight_tile(bk, t)
                    ps = full(bk, f"PV{h}")
                    high(oTh[:, h, :], ps[:, :])
                    if final:
                        for c in SPLIT_IN_SLOT[h]:
                            w13_high_part(c, 0)
                if not final:
                    full(bk, "VT")
                    high(vh[:, :, :], blocks(bk.use("VT")[0]))
                    normed_keys_high(bk)
                    softmax_exp(u + 1, 0)
                if prep:
                    for t in O_TILES:
                        weight_tile(bk, t)

            units(act, unit)

            def w2_high_part(c, n):
                act.wait_ge(w2_in[c % 2], 32 * (n * (NS // 2) + c // 2 + 1))
                A(w2h[:, c, :], w2st[:, c % 2, :], ACT.Copy).then_inc(w2_high, 1)

            def normalise_tokens(tile, t, n_before):
                act.wait_ge(shifts_done, 1)
                if n_before is not None:
                    act.wait_ge(quantised, n_before)
                A(q_y[:, t % 2, :], xres[:, bass.ds(tile, 1), :].rearrange("p a d -> p (a d)"), ACT.Identity,
                  bias=shift[:, bass.ds(tile, 1)], scale=rstd[:, bass.ds(tile, 1)]).then_inc(y_done, 1)

            def logits_out(bk):
                ps = full(bk, "RT")
                A(lgT[0:NE, :], ps[0:NE, :], ACT.Copy).then_inc(bk.freed[bk.use("RT")[0]], 1)

            def quantised_blocks(bk, t):
                ps = full(bk, f"QT{t}").bitcast(BF16)
                A(tokens_qT[:, t % 2, :, :], ps[:, 0:D].rearrange("p (k n) -> p k n", k=KC), ACT.Copy)\
                    .then_inc(bk.freed[bk.use(f"QT{t}")[0]], 1)

            def tokens_high(bk, t):
                full(bk, f"XT{t}")
                A(xh[:, :, t * P:(t + 1) * P], blocks(bk.use(f"XT{t}")[0]), ACT.Copy).then_inc(xh_done, 1)

            def router_exp(b):
                act.wait_ge(logits_less_max, b + 1)
                A(le[:, :, :], lt[:, :, :], ACT.Exp).then_inc(logits_exp, 1)

            def hidden_act(bk, c, n_tok):
                name, rows = (f"a{c}", P) if c < HC else ("ab", HT)
                ps = full(bk, name)
                last = A(gate_act[0:rows, c % 2, 0:n_tok], ps[0:rows, 0:n_tok], ACT.Silu)
                last.then_inc(bk.freed[bk.use(name)[0]] if c < HC else act_done, 1)

            def hidden_high(bk, c, n_tok):
                rows = P if c < HC else HT
                bank, n = bk.use(f"b{c}" if c < HC else "ab")
                act.wait_ge(bk.freed[bank], n + 1)
                A(hh[0:rows, c, 0:n_tok], hid[0:rows, c % 2, 0:n_tok], ACT.Copy).then_inc(hh_done, 1)

            act.wait_ge(attn_done, 1)
            act.wait_ge(route_consts, 6)
            for c in range(2):
                w2_high_part(c, 0)
            for t in range(2):
                normalise_tokens(t, t, None)
            for t in range(TB):
                quantised_blocks(before, t)
                if t + 2 < TB:
                    normalise_tokens(t + 2, t + 2, t + 1)
            act.wait_ge(wg_in, 16)
            A(wgh[:, :, :], wg[:, :, :], ACT.Copy).then_inc(wg_high, 1)
            for t in range(TB):
                tokens_high(before, t)
            for c in range(2, NS):
                w2_high_part(c, 0)
            for t in range(2):
                normalise_tokens(TB + t, t, TB + t - 1)

            def shared(b, ahead, next_two):
                bk = shared_banks(b, ahead)
                n_x = (b + 1) * TB
                for c in range(NS):
                    hidden_act(bk, c, T)
                    if ahead and c < TB:
                        quantised_blocks(bk, c)
                    hidden_high(bk, c, T)
                    if ahead and c + 2 < TB:
                        normalise_tokens(n_x + c + 2, c + 2, n_x + c + 1)
                    if c == 0:
                        logits_out(bk)
                    if c == 2:
                        router_exp(b)
                    if not ahead and c:
                        w13_high_part(c - 1, 1)
                if ahead:
                    for t in range(TB):
                        tokens_high(bk, t)
                    if next_two:
                        for t in range(2):
                            normalise_tokens(n_x + TB + t, t, n_x + TB + t - 1)
                else:
                    w13_high_part(HC, 1)
                    for t in range(CAP_T):
                        tokens_high(bk, t)

            with act.Fori(0, B - 2) as b:
                shared(b, True, True)
            shared(B - 2, True, False)
            shared(B - 1, False, False)

            def expert(e, ahead):
                bk = expert_banks(e, ahead)
                for c in range(NS):
                    hidden_act(bk, c, CAP)
                    w2_high_part(c, e + 1)
                    hidden_high(bk, c, CAP)
                    if ahead and c:
                        w13_high_part(c - 1, e + 2)
                if ahead:
                    w13_high_part(HC, e + 2)
                    for t in range(CAP_T):
                        tokens_high(bk, t)

            with act.Fori(0, NE - 1) as e:
                expert(e, True)
            expert(NE - 1, False)

        @block.vector
        def _(dve):
            V = nc.vector

            def full(bk, name):
                bank, n = bk.use(name)
                dve.wait_ge(bk.filled[bank], n + 1)
                return psum[bank]

            def low(bk, name, dst, src, hi_src, hi_count):
                dve.wait_ge(hi_done, hi_count)
                V.tensor_tensor(dst, src, hi_src.bitcast(F32), ALU.subtract)\
                    .then_inc(bk.freed[bk.use(name)[0]], 1)

            def weight_low(bk, t, n):
                bank = bk.use(f"w_{t}")[0]
                low(bk, f"w_{t}", w_dst(t, False), blocks(bank), w_dst(t, True), n)

            def flat(ap):
                return ap.rearrange("p a d -> p (a d)")

            def inverse_root(y, n, src, scale, eps):
                v, t = chain_v[:, 0:n], chain_t[:, 0:n]
                V.tensor_scalar(v, src, scale, eps, ALU.mult, ALU.add)
                dve.drain()
                V.tensor_scalar(y.bitcast(I32), v.bitcast(I32), 1, None, ALU.logical_shift_right)
                dve.drain()
                V.tensor_scalar(y.bitcast(I32), y.bitcast(I32), -1.0, float(0x5F3759DF), ALU.mult, ALU.add)
                for _ in range(3):
                    dve.drain()
                    V.tensor_tensor(t, v, y, ALU.mult)
                    dve.drain()
                    V.tensor_tensor(t, t, y, ALU.mult)
                    dve.drain()
                    V.tensor_scalar(t, t, -0.5, 1.5, ALU.mult, ALU.add)
                    dve.drain()
                    last = V.tensor_tensor(y, y, t, ALU.mult)
                dve.drain()
                return last

            def tile_stats(tile, t, stats=stats):
                V.bn_stats(stats[:, t, :], flat(xres[:, bass.ds(tile, 1), :]))

            def means(t0, n=TB, stats=stats, mv=mv):
                dve.drain()
                for t in range(n):
                    V.bn_aggr(mv[:, t, :], stats[:, t, :])
                dve.drain()
                V.tensor_copy(mean[:, bass.ds(t0, n)], flat(mv[:, 0:n, 0:1]))
                V.tensor_copy(rstd[:, bass.ds(t0, n)], flat(mv[:, 0:n, 1:2]))

            def deviations(t0, n=TB):
                dve.drain()
                rows = rstd[:, bass.ds(t0, n)]
                inverse_root(rows, n, rows, 1.0, LN_EPS)

            def finish_norm(t0, n=TB, stats=stats, mv=mv):
                means(t0, n, stats, mv)
                deviations(t0, n)

            def query_low(bk, h, n, n_sq):
                dve.wait_ge(sq_done, n_sq)
                low(bk, f"Q{h}", qTl[:, h, :], psum[bk.use(f"Q{h}")[0]][:, :], qTh[:, h, :], n)

            def take_sums(bk, h):
                ps = full(bk, f"SS{h}")
                V.tensor_copy(ss[:, 4 * h:4 * h + (8 if h == REP - 1 else 4)],
                              ps[:, 0:8 if h == REP - 1 else 4]).then_inc(bk.freed[bk.use(f"SS{h}")[0]], 1)

            def key_norms():
                dve.drain()
                inverse_root(sc[:, :], 20, ss[:, :], 1.0 / HD, QK_EPS)
                V.tensor_scalar(sc[:, 0:16], sc[:, 0:16], SCALE, None, ALU.mult).then_inc(norms_done, 1)

            def normed_keys(bk):
                ps = full(bk, "RK")
                V.scalar_tensor_tensor(out=kraw[:], in0=kraw[:], scalar=qk_scale[:, 0:1], in1=ps[:, :],
                                       op0=ALU.mult, op1=ALU.mult).then_inc(bk.freed[bk.use("RK")[0]], 1)

            def keys_low(bk, n):
                dve.wait_ge(hi_done, n)
                V.tensor_tensor(kTl[:], kraw[:], kTh[:].bitcast(F32), ALU.subtract).then_inc(k_ready, 1)

            def softmax_max(u, h):
                for j in range(TB):
                    c = 4 * h + j
                    dve.wait_ge(s_filled, 16 * u + c + 1)
                    V.tensor_reduce(mx[:, c:c + 1], psum[j][:, 0:(j + 1) * P], AX.X, ALU.max)
                    if j % 2:
                        dve.drain()
                        V.scalar_tensor_tensor(out=nbias[:, c - 1:c + 1], in0=mx[:, c - 1:c + 1], scalar=-1.0,
                                               in1=sc[:, c - 1:c + 1], op0=ALU.mult, op1=ALU.mult)\
                            .then_inc(bias_done, 1)

            def softmax_norm(u, h):
                dve.wait_ge(exp_done, 16 * u + 4 * h + 4)
                V.reciprocal(rinv[:, 0:4], rowsum[:, 4 * h:4 * h + 4])
                dve.drain()
                for j in range(TB):
                    cols = slice(P_OFF[j], P_OFF[j + 1])
                    last = V.tensor_scalar(probs[:, cols], probs[:, cols], rinv[:, j:j + 1], None, ALU.mult)
                last.then_inc(norm_done, 1)

            dve.wait_ge(scales_in, 32)
            V.tensor_tensor(qk_scale[:], qs_col[:, 0:1], qs_col[:, 1:2], ALU.mult)

            def x_low(b, t):
                cols = slice((b * TB + t) * P, (b * TB + t + 1) * P)
                name = f"x{b}{t}"
                low(first, name, xTl[:, :, cols], blocks(first.use(name)[0]), xTh[:, :, cols],
                    HI_FIRST[name] + 1)

            def shift_of(t0, n, done=None):
                V.scalar_tensor_tensor(out=shift[:, t0:t0 + n], in0=mean[:, t0:t0 + n], scalar=-1.0,
                                       in1=rstd[:, t0:t0 + n], op0=ALU.mult, op1=ALU.mult)\
                    .then_inc(done or mean_done, 1 if done else n // TB)

            dve.wait_ge(x_in[0], 16)
            for t in range(TB):
                tile_stats(t, t)
            finish_norm(0)
            shift_of(0, TB)
            for i, t in enumerate(TILES):
                if i == EARLY_TILES:
                    for n in range(TB):
                        x_low(0, n)
                weight_low(first, t, HI_FIRST[f"w_{t}"] + 1)
            for h in range(REP):
                query_low(first, h, HI_FIRST[f"Q{h}"] + 1, h + 1)
                if h:
                    take_sums(first, h - 1)
                if h < B - 1:
                    dve.wait_ge(x_in[h + 1], 16)
                    for t in range(TB):
                        tile_stats((h + 1) * TB + t, h * TB + t, first_stats)
            finish_norm(TB, NT - TB, first_stats, first_mv)
            shift_of(TB, NT - TB)
            take_sums(first, REP - 1)
            key_norms()
            low(first, "VT", vl[:, :, :], blocks(first.use("VT")[0]), vh[:, :, :], HI_FIRST["VT"] + 1)
            for t in range(TB):
                x_low(1, t)
            normed_keys(first)
            keys_low(first, HI_FIRST["RK"] + 1)
            softmax_max(0, 0)
            softmax_norm(0, 0)

            for i in range(2 * TB):
                x_low(2 + i // TB, i % TB)
                dve.wait_ge(ctx_abs, i + 1)
                V.tensor_reduce(ctx_part[:, i:i + 1], ctx_all[:, i % 4, :, :].rearrange("p k n -> p (k n)"),
                                AX.X, ALU.max).then_inc(ctx_read, 1)
            dve.drain()
            V.tensor_reduce(amax[:, 0:1], ctx_part[:, 0:B * KC // 2], AX.X, ALU.max).then_inc(ctx_amax, 1)

            def largest_magnitude(most, least, dst):
                dve.drain()
                V.tensor_reduce(extremes[:, 0:1], most, AX.X, ALU.max)
                V.tensor_reduce(extremes[:, 1:2], least, AX.X, ALU.min)
                dve.drain()
                return V.scalar_tensor_tensor(out=dst, in0=extremes[:, 1:2], scalar=-1.0, in1=extremes[:, 0:1],
                                              op0=ALU.mult, op1=ALU.max)

            def scale_from(src, dst):
                V.tensor_scalar(dst, src, FP8_EPS, None, ALU.max)
                dve.drain()
                V.reciprocal(dst, dst)
                dve.drain()
                V.tensor_scalar(dst, dst, FP8_MAX, None, ALU.mult)
                dve.drain()

            dve.wait_ge(ctx_amax_all, 1)
            scale_from(amax[:, 1:2], f8scale[:, 0:1])

            def to_fp8(y, m, scale, dst):
                V.tensor_scalar(y, y, scale, FP8_MAX, ALU.mult, ALU.min)
                dve.drain()
                V.tensor_scalar(m.bitcast(I32), y.bitcast(I32), EXPONENT, None, ALU.bitwise_and)
                dve.drain()
                V.tensor_scalar(m, m, FP8_LEAST, ROUND_AT, ALU.max, ALU.mult)
                dve.drain()
                V.scalar_tensor_tensor(out=y, in0=y, scalar=-FP8_MAX, in1=m, op0=ALU.max, op1=ALU.add)
                dve.drain()
                return V.tensor_tensor(dst, y, m, ALU.subtract)

            def quantise_ctx(u, half):
                if half == 0:
                    dve.wait_ge(ctx_in, (u + 1) * 16)
                cols = slice(half * D // 2, (half + 1) * D // 2)
                last = to_fp8(ctx_stage[:, cols], ctx_m[:], f8scale[:, 0:1], ctx_q[:, cols])
                if half == 1:
                    last.then_inc(ctxq_done, 1)

            def row_extremes(t):
                row = xres[:, bass.ds(t, 1), :].rearrange("p a d -> p (a d)")
                V.tensor_reduce(rowmax[:, bass.ds(t, 1)], row, AX.X, ALU.max)
                V.tensor_reduce(rowmin[:, bass.ds(t, 1)], row, AX.X, ALU.min)

            def w13_low_part(c, n):
                dve.wait_ge(w13_high, n * NS + c + 1)
                V.tensor_tensor(w13_chunk(w13l, c), w13_chunk(w13st, c), w13_chunk(w13h, c).bitcast(F32),
                                ALU.subtract).then_inc(w13_low, 1)

            def unit(u, g, b, b_next, prep, final):
                bk = banks(u, g, prep, final)

                last_group = isinstance(g, int)
                previous_norm = last_group and not (isinstance(b, int) and b == 0)

                def hi(name):
                    return hi_at(u, g, prep, final, name)

                if prep:
                    for t, _ in PREP_START:
                        weight_low(bk, t, hi(f"w_{t}"))
                for h in range(REP):
                    if prep and h == 0:
                        softmax_max(u, 1)
                    if h == 0 and not final:
                        query_low(bk, 0, hi("Q0"), REP * (u + 1) + 1)
                    if h < REP - 1 and not (prep and h == 0):
                        softmax_max(u, h + 1)
                    for c in "ABC":
                        start, n, _ = CHUNKS[c]
                        low(bk, f"{c}{h}", pTl[:, start:start + n], psum[bk.use(f"{c}{h}")[0]][:, 0:n],
                            pTh[:, start:start + n], hi(f"{c}{h}"))
                    if h < 2:
                        quantise_ctx(u, h)
                    if h and not final:
                        query_low(bk, h, hi(f"Q{h}"), REP * (u + 1) + h + 1)
                    if h < REP - 1:
                        softmax_norm(u, h + 1)
                    if prep:
                        for t, _ in PREP_IN_SLOT[h]:
                            weight_low(bk, t, hi(f"w_{t}"))
                    low(bk, f"PV{h}", oTl[:, h, :], psum[bk.use(f"PV{h}")[0]][:, :], oTh[:, h, :], hi(f"PV{h}"))
                    if not final:
                        take_sums(bk, h)
                    if previous_norm:
                        row_extremes((b - 1) * TB + h)
                        tile_stats((b - 1) * TB + h, h)
                if not final:
                    low(bk, "VT", vl[:, :, :], blocks(bk.use("VT")[0]), vh[:, :, :], hi("VT"))
                    key_norms()

                def add(m, signal=None):
                    ps = full(bk, f"O{m}")
                    row = xres[:, bass.ds(b * TB + m, 1), :].rearrange("p a d -> p (a d)")
                    V.tensor_tensor(row, row, ps[:, :], ALU.add).then_inc(signal or bk.freed[bk.use(f"O{m}")[0]], 1)

                if final:
                    means((b - 1) * TB)
                    dve.drain()
                    for m in range(TB):
                        add(m, attn_done if m == TB - 1 else None)
                        dve.drain()
                        row_extremes(b * TB + m)
                        tile_stats(b * TB + m, m)
                    return
                add(0)
                add(1)
                normed_keys(bk)
                keys_low(bk, hi("KN"))
                add(2)
                softmax_max(u + 1, 0)
                add(3)
                softmax_norm(u + 1, 0)
                if previous_norm:
                    means((b - 1) * TB)
                if prep:
                    for t in O_TILES:
                        weight_low(bk, t, hi(f"w_{t}"))

            units(dve, unit)

            means((B - 1) * TB)
            deviations(0, NT)
            for e in (rowmax, rowmin):
                V.tensor_tensor(e[:], e[:], mean[:], ALU.subtract)
            dve.drain()
            for e in (rowmax, rowmin):
                V.tensor_tensor(e[:], e[:], rstd[:], ALU.mult)
            largest_magnitude(rowmax[:], rowmin[:], amax[:, 2:3]).then_inc(x_amax, 1)
            shift_of(0, NT, shifts_done)
            dve.wait_ge(x_amax_all, 1)
            scale_from(amax[:, 3:4], f8scale[:, 1:2])
            V.tensor_scalar(f8scale[:, 3:4], amax[:, 1:2], FP8_EPS, 1.0 / FP8_MAX, ALU.max, ALU.mult)
            V.tensor_scalar(f8scale[:, 2:3], amax[:, 3:4], FP8_EPS, 1.0 / FP8_MAX, ALU.max, ALU.mult)
            dve.drain()
            V.tensor_tensor(f8scale[:, 2:3], f8scale[:, 2:3], f8scale[:, 3:4], ALU.mult)
            dve.drain()

            def quantise_tokens(tile, t):
                dve.wait_ge(y_done, tile + 1)
                to_fp8(q_y[:, t % 2, :], q_m[:], f8scale[:, 1:2], tokens_q[:, t % 2, :]).then_inc(quantised, 1)
                dve.drain()

            def add_cross_attention(bk, tile, t, b):
                ps = full(bk, f"XA{t}")
                dve.wait_ge(mask_read, b * TB + t)
                dve.wait_ge(mask_in, 16 * (b + 1))
                V.scalar_tensor_tensor(out=attended[:], in0=ps[:, :], scalar=f8scale[:, 2:3], in1=mask_b[:],
                                       op0=ALU.mult, op1=ALU.add).then_inc(bk.freed[bk.use(f"XA{t}")[0]], 1)
                dve.drain()
                row = flat(xres[:, bass.ds(tile, 1), :])
                V.tensor_tensor(row, row, attended[:], ALU.add).then_inc(mask_read, 1)
                dve.drain()
                tile_stats(tile, t)

            def normalise_batch(b, first_batch=False):
                finish_norm(b * TB)
                if not first_batch:
                    dve.wait_ge(tokens_sent, 16 * TB * b)
                    dve.wait_ge(meta_sent, 16 * TB * b)
                for t in range(TB):
                    tile = b * TB + t
                    V.tensor_scalar(x3n[:, t, :], flat(xres[:, bass.ds(tile, 1), :]),
                                    mean[:, bass.ds(tile, 1)], rstd[:, bass.ds(tile, 1)],
                                    ALU.subtract, ALU.mult).then_inc(x3n_done, 1)

            def tokens_low(bk, t, n):
                dve.wait_ge(xh_done, n)
                name = f"XT{t}"
                cols = slice(t * P, (t + 1) * P)
                V.tensor_tensor(xl[:, :, cols], blocks(bk.use(name)[0]), xh[:, :, cols].bitcast(F32),
                                ALU.subtract).then_inc(bk.freed[bk.use(name)[0]], 1)

            def over_experts(ap):
                return ap.rearrange("p (t a) -> p t a", a=1).to_broadcast([P, TB, NE])

            def over_tiles(ap):
                return ap.rearrange("p (a e) -> p a e", a=1).to_broadcast([P, TB, NE])

            def choose_expert(bk, b):
                ps = full(bk, "LT")
                V.tensor_copy(lg[:], blocks(bk.use("LT")[0])[:, :, 0:NE])\
                    .then_inc(bk.freed[bk.use("LT")[0]], 1)
                dve.drain()
                V.tensor_reduce(r_max[:], lg[:], AX.X, ALU.max)
                dve.drain()
                V.tensor_tensor(lt[:], lg[:], over_experts(r_max[:]), ALU.subtract).then_inc(logits_less_max, 1)
                dve.drain()
                V.tensor_scalar(pos[:], lt[:], 0.0, float(NE), ALU.is_lt, ALU.mult)
                dve.drain()
                V.tensor_tensor(pos[:], pos[:], over_tiles(expert_id[:]), ALU.add)
                dve.drain()
                V.tensor_reduce(r_idx[:], pos[:], AX.X, ALU.min)
                dve.drain()
                V.tensor_tensor(onehot[:], over_tiles(expert_id[:]), over_experts(r_idx[:]), ALU.is_equal)\
                    .then_inc(onehot_done, 1)
                dve.wait_ge(logits_exp, b + 1)
                V.tensor_reduce(r_sum[:], le[:], AX.X, ALU.add)
                dve.drain()
                V.reciprocal(meta[:, :, 1:2].rearrange("p t a -> p (t a)"), r_sum[:])
                V.tensor_copy(meta[:, :, 0:1].rearrange("p t a -> p (t a)"), token_code[:])
                dve.drain()
                V.tensor_scalar(token_code[:], token_code[:], float(T), None, ALU.subtract)

            def place_tokens(bk, b):
                ps = full(bk, "CS")
                n = TB * NE
                V.tensor_tensor(pos[:], ps[:, 0:n].rearrange("p (t e) -> p t e", e=NE), over_tiles(carry[:]),
                                ALU.add)
                dve.drain()
                V.tensor_tensor(carry[:], ps[:, n:n + NE], carry[:], ALU.add)\
                    .then_inc(bk.freed[bk.use("CS")[0]], 1)
                dve.drain()
                V.tensor_tensor(pos[:], pos[:], onehot[:], ALU.mult)
                dve.drain()
                V.tensor_reduce(r_sel[:], pos[:], AX.X, ALU.add)
                V.tensor_scalar(r_t[:], r_idx[:], float(CAP), -1.0, ALU.mult, ALU.add)
                dve.drain()
                V.tensor_scalar(r_keep[:], r_sel[:], CAP + 0.5, None, ALU.is_lt)
                V.tensor_tensor(r_t[:], r_t[:], r_sel[:], ALU.add)
                dve.drain()
                away = float(2 * NE * CAP)
                V.tensor_scalar(r_sum[:], r_t[:], away, None, ALU.subtract)
                dve.drain()
                V.tensor_tensor(r_sum[:], r_sum[:], r_keep[:], ALU.mult)
                dve.drain()
                V.tensor_scalar(slot_w[:, :], r_sum[:], away, None, ALU.add).then_inc(slots_done, 1)
                dve.drain()

            def w2_low_part(c, n):
                dve.wait_ge(w2_high, n * NS + c + 1)
                V.tensor_tensor(w2l[:, c, :], w2st[:, c % 2, :], w2h[:, c, :].bitcast(F32), ALU.subtract)\
                    .then_inc(w2_low, 1)

            def hidden(bk, c, n_tok, n_body):
                if c < HC:
                    ps = full(bk, f"b{c}")
                    bank, n = bk.use(f"a{c}")
                    dve.wait_ge(bk.freed[bank], n + 1)
                    V.tensor_tensor(hid[:, c % 2, 0:n_tok], gate_act[:, c % 2, 0:n_tok], ps[:, 0:n_tok], ALU.mult)\
                        .then_inc(bk.freed[bk.use(f"b{c}")[0]], 1)
                    dve.wait_ge(hh_done, n_body * NS + c + 1)
                    V.tensor_tensor(hl[:, c, 0:n_tok], hid[:, c % 2, 0:n_tok], hh[:, c, 0:n_tok].bitcast(F32),
                                    ALU.subtract).then_inc(hl_done, 1)
                else:
                    ps = full(bk, "ab")
                    dve.wait_ge(act_done, n_body + 1)
                    V.tensor_tensor(hid[0:HT, c % 2, 0:n_tok], gate_act[0:HT, c % 2, 0:n_tok], ps[HT:P, 0:n_tok],
                                    ALU.mult).then_inc(bk.freed[bk.use("ab")[0]], 1)
                    dve.wait_ge(hh_done, n_body * NS + c + 1)
                    V.tensor_tensor(hh[HT:P, c, 0:n_tok], hid[0:HT, c % 2, 0:n_tok],
                                    hh[0:HT, c, 0:n_tok].bitcast(F32), ALU.subtract).then_inc(hl_done, 1)

            def add_shared(bk, tile, m):
                ps = full(bk, f"D{m}")
                row = flat(xres[:, bass.ds(tile, 1), :])
                V.tensor_tensor(row, row, ps[:, :], ALU.add).then_inc(bk.freed[bk.use(f"D{m}")[0]], 1)

            for t in range(TB):
                if t >= 2:
                    full(before, f"QT{t - 2}")
                quantise_tokens(t, t)
                if t:
                    add_cross_attention(before, t - 1, t - 1, 0)
            add_cross_attention(before, TB - 1, TB - 1, 0)
            normalise_batch(0, True)
            for c in range(2):
                w2_low_part(c, 0)
            dve.wait_ge(wg_high, 1)
            V.tensor_tensor(wgl[:, :, :], wg[:, :, :], wgh[:, :, :].bitcast(F32), ALU.subtract).then_inc(wg_low, 1)
            for t in range(TB):
                tokens_low(before, t, t + 1)
            for c in range(2, NS):
                w2_low_part(c, 0)
            for t in range(2):
                quantise_tokens(TB + t, t)
            dve.wait_ge(route_consts, 6)

            def shared(b, ahead, next_two):
                bk = shared_banks(b, ahead)
                next_tile = (b + 1) * TB
                for c in range(NS):
                    hidden(bk, c, T, b)
                    if ahead and c < 2:
                        full(bk, f"QT{c}")
                        quantise_tokens(next_tile + 2 + c, c)
                    if c == 2:
                        choose_expert(bk, b)
                    if not ahead and c:
                        w13_low_part(c - 1, 1)
                    if c == 4:
                        place_tokens(bk, b)
                    if ahead and 1 <= c <= TB:
                        add_cross_attention(bk, next_tile + c - 1, c - 1, b + 1)
                if ahead:
                    normalise_batch(b + 1)
                add_shared(bk, b * TB, 0)
                add_shared(bk, b * TB + 1, 1)
                if not ahead:
                    w13_low_part(HC, 1)
                add_shared(bk, b * TB + 2, 2)
                for t in range(TB if ahead else CAP_T):
                    tokens_low(bk, t, (b + 1) * TB + t + 1)
                add_shared(bk, b * TB + 3, 3)
                if next_two:
                    for t in range(2):
                        quantise_tokens(next_tile + TB + t, t)

            with dve.Fori(0, B - 2) as b:
                shared(b, True, True)
            shared(B - 2, True, False)
            shared(B - 1, False, False)

            dve.wait_ge(slot_meta_in, 16)
            V.tensor_scalar(slot_token[:], flat(slot_meta[:, :, 0:1]), -1.0, float(NOBODY), ALU.mult, ALU.add)
            dve.drain()
            V.tensor_scalar(row_from[:], slot_token[:], float(B * T - 1), None, ALU.min)
            V.tensor_scalar(row_to[:], slot_token[:], 0.0, None, ALU.add).then_inc(rows_known, 1)

            def answer(bk, e, m, first):
                ps = full(bk, f"D{m}")
                dve.wait_ge(slot_x_in[m], 16 * (e + 1))
                if not first:
                    dve.wait_ge(answers_out[m], 16 * e)
                V.scalar_tensor_tensor(out=expert_out[:, m, :], in0=ps[:, :],
                                       scalar=flat(slot_meta[:, bass.ds(e * CAP_T + m, 1), 1:2]),
                                       in1=slot_x[:, m, :], op0=ALU.mult, op1=ALU.add)\
                    .then_inc(bk.freed[bk.use(f"D{m}")[0]], 1)

            def expert(e, ahead, first=False):
                bk = expert_banks(e, ahead)
                for c in range(NS):
                    hidden(bk, c, CAP, B + e)
                    w2_low_part(c, e + 1)
                    if ahead and c:
                        w13_low_part(c - 1, e + 2)
                if ahead:
                    w13_low_part(HC, e + 2)
                    for t in range(CAP_T):
                        tokens_low(bk, t, NT + e * CAP_T + CAP_T + t + 1)
                for m in range(CAP_T):
                    answer(bk, e, m, first)

            expert(0, True, True)
            with dve.Fori(1, NE - 1) as e:
                expert(e, True)
            expert(NE - 1, False)


_INS = ['x', 'ctx_2048', 'mask_Bx1xS2_ff0', 'L0_attn_Wq', 'L0_attn_Wk', 'L0_attn_Wv', 'L0_attn_Wo',
        'L0_attn_q_scale', 'L0_attn_k_scale', 'L0_ffn_Wg', 'L0_ffn_W1', 'L0_ffn_W3', 'L0_ffn_W2',
        'L0_ffn_sw1', 'L0_ffn_sw3', 'L0_ffn_sw2']
_OUTS = [((B, T, D), 'float32')]


def kernel(**inputs):
    import numpy as _np
    import concourse.bacc as _bacc
    from concourse import mybir as _mybir
    from concourse.bass_utils import run_bass_kernel_spmd as _run

    nc = _bacc.Bacc("TRN2", target_bir_lowering=False, num_devices=1)
    arrays, args = {}, []
    for name in _INS:
        a = _np.ascontiguousarray(inputs[name])
        arrays[f"in_{name}_dram"] = a
        args.append(nc.dram_tensor(f"in_{name}_dram", a.shape, _mybir.dt.from_np(a.dtype), kind="ExternalInput").ap())
    for i, (shape, dtype) in enumerate(_OUTS):
        dt = _mybir.dt.from_np(_np.dtype(dtype))
        args.append(nc.dram_tensor(f"out_{i}_dram", shape, dt, kind="ExternalOutput").ap())
    decoder(nc, *args)
    r = _run(nc, [arrays], core_ids=[0])
    got = tuple(r.results[0][f"out_{i}_dram"] for i in range(len(_OUTS)))
    return got[0]
```
